# Optimizing a Trainium2 kernel written in Bass

```python
import numpy as np
import jax
import jax.numpy as jnp

def _softmax(x, axis=-1):
    return jax.nn.softmax(x, axis=axis)

def _gelu(x):
    return jax.nn.gelu(x, approximate=True)

def _silu(x):
    return jax.nn.silu(x)

def _sigmoid(x):
    return jax.nn.sigmoid(x)

def _layernorm(x, axis=-1, eps=1e-05):
    m = jnp.mean(x, axis=axis, keepdims=True)
    v = jnp.var(x, axis=axis, keepdims=True)
    return (x - m) / jnp.sqrt(v + eps)

def _scatter_add(tgt, idx, src, axis=0):
    return tgt.at[idx].add(src)

def _segment_sum(src, seg, n):
    return jax.ops.segment_sum(src, seg, n)
kernel_name = 'mk_gps_d1_gnn_r8_761aa2'

def setup_inputs(seed: int=0):
    np.random.seed(seed)
    _w = jnp.asarray

    def _rec_inputs():
        import jax
        import jax.numpy as jnp
        _gk = jax.random.key(seed)
        x = -0.0002117 + 1 * jax.random.normal(jax.random.fold_in(_gk, 1), (1250, 512), jnp.float32)
        src = jax.random.randint(jax.random.fold_in(_gk, 2), (20000,), 0, 1250, jnp.int32)
        dst = jax.random.randint(jax.random.fold_in(_gk, 3), (20000,), 0, 1250, jnp.int32)
        _o = jnp.argsort(dst, stable=True)
        src = src[_o]
        dst = dst[_o]
        return (x, src, dst)
    x, src, dst = _rec_inputs()

    def _L0_gnn_setup():
        import jax, jax.numpy as jnp
        import numpy as np
        N_NODES = 6250
        N_EDGES = 100000
        D_IN = 512
        D_OUT = 512
        key = jax.random.key(seed)
        k1, k2, k3, k4, k5 = jax.random.split(key, 5)
        local_feats = jax.random.normal(k1, (N_NODES, D_IN), dtype=jnp.float32)
        src = jax.random.randint(k2, (N_EDGES,), 0, N_NODES, dtype=jnp.int64)
        dst = jax.random.randint(k3, (N_EDGES,), 0, N_NODES, dtype=jnp.int64)
        lim = (6.0 / (D_IN + D_OUT)) ** 0.5
        W_self = jax.random.uniform(k4, (D_OUT, D_IN), minval=-lim, maxval=lim, dtype=jnp.float32)
        W_neigh = jax.random.uniform(k5, (D_OUT, D_IN), minval=-lim, maxval=lim, dtype=jnp.float32)
        b = jnp.zeros((D_OUT,), dtype=jnp.float32)
        return {'local_feats': local_feats, 'src': src, 'dst': dst, 'layer': 0, 'W_self': W_self, 'W_neigh': W_neigh, 'b': b}
    _L0_gnn_all = _L0_gnn_setup()
    _L0_gnn_in = {k: v for k, v in _L0_gnn_all.items() if k in ('W_self', 'W_neigh', 'b')}
    del _L0_gnn_all

    def _L0_mix_setup():
        import jax, jax.numpy as jnp
        import numpy as np
        EPS_STAB = 1e-09
        BN_EPS = 1e-05
        key = jax.random.key(seed)
        ks = jax.random.split(key, 5)
        B, N, C = (2, 512, 512)
        s = 1.0 / np.sqrt(C)
        d = {'inputs': jax.random.normal(ks[0], (B, N, C), jnp.float32)}
        for i, w in enumerate(['Wq', 'Wk', 'Wv', 'Wo']):
            d[w] = jax.random.normal(ks[1 + i], (C, C), jnp.float32) * s
        for b in ['bq', 'bk', 'bv', 'bo']:
            d[b] = jnp.zeros((C,), jnp.float32)
        d['bn_scale'] = jnp.ones((C,), jnp.float32)
        d['bn_bias'] = jnp.zeros((C,), jnp.float32)
        d['bn_mean'] = jnp.zeros((C,), jnp.float32)
        d['bn_var'] = jnp.ones((C,), jnp.float32)
        return d
    _L0_mix_all = _L0_mix_setup()
    _L0_mix_in = {k: v for k, v in _L0_mix_all.items() if k in ('Wq', 'bq', 'Wk', 'bk', 'Wv', 'bv', 'Wo', 'bo', 'bn_scale', 'bn_bias', 'bn_mean', 'bn_var')}
    del _L0_mix_all

    def _L0_ffn_setup():
        import jax, jax.numpy as jnp
        import numpy as np
        D, NH, HID, E = (512, 8, 256, 8)
        EPS = 1e-05

        def _layernorm(x, g, b):
            mu = jnp.mean(x, axis=-1, keepdims=True)
            var = jnp.mean(jnp.square(x - mu), axis=-1, keepdims=True)
            return (x - mu) * jax.lax.rsqrt(var + EPS) * g + b
        key = jax.random.key(seed)
        ks = jax.random.split(key, 20)
        s = 0.02
        inp = {'x': jax.random.normal(ks[0], (4, 1024, D), jnp.float32), 'Wq': jax.random.normal(ks[1], (D, D), jnp.float32) * s, 'bq': jnp.zeros((D,), jnp.float32), 'Wk': jax.random.normal(ks[2], (D, D), jnp.float32) * s, 'bk': jnp.zeros((D,), jnp.float32), 'Wv': jax.random.normal(ks[3], (D, D), jnp.float32) * s, 'bv': jnp.zeros((D,), jnp.float32), 'Wo': jax.random.normal(ks[4], (D, D), jnp.float32) * s, 'bo': jnp.zeros((D,), jnp.float32), 'g1': jnp.ones((D,), jnp.float32), 'beta1': jnp.zeros((D,), jnp.float32), 'g2': jnp.ones((D,), jnp.float32), 'beta2': jnp.zeros((D,), jnp.float32), 'Wg': jax.random.normal(ks[5], (D, E), jnp.float32) * s, 'bg': jnp.zeros((E,), jnp.float32), 'W1': jax.random.normal(ks[6], (E, D, HID), jnp.float32) * s, 'b1': jnp.zeros((E, HID), jnp.float32), 'W2': jax.random.normal(ks[7], (E, HID, D), jnp.float32) * s, 'b2': jnp.zeros((E, D), jnp.float32)}
        return inp
    _L0_ffn_all = _L0_ffn_setup()
    _L0_ffn_in = {k: v for k, v in _L0_ffn_all.items() if k in ('Wq', 'bq', 'Wk', 'bk', 'Wv', 'bv', 'Wo', 'bo', 'g1', 'beta1', 'g2', 'beta2', 'Wg', 'bg', 'W1', 'b1', 'W2', 'b2')}
    del _L0_ffn_all
    return {'x': x, 'src': src, 'dst': dst, 'L0_gnn_W_self': _L0_gnn_in['W_self'], 'L0_gnn_W_neigh': _L0_gnn_in['W_neigh'], 'L0_gnn_b': _L0_gnn_in['b'], 'L0_mix_Wq': _L0_mix_in['Wq'], 'L0_mix_bq': _L0_mix_in['bq'], 'L0_mix_Wk': _L0_mix_in['Wk'], 'L0_mix_bk': _L0_mix_in['bk'], 'L0_mix_Wv': _L0_mix_in['Wv'], 'L0_mix_bv': _L0_mix_in['bv'], 'L0_mix_Wo': _L0_mix_in['Wo'], 'L0_mix_bo': _L0_mix_in['bo'], 'L0_mix_bn_scale': _L0_mix_in['bn_scale'], 'L0_mix_bn_bias': _L0_mix_in['bn_bias'], 'L0_mix_bn_mean': _L0_mix_in['bn_mean'], 'L0_mix_bn_var': _L0_mix_in['bn_var'], 'L0_ffn_Wq': _L0_ffn_in['Wq'], 'L0_ffn_bq': _L0_ffn_in['bq'], 'L0_ffn_Wk': _L0_ffn_in['Wk'], 'L0_ffn_bk': _L0_ffn_in['bk'], 'L0_ffn_Wv': _L0_ffn_in['Wv'], 'L0_ffn_bv': _L0_ffn_in['bv'], 'L0_ffn_Wo': _L0_ffn_in['Wo'], 'L0_ffn_bo': _L0_ffn_in['bo'], 'L0_ffn_g1': _L0_ffn_in['g1'], 'L0_ffn_beta1': _L0_ffn_in['beta1'], 'L0_ffn_g2': _L0_ffn_in['g2'], 'L0_ffn_beta2': _L0_ffn_in['beta2'], 'L0_ffn_Wg': _L0_ffn_in['Wg'], 'L0_ffn_bg': _L0_ffn_in['bg'], 'L0_ffn_W1': _L0_ffn_in['W1'], 'L0_ffn_b1': _L0_ffn_in['b1'], 'L0_ffn_W2': _L0_ffn_in['W2'], 'L0_ffn_b2': _L0_ffn_in['b2']}

def reference(x, src, dst, L0_gnn_W_self, L0_gnn_W_neigh, L0_gnn_b, L0_mix_Wq, L0_mix_bq, L0_mix_Wk, L0_mix_bk, L0_mix_Wv, L0_mix_bv, L0_mix_Wo, L0_mix_bo, L0_mix_bn_scale, L0_mix_bn_bias, L0_mix_bn_mean, L0_mix_bn_var, L0_ffn_Wq, L0_ffn_bq, L0_ffn_Wk, L0_ffn_bk, L0_ffn_Wv, L0_ffn_bv, L0_ffn_Wo, L0_ffn_bo, L0_ffn_g1, L0_ffn_beta1, L0_ffn_g2, L0_ffn_beta2, L0_ffn_Wg, L0_ffn_bg, L0_ffn_W1, L0_ffn_b1, L0_ffn_W2, L0_ffn_b2):
    import jax
    import jax.numpy as jnp

    def _L0_gnn_ref(local_feats, src, dst, layer, W_self, W_neigh, b):
        import jax, jax.numpy as jnp
        import numpy as np
        N_NODES = 6250
        N_EDGES = 100000
        D_IN = 512
        D_OUT = 512
        'DistSAGEConv forward: mean neighbor aggregation + fc_self + fc_neigh + bias + ReLU.\n            `layer` only selects which hop in the distributed impl; aggregation math is identical.\n            '
        n = local_feats.shape[0]
        msg = local_feats[src]
        agg = jax.ops.segment_sum(msg, dst, num_segments=n)
        deg = jax.ops.segment_sum(jnp.ones((src.shape[0],), local_feats.dtype), dst, num_segments=n)
        h_neigh = agg / jnp.maximum(deg, 1.0)[:, None]
        rst = local_feats @ W_self.T + h_neigh @ W_neigh.T + b
        return jax.nn.relu(rst)

    def _L0_mix_ref(inputs, Wq, bq, Wk, bk, Wv, bv, Wo, bo, bn_scale, bn_bias, bn_mean, bn_var):
        import jax, jax.numpy as jnp
        import numpy as np
        EPS_STAB = 1e-09
        BN_EPS = 1e-05
        q = inputs @ Wq + bq
        k = inputs @ Wk + bk
        v = inputs @ Wv + bv
        att = jax.nn.softmax(jnp.einsum('bmc,bnc->bmn', q, k), axis=-1)
        att = att / (EPS_STAB + jnp.sum(att, axis=1, keepdims=True))
        out = v * jnp.sum(att, axis=1)[..., None]
        out = out @ Wo + bo
        out = (out - bn_mean) * jax.lax.rsqrt(bn_var + BN_EPS) * bn_scale + bn_bias
        return jax.nn.relu(out) + inputs

    def _L0_ffn_ref(x, Wq, bq, Wk, bk, Wv, bv, Wo, bo, g1, beta1, g2, beta2, Wg, bg, W1, b1, W2, b2):
        import jax, jax.numpy as jnp
        import numpy as np
        D, NH, HID, E = (512, 8, 256, 8)
        EPS = 1e-05

        def _layernorm(x, g, b):
            mu = jnp.mean(x, axis=-1, keepdims=True)
            var = jnp.mean(jnp.square(x - mu), axis=-1, keepdims=True)
            return (x - mu) * jax.lax.rsqrt(var + EPS) * g + b
        B, S, _ = x.shape
        dh = D // NH
        q = (x @ Wq + bq).reshape(B, S, NH, dh)
        k = (x @ Wk + bk).reshape(B, S, NH, dh)
        v = (x @ Wv + bv).reshape(B, S, NH, dh)
        scores = jnp.einsum('bqhd,bkhd->bhqk', q, k) / jnp.sqrt(jnp.float32(dh)).astype(x.dtype)
        attn = jax.nn.softmax(scores, axis=-1)
        ctx = jnp.einsum('bhqk,bkhd->bqhd', attn, v).reshape(B, S, D)
        sa = ctx @ Wo + bo
        x = _layernorm(x + sa, g1, beta1)
        t = x.reshape(-1, D)
        logits = t @ Wg + bg
        idx = jnp.argmax(logits, axis=-1)
        h = jax.nn.gelu(jnp.einsum('td,edh->teh', t, W1) + b1, approximate=False)
        y = jnp.einsum('teh,ehd->ted', h, W2) + b2
        onehot = jax.nn.one_hot(idx, E, dtype=t.dtype)
        moe = jnp.einsum('ted,te->td', y, onehot).reshape(B, S, D)
        return _layernorm(x + moe, g2, beta2)
    xn = _layernorm(x, axis=-1)
    x = x + _L0_gnn_ref(xn, src, dst, 0, L0_gnn_W_self, L0_gnn_W_neigh, L0_gnn_b) + _L0_mix_ref(xn[None], L0_mix_Wq, L0_mix_bq, L0_mix_Wk, L0_mix_bk, L0_mix_Wv, L0_mix_bv, L0_mix_Wo, L0_mix_bo, L0_mix_bn_scale, L0_mix_bn_bias, L0_mix_bn_mean, L0_mix_bn_var)[0]
    x = x + _L0_ffn_ref(_layernorm(x, axis=-1)[None], L0_ffn_Wq, L0_ffn_bq, L0_ffn_Wk, L0_ffn_bk, L0_ffn_Wv, L0_ffn_bv, L0_ffn_Wo, L0_ffn_bo, L0_ffn_g1, L0_ffn_beta1, L0_ffn_g2, L0_ffn_beta2, L0_ffn_Wg, L0_ffn_bg, L0_ffn_W1, L0_ffn_b1, L0_ffn_W2, L0_ffn_b2)[0]
    return x

_drawn_inputs = setup_inputs


def setup_inputs(seed=0):
    import zlib

    import numpy as np

    out = dict(_drawn_inputs(seed))
    spreads = {'L0_gnn_b': (0.0, 0.1),
     'L0_mix_bq': (0.0, 0.8),
     'L0_mix_bk': (0.0, 2.0),
     'L0_mix_bv': (0.0, 0.1),
     'L0_mix_bo': (0.0, 0.1),
     'L0_mix_bn_scale': (1.0, 0.2),
     'L0_mix_bn_bias': (0.0, 0.1),
     'L0_mix_bn_mean': (0.0, 0.1),
     'L0_mix_bn_var': (1.0, 0.2),
     'L0_ffn_bq': (0.0, 0.8),
     'L0_ffn_bk': (0.0, 2.0),
     'L0_ffn_bv': (0.0, 0.461),
     'L0_ffn_bo': (0.0, 0.509),
     'L0_ffn_g1': (1.0, 0.2),
     'L0_ffn_beta1': (0.0, 0.1),
     'L0_ffn_g2': (1.0, 0.2),
     'L0_ffn_beta2': (0.0, 0.1),
     'L0_ffn_bg': (0.0, 0.398),
     'L0_ffn_b1': (0.0, 0.8),
     'L0_ffn_b2': (0.0, 0.1)}
    factors = {'L0_mix_Wq': 8.0,
     'L0_mix_Wk': 8.0,
     'L0_ffn_Wq': 8.0,
     'L0_ffn_Wk': 8.0,
     'L0_ffn_Wv': 7.395,
     'L0_ffn_Wo': 3.039}
    for name, (base, spread) in spreads.items():
        noise = np.random.default_rng([zlib.crc32(name.encode()), seed]).standard_normal(out[name].shape)
        drawn = base * np.exp(spread * noise) if base else spread * noise
        out[name] = jnp.asarray(drawn.astype(out[name].dtype))
    for name, factor in factors.items():
        out[name] = (out[name] * factor).astype(out[name].dtype)
    return out
```

```python
import concourse.bass as bass
from concourse import mybir
from contextlib import ExitStack

F32 = mybir.dt.float32
F32R = mybir.dt.float32r
BF16 = mybir.dt.bfloat16
F16 = mybir.dt.float16
I32 = mybir.dt.int32
U32 = mybir.dt.uint32
ALU = mybir.AluOpType
ACT = mybir.ActivationFunctionType
AX = mybir.AxisListType

N, D, E = 1250, 512, 20000
P = 128
T = -(-N // P)
NP = T * P
KC = D // P
PIECES = [(0, 512), (512, 1024), (1024, NP)]
CE = 125
CH = E // CE
CP = CH // 2
NH, DH = 8, 64
NE, HID = 8, 256
UNITS = NH * T
LN_EPS = 1e-5
BIG = 10000.0


def rows(t):
    return min(P, N - t * P)


def cols(t):
    return slice(t * P, t * P + rows(t))


def gps_layer(nc, x, src, dst, w_all, mix_bq, mix_bv, mix_rows, ffn_bq, ffn_bk, ffn_rows,
              wg, bg, b1, b2, out):
    ctx = ExitStack()
    with ctx:
        arena = ctx.enter_context(nc.sbuf_tensor("arena", [P, 212480 // 4], F32))
        base = (nc.sbuf_base - 212480)
        at = [base + (-base) % 32]

        def place(name, shape, dt, offset):
            return nc.alloc_sbuf_tensor_at(name, shape, dt, offset=offset)

        def region(size):
            o = at[0]
            at[0] += -(-size // 32) * 32
            return o

        r_act, r_b, r_w, r_stage = region(40960), region(40960), region(32768), region(8192)
        r_acc, r_p, r_rows, r_over = region(20480), region(10240), region(12288), region(40960)

        def small(name, shape, dt):
            n = 1
            for s in shape[1:]:
                n *= s
            return place(name, shape, dt, region(n * mybir.dt.size(dt)))

        act_h = place("act_h", [P, KC, NP], F32R, r_act)
        act_l = place("act_l", [P, KC, NP], F32R, r_act + 20480)
        ctx_rows = place("ctx_rows", [P, T, D], F32, r_act)
        big = place("big", [P, 2 * KC, NP], F32R, r_b)
        y_h = place("y_h", [P, T, D], F32R, r_b)
        y_l = place("y_l", [P, T, D], F32R, r_b + 20480)
        rows_b = place("rows_b", [P, T, D], F32, r_b)
        mask = place("mask", [P, NE, NP], BF16, r_b)
        w_h = place("w_h", [P, 2, KC, D], F32R, r_w)
        w_l = place("w_l", [P, 2, KC, D], F32R, r_w + 16384)
        stage = place("stage", [P, KC, D], F32, r_stage)
        acc = place("acc", [P, T, D], F32, r_acc)
        prob = place("prob", [P, 2, NP], F32, r_p)
        adj_h = place("adj_h", [P, NP], F32R, r_p)
        adj_l = place("adj_l", [P, NP], F32R, r_p + 5120)
        tmp = place("tmp", [P, 2, NP], F32, r_p)
        row_c = place("row_c", [P, 6, D], F32, r_rows)
        fold_h = place("fold_h", [P, KC, D], F32R, r_over)
        fold_l = place("fold_l", [P, KC, D], F32R, r_over + 8192)
        o = r_over + 16384
        col_acc = place("col_acc", [P, NP], F32, o); o += 5120
        hot_src = place("hot_src", [P, 2 * NP], BF16, o); o += 5120
        hot_dst = place("hot_dst", [P, 2 * P], BF16, o); o += 512
        iota16 = place("iota16", [P, NP], F16, o); o += 2560
        bv_rep_h = place("bv_rep_h", [P, KC, P], F32R, o); o += 2048
        bv_rep_l = place("bv_rep_l", [P, KC, P], F32R, o); o += 2048
        edge_i = place("edge_i", [CP, 4, CE], I32, o)
        edge_f = place("edge_f", [CP, 4, CE], F32, o + 2016); o += 4032
        work1 = place("work1", [P, D], F32, o); o += 2048
        assert o <= r_over + 40960
        val = place("val", [P, T, NH, 3 * DH], BF16, r_over)
        pt_h = place("pt_h", [P, 2, T, P], F16, r_over + 30720)
        pt_l = place("pt_l", [P, 2, T, P], F16, r_over + 35840)
        tok = place("tok", [P, T, D], F32, r_over)
        hid_h = place("hid_h", [P, 2, 640], F32R, r_over + 30720)
        hid_l = place("hid_l", [P, 2, 640], F32R, r_over + 35840)
        ident = small("ident", [P, P], F32)
        ones = small("ones", [P, P], F32)
        zero16 = small("zero16", [P, D], BF16)
        ones16 = small("ones16", [P, 2], BF16)
        edge_t = small("edge_t", [CE, 2 * CH], F32)
        lohi = small("lohi", [CP, 4], F32)
        mv = small("mv", [P, T, 2], F32)
        st6 = small("st6", [P, 2, 6], F32)
        ve = small("ve", [P, T], F32)
        rs = small("rs", [P, T], F32)
        nr = small("nr", [P, T], F32)
        rdeg = small("rdeg", [P, T], F32)
        z_mix = small("z_mix", [P, T], F32)
        nmax = small("nmax", [P, T], F32)
        cfac = small("cfac", [P, T], F32)
        zt = small("zt", [P, T], F32)
        nm = small("nm", [P, 2], F32)
        zz = small("zz", [P, 2], F32)
        rz = small("rz", [P, 2], F32)
        cols_c = small("cols_c", [P, 4 * KC + 16 + 1], F32)
        bq_pair = small("bq_pair", [P, KC, 2], F32R)
        bt = small("bt", [P, KC], F32)
        tile_lo = small("tile_lo", [T, 2], F32)
        span = small("span", [T, 4], F32)
        span_i = small("span_i", [T, 2], I32)
        diag = place("diag", [CP, 4, CP], F32, r_w)
        cover = place("cover", [T, CH], F32, r_w + 1280)
        cover2 = place("cover2", [T, CH], F32, r_w + 1920)
        chunk_no = place("chunk_no", [T, CH], F32, r_w + 2560)
        wg_h = place("wg_h", [P, KC, P], F32R, r_b + 20480)
        wg_l = place("wg_l", [P, KC, P], F32R, r_b + 22528)
        wg_f = place("wg_f", [P, KC, P], F32, r_b + 24576)
        lg_t = place("lg_t", [NE, NP], F32, r_b + 26624)
        oh_t = place("oh_t", [NE, NP], F32R, r_b + 31744)
        b2_f = place("b2_f", [NE, D], F32, r_over + 26048)
        sel = place("sel", [NE, NE, P], F32R, r_b + 36864)
        b2_h = place("b2_h", [NE, D], F32R, r_over + 24000)
        b2_l = place("b2_l", [NE, D], F32R, r_over + 20480)
        lg = place("lg", [P, T, NE], F32, r_over + 22528)
        m8 = place("m8", [P, T, 8], F32, r_over + 22848)
        ix = place("ix", [P, T, 8], U32, r_over + 23168)
        ixf = place("ixf", [P, T], F32, r_over + 23488)
        oh = place("oh", [P, T, NE], F32, r_over + 23552)
        iota8 = small("iota8", [P, NE], F32)
        cten = place("cten", [P, DH], F32, region(256))
        assert at[0] <= nc.sbuf_usable_end, (at[0], nc.sbuf_usable_end)

        c_mbq, c_mbv = cols_c[:, 0:KC], cols_c[:, KC:2 * KC]
        c_fbq, c_fbk = cols_c[:, 2 * KC:3 * KC], cols_c[:, 3 * KC:4 * KC]
        c_b1, c_bg = cols_c[:, 4 * KC:4 * KC + 16], cols_c[0:NE, 4 * KC + 16:4 * KC + 17]

        qk_dram = nc.dram_tensor("qk_dram", [2, NH, 2, DH, NP], F32, kind="Internal").ap()

        slot = {s: ctx.enter_context(nc.psum_tensor(s, [P, 512 * n], F32))[:, :]
                for s, n in (("W0", 3), ("W1", 3), ("N0", 1), ("N1", 1))}

        def sem(name):
            return ctx.enter_context(nc.semaphore(name))

        filled = {s: sem("filled_" + s) for s in slot}
        drained = {s: sem("drained_" + s) for s in slot}
        jobs, used = {}, {s: 0 for s in slot}

        def book(key, s):
            jobs[key] = (s, used[s])
            used[s] += 1

        book("edges", "N0")
        book("ranges", "N1")
        for k in range(KC):
            book(("xT", k), "W%d" % (k % 2))
        for t in range(T):
            book(("y", t), "N%d" % (t % 2))
        for t in range(T):
            book(("hist", t), "W%d" % (t % 2))
            book(("self", t), "N0")
            book(("agg", t), "N1")
        for m in range(KC):
            book(("foldM", m), "N%d" % (m % 2))
        book("bt", "N0")
        for m in range(KC):
            book(("tT", m), "W%d" % (m % 2))
        for t in range(T):
            book(("score", t), "W%d" % (t % 2))
        for m in range(KC):
            book(("foldN", m), "N%d" % (m % 2))
        book("bvo", "N0")
        book("colsum", "N1")
        for t in range(T):
            book(("o", t), "N%d" % (t % 2))
        for k in range(KC):
            book(("uT", k), "W%d" % (k % 2))
        for t in range(T):
            book(("v", t), "N%d" % (t % 2))
        for i in range(2 * KC):
            book(("qk", i), "W%d" % (i % 2))
        for i in range(UNITS):
            book(("S", i), "W0")
            book(("PT", i), "W1")
            book(("AV", i), "N%d" % (i % 2))
        for k in range(KC):
            book(("cT", k), "W%d" % (k % 2))
        for t in range(T):
            book(("sa", t), "N%d" % (t % 2))
        for k in range(KC):
            book(("tkT", k), "W%d" % (k % 2))
        book("logits", "W0")
        book("lgrows", "N0")
        book("ohT", "W1")
        for e in range(NE):
            book(("mask", e), "W%d" % (e % 2))

        def wait_filled(eng, key):
            s, n = jobs[key]
            eng.wait_ge(filled[s], n + 1)
            return slot[s]

        def wait_drained(eng, key):
            s, n = jobs[key]
            eng.wait_ge(drained[s], n + 1)

        s_x = [sem("x_in%d" % t) for t in range(T)]
        s_edge, s_const = sem("edges_in"), sem("column_constants_in")
        s_rowc, s_ffnrow = sem("mix_rows_in"), sem("ffn_rows_in")
        s_stage, s_split, s_scaled = sem("weights_in"), sem("weights_split"), sem("q_weights_scaled")
        s_bq8 = sem("bq_scaled")
        s_setup = sem("setup")
        s_step = sem("vector_step")
        s_ef, s_dg, s_span = sem("edge_floats"), sem("diag_ready"), sem("span_ready")
        s_var, s_sqrt = sem("variance_ready"), sem("sqrt_ready")
        s_rows = sem("normalised_rows")
        s_hi = sem("hi_written")
        s_hot, s_hotfree = sem("onehots_ready"), sem("onehots_used")
        s_max, s_exp, s_pfree = sem("mix_max"), sem("mix_exp"), sem("mix_prob_used")
        s_bqp, s_bvr = sem("bq_pair_ready"), sem("bv_rep_ready")
        s_v32, s_v1, s_v2r, s_v2, s_v3 = (sem("v_sum"), sem("v_part1"), sem("v_rest"), sem("v_part2"),
                                          sem("v_part3"))
        s_store = [sem("qk_store%d" % i) for i in range(4)]
        s_stack = [sem("stack_in%d" % i) for i in range(2)]
        s_amax, s_aexp, s_aptr = sem("att_max"), sem("att_exp"), sem("att_prob_hi")
        s_pads, s_mixdone = sem("pads_zeroed"), sem("mix_rows_done")
        s_tok, s_route = sem("tokens_ready"), sem("router_step")
        s_wg, s_b2 = sem("router_weights_in"), sem("b2_in")
        s_gelu, s_hm, s_hh, s_hl = sem("gelu"), sem("hidden_masked"), sem("hidden_hi"), sem("hidden_lo")
        s_hfill = [sem("h_filled%d" % i) for i in range(3)]
        s_y, s_yd, s_hused = sem("y_filled"), sem("y_drained"), sem("hidden_used")
        s_fin, s_out = sem("row_final"), sem("out_stored")

        W_NEIGH, W_SELF, W_QT, W_KT, W_VT, W_MO, W_V, W_Q, W_K, W_O = range(10)
        LAST_USE = {W_NEIGH: ("y", T - 1), W_SELF: ("self", T - 1), W_QT: ("foldM", KC - 1), W_KT: "bt",
                    W_VT: ("foldN", KC - 1), W_MO: "bvo", W_V: ("v", T - 1), W_Q: ("qk", KC - 1),
                    W_K: ("qk", 2 * KC - 1), W_O: ("sa", T - 1)}
        UP, DOWN = 10, 11
        GROUPS = 2 * NE // 2
        n_units = UP + 2 * GROUPS
        STEPS = GROUPS * KC
        HT = NP // 2
        PW = HT // 2

        def source(u):
            return w_all[u] if u < UP else w_all[UP + (u - UP) % NE]

        block = ctx.enter_context(nc.Block())

        @block.sync
        def _(sp):
            sp.dma_start(edge_i[:, 0:2, :], src.rearrange("(j p e) -> p j e", j=2, p=CP)).then_inc(s_edge, 16)
            sp.dma_start(edge_i[:, 2:4, :], dst.rearrange("(j p e) -> p j e", j=2, p=CP)).then_inc(s_edge, 16)
            for t in range(T):
                sp.dma_start(acc[0:rows(t), t, :], x[cols(t), :]).then_inc(s_x[t], 16)
            for i, a in enumerate((mix_bq, mix_bv, ffn_bq, ffn_bk)):
                sp.dma_start(cols_c[:, i * KC:(i + 1) * KC], a).then_inc(s_const, 16)
            sp.dma_start(c_b1, b1).then_inc(s_const, 16)
            sp.dma_start(c_bg, bg).then_inc(s_const, 16)

            def unit(u):
                if u:
                    sp.wait_ge(s_split, 2 * u)
                sp.dma_start(stage[:, :, :], source(u)).then_inc(s_stage, 16)

            unit(0)
            for i in range(6):
                sp.dma_start(row_c[:, i, :], mix_rows[i:i + 1, :].to_broadcast([P, D])).then_inc(s_rowc, 16)
            for u in range(1, W_Q):
                unit(u)
            sp.wait_ge(s_mixdone, T)
            for i in range(6):
                sp.dma_start(row_c[:, i, :], ffn_rows[i:i + 1, :].to_broadcast([P, D])).then_inc(s_ffnrow, 16)
            for u in (W_Q, W_K):
                unit(u)
            for i in range(2 * KC):
                wait_drained(sp, ("qk", i))
                for part in range(2):
                    for hh in range(2):
                        sp.dma_start(qk_dram[i // KC, 2 * (i % KC) + hh, part],
                                     big[hh * DH:(hh + 1) * DH, part * KC + i % KC, :].bitcast(F32)) \
                          .then_inc(s_store[i % 4], 16)
            for i in range(4):
                sp.wait_ge(s_store[i], 2 * 64)
            for h in range(NH):
                if h >= 2:
                    wait_filled(sp, ("S", (h - 1) * T - 1))
                b = 3 * (h % 2)
                sp.dma_start(big[:, b, :].bitcast(F32), qk_dram[0, h].rearrange("a d n -> (a d) n")).then_inc(s_stack[h % 2], 16)
                for part in range(2):
                    for rep in range(2):
                        sp.dma_start(big[rep * DH:(rep + 1) * DH, b + 1 + part, :].bitcast(F32), qk_dram[1, h, part]) \
                          .then_inc(s_stack[h % 2], 16)
            unit(W_O)
            unit(UP)
            wait_filled(sp, ("sa", T - 1))
            sp.wait_ge(s_pads, 3)
            sp.dma_start(wg_f[:, :, 0:NE], wg).then_inc(s_wg, 16)
            sp.dma_start(b2_f[:, :], b2).then_inc(s_b2, 16)
            for u in range(DOWN, n_units):
                unit(u)
            for t in range(T):
                sp.wait_ge(s_fin, t + 1)
                sp.dma_start(out[cols(t), :], tok[0:rows(t), t, :]).then_inc(s_out, 16)
            sp.wait_ge(s_out, 16 * T)

        @block.gpsimd
        def _(pool):
            pool.memset(ident[:, :], 0.0).then_inc(s_setup, 1)
            pool.memset(ones[:, :], 1.0).then_inc(s_setup, 1)
            pool.memset(ones16[:, :], 1.0).then_inc(s_setup, 1)
            pool.memset(mv[:, :, :], 1.0).then_inc(s_setup, 1)
            pool.wait_ge(s_setup, 4)
            pool.affine_select(out=ident[:, :], in_=ident[:, :], compare_op=ALU.not_equal, fill=1.0,
                               base=0, pattern=[[-1, P]], channel_multiplier=1).then_inc(s_setup, 1)
            pool.iota(tile_lo[:, 0:1], [[0, 1]], 0, P, allow_small_or_imprecise_dtypes=True).then_inc(s_setup, 1)
            pool.iota(tile_lo[:, 1:2], [[0, 1]], P - 1, P, allow_small_or_imprecise_dtypes=True).then_inc(s_setup, 1)
            pool.iota(chunk_no[:, :], [[1, CH]], 0, 0, allow_small_or_imprecise_dtypes=True).then_inc(s_setup, 1)
            pool.iota(iota16[:, :], [[1, NP]], 0, 0, allow_small_or_imprecise_dtypes=True).then_inc(s_setup, 1)
            pool.memset(zero16[:, :], 0.0).then_inc(s_setup, 1)
            pool.iota(iota8[:, :], [[1, NE]], 0, 0, allow_small_or_imprecise_dtypes=True).then_inc(s_setup, 1)
            pool.sem_inc(s_hotfree, 2)
            for a in (act_h, act_l):
                pool.memset(a[:, :, N:NP].bitcast(F32), 0.0).then_inc(s_setup, 1)
            for u in range(n_units):
                pool.wait_ge(s_stage, 16 * (u + 1))
                if u == 0:
                    pool.wait_ge(s_span, 1)
                elif u - 2 in LAST_USE:
                    wait_filled(pool, LAST_USE[u - 2])
                elif u >= 2:
                    g = (u - 2 - UP) // 2
                    if (u - UP) % 2:
                        pool.wait_ge(s_hused, KC * (g + 1))
                    else:
                        r = 2 * KC * (g + 1) - 1
                        pool.wait_ge(s_hfill[r % 3], r // 3 + 1)
                if u == W_Q:
                    pool.tensor_scalar(stage[:, :, :], stage[:, :, :], DH ** -0.5, None, ALU.mult).then_inc(s_scaled, 1)
                    pool.wait_ge(s_scaled, 1)
                pool.tensor_copy(w_h[:, u % 2], stage[:, :, :]).then_inc(s_split, 1)
                pool.wait_ge(s_split, 2 * u + 1)
                pool.tensor_tensor(w_l[:, u % 2], stage[:, :, :], w_h[:, u % 2].bitcast(F32), ALU.subtract) \
                    .then_inc(s_split, 1)

        @block.tensor
        def _(pe):
            def begin(key):
                s, n = jobs[key]
                if n:
                    pe.wait_ge(drained[s], n)
                return slot[s]

            def end(ins, key):
                ins.then_inc(filled[jobs[key][0]], 1)

            def weights(u):
                pe.wait_ge(s_split, 2 * (u + 1))
                return w_h[:, u % 2], w_l[:, u % 2]

            def rows_product(out_ap, ah, al, sl, wh, wl, start=True, stop=True):
                steps = [(a, w, k) for k in range(KC) for a, w in ((ah, wh), (ah, wl), (al, wh))]
                for i, (a, w, k) in enumerate(steps):
                    last = pe.matmul(out_ap, a[:, k, sl], w[:, k, :], start=start and i == 0,
                                     stop=stop and i == len(steps) - 1)
                return last

            def feature_product(out_t, wh, wl, m, ah, al, pieces=PIECES):
                for c0, c1 in pieces:
                    steps = [(a, w, k) for k in range(KC) for a, w in ((ah, wh), (al, wh), (ah, wl))]
                    for i, (a, w, k) in enumerate(steps):
                        last = pe.matmul(out_t[:, c0:c1], w[:, k, m], a[:, k, c0:c1],
                                         start=i == 0, stop=i == len(steps) - 1)
                return last

            def transposes(tag, src_rows, ready):
                for k in range(KC):
                    o_ = begin((tag, k))
                    for t in range(T):
                        if k == 0:
                            ready(t)
                        last = pe.transpose(o_[:, cols(t)], src_rows[0:rows(t), t, k * P:(k + 1) * P],
                                            ident[0:rows(t), 0:rows(t)])
                    end(last, (tag, k))

            def chunk(m):
                return slice(m * P, (m + 1) * P)

            pe.wait_ge(s_setup, 13)
            pe.wait_ge(s_ef, 1)
            o_ = begin("edges")
            for j in range(4):
                last = pe.transpose(o_[0:CE, j * CP:(j + 1) * CP], edge_f[:, j, :], ident[0:CP, 0:CP])
            end(last, "edges")
            pe.wait_ge(s_dg, 4)
            o_ = begin("ranges")
            end(pe.matmul(o_[0:T, 0:2 * CH], ones[0:CP, 0:T], diag[:, :, :], start=True, stop=True), "ranges")

            transposes("xT", rows_b, lambda t: pe.wait_ge(s_rows, t + 1))
            wh, wl = weights(W_NEIGH)
            for k in range(KC):
                wait_drained(pe, ("xT", k))
            for t in range(T):
                end(rows_product(begin(("y", t))[0:rows(t), :], act_h, act_l, cols(t), wh, wl), ("y", t))

            pe.wait_ge(s_span, 1)
            count = pe.alloc_register("pe_chunks")
            pe.reg_mov(count, 0)
            for t in range(T):
                o_ = begin(("hist", t))
                for b in range(3):
                    pe.matmul(o_[:, b * 512:(b + 1) * 512], zero16[:, 0:P], zero16[:, :], start=True, stop=True)
                c_first = pe.value_load(span_i[t:t + 1, 0:1], min_val=0, max_val=CH - 1)
                c_end = pe.value_load(span_i[t:t + 1, 1:2], min_val=1, max_val=CH)
                with pe.Fori(c_first, c_end) as c:
                    pe.reg_add(count, count, 1)
                    ticket = pe.snap(count)
                    pe.wait_ge(s_hot, ticket)
                    buf = pe.snap(ticket & 1)
                    for j in range(T):
                        pe.matmul(o_[:, chunk(j)], hot_src[0:CE, bass.ds(buf * NP + j * P, P)],
                                  hot_dst[0:CE, bass.ds(buf * P, P)], start=False, stop=True,
                                  skip_group_check=True)
                    pe.matmul(o_[:, NP:NP + 1], hot_dst[0:CE, bass.ds(buf * P, P)], ones16[0:CE, 0:1],
                              start=False, stop=True, skip_group_check=True).then_inc(s_hotfree, 1)
                end(pe.matmul(o_[:, NP + 2:NP + 3], zero16[:, 0:P], zero16[:, 0:1], start=False, stop=True,
                              skip_group_check=True), ("hist", t))
                wh, wl = weights(W_SELF)
                end(rows_product(begin(("self", t))[0:rows(t), :], act_h, act_l, cols(t), wh, wl), ("self", t))
                o_ = begin(("agg", t))
                wait_drained(pe, ("hist", t))
                if t == 0:
                    for tt in (T - 2, T - 1):
                        wait_drained(pe, ("y", tt))
                steps = [(a, y, j) for j in range(T) for a, y in ((adj_h, y_h), (adj_h, y_l), (adj_l, y_h))]
                for i, (a, y, j) in enumerate(steps):
                    last = pe.matmul(o_[0:rows(t), :], a[0:rows(j), j * P:j * P + rows(t)], y[0:rows(j), j, :],
                                     start=i == 0, stop=i == len(steps) - 1)
                end(last, ("agg", t))

            qh, ql = weights(W_QT)
            kh, kl = weights(W_KT)
            for m in range(KC):
                end(rows_product(begin(("foldM", m)), qh, ql, chunk(m), kh, kl), ("foldM", m))
            pe.wait_ge(s_bqp, 2)
            o_ = begin("bt")
            for m in range(KC):
                steps = [(w, k) for k in range(KC) for w in (kh, kl)]
                for i, (w, k) in enumerate(steps):
                    last = pe.matmul(o_[:, 2 * m:2 * m + 2], w[:, k, chunk(m)], bq_pair[:, k, :],
                                     start=i == 0, stop=i == len(steps) - 1)
            end(last, "bt")
            for m in range(KC):
                wait_drained(pe, ("foldM", m))
            for m in range(KC):
                end(feature_product(begin(("tT", m)), fold_h, fold_l, chunk(m), act_h, act_l), ("tT", m))
            for m in range(KC):
                wait_drained(pe, ("tT", m))
            for t in range(T):
                o_ = begin(("score", t))
                for c0, c1 in PIECES:
                    steps = [(a, b, k) for k in range(KC) for a, b in ((0, act_h), (0, act_l), (KC, act_h))]
                    for i, (a, b, k) in enumerate(steps):
                        last = pe.matmul(o_[0:rows(t), c0:c1], big[:, a + k, cols(t)], b[:, k, c0:c1],
                                         start=i == 0, stop=i == len(steps) - 1)
                end(last, ("score", t))

            vh, vl = weights(W_VT)
            oh_, ol_ = weights(W_MO)
            for m in range(KC):
                end(rows_product(begin(("foldN", m)), vh, vl, chunk(m), oh_, ol_), ("foldN", m))
            pe.wait_ge(s_bvr, 2 * KC)
            end(rows_product(begin("bvo"), bv_rep_h, bv_rep_l, slice(0, P), oh_, ol_), "bvo")
            pe.wait_ge(s_pfree, T)
            o_ = begin("colsum")
            for t in range(T):
                last = pe.matmul(o_[0:rows(t), t:t + 1], col_acc[:, cols(t)], ones[:, 0:1], start=True, stop=True)
            end(last, "colsum")
            for m in range(KC):
                wait_drained(pe, ("foldN", m))
            for t in range(T):
                end(rows_product(begin(("o", t))[0:rows(t), :], act_h, act_l, cols(t), fold_h, fold_l), ("o", t))

            transposes("uT", rows_b, lambda t: pe.wait_ge(s_rows, T + t + 1))
            for k in range(KC):
                wait_drained(pe, ("uT", k))
            wh, wl = weights(W_V)
            for t in range(T):
                end(rows_product(begin(("v", t))[0:rows(t), :], act_h, act_l, cols(t), wh, wl), ("v", t))
            for i in range(2 * KC):
                wh, wl = weights(W_Q + i // KC)
                end(feature_product(begin(("qk", i)), wh, wl, chunk(i % KC), act_h, act_l), ("qk", i))

            def scores(i):
                h, t = divmod(i, T)
                if t == 0:
                    pe.wait_ge(s_stack[h % 2], 80 * (h // 2 + 1))
                o_ = begin(("S", i))
                b = 3 * (h % 2)
                for c0, c1 in PIECES:
                    for part in range(2):
                        last = pe.matmul(o_[0:rows(t), c0:c1], big[:, b, cols(t)], big[:, b + 1 + part, c0:c1],
                                         start=part == 0, stop=part == 1)
                end(last, ("S", i))

            def turn(i):
                t = i % T
                pe.wait_ge(s_aexp, i + 1)
                o_ = begin(("PT", i))
                for kt in range(T):
                    last = pe.transpose(o_[:, kt * P:kt * P + rows(t)], prob[0:rows(t), i % 2, chunk(kt)],
                                        ident[0:rows(t), 0:rows(t)])
                end(last, ("PT", i))

            def values(i):
                h, t = divmod(i, T)
                wait_drained(pe, ("PT", i))
                if i == 0:
                    pe.wait_ge(s_v3, T)
                o_ = begin(("AV", i))
                for kt in range(T):
                    r = rows(kt)
                    pe.matmul(o_[0:rows(t), 0:3 * DH], pt_h[0:r, i % 2, kt, 0:rows(t)], val[0:r, kt, h, :],
                              start=kt == 0, stop=False, skip_group_check=True)
                    last = pe.matmul(o_[0:rows(t), 0:2 * DH], pt_l[0:r, i % 2, kt, 0:rows(t)],
                                     val[0:r, kt, h, 0:2 * DH], start=False, stop=kt == T - 1,
                                     skip_group_check=True)
                end(last, ("AV", i))

            for i in range(UNITS + 2):
                if i < UNITS:
                    scores(i)
                if i >= 2:
                    values(i - 2)
                if 1 <= i <= UNITS:
                    turn(i - 1)

            wait_drained(pe, ("AV", UNITS - 2))
            wait_drained(pe, ("AV", UNITS - 1))
            transposes("cT", ctx_rows, lambda t: None)
            for k in range(KC):
                wait_drained(pe, ("cT", k))
            wh, wl = weights(W_O)
            for t in range(T):
                end(rows_product(begin(("sa", t))[0:rows(t), :], big[:, 0:KC], big[:, KC:2 * KC], cols(t), wh, wl),
                    ("sa", t))

            transposes("tkT", tok, lambda t: pe.wait_ge(s_tok, t + 1))
            for k in range(KC):
                wait_drained(pe, ("tkT", k))
            pe.wait_ge(s_route, 2)
            end(feature_product(begin("logits"), wg_h, wg_l, slice(0, P), act_h, act_l), "logits")
            o_ = begin("lgrows")
            wait_drained(pe, "logits")
            for t in range(T):
                last = pe.transpose(o_[0:rows(t), t * NE:(t + 1) * NE], lg_t[:, cols(t)], ident[0:NE, 0:NE])
            end(last, "lgrows")
            o_ = begin("ohT")
            pe.wait_ge(s_route, 2 + T)
            for t in range(T):
                last = pe.transpose(o_[0:NE, cols(t)], oh[0:rows(t), t, :], ident[0:rows(t), 0:rows(t)])
            end(last, "ohT")
            wait_drained(pe, "ohT")
            pe.wait_ge(s_route, 2 + T + NE + 2)
            for e in range(NE):
                o_ = begin(("mask", e))
                for c0, c1 in PIECES:
                    last = pe.matmul(o_[:, c0:c1], sel[:, e, :], oh_t[:, c0:c1], start=True, stop=True)
                end(last, ("mask", e))
            for s in slot:
                pe.wait_ge(drained[s], used[s])

            def up(n):
                g, j = divmod(n, KC)
                half = g // (NE // 2)
                wh, wl = weights(UP + 2 * g)
                for p in range(2):
                    r = 2 * n + p
                    if r >= 3:
                        pe.wait_ge(s_gelu, r - 2)
                    c0 = half * HT + p * PW
                    last = feature_product(hbank[r % 3], wh, wl, chunk(j), act_h[:, :, c0:c0 + PW],
                                           act_l[:, :, c0:c0 + PW], pieces=[(0, PW)])
                    last.then_inc(s_hfill[r % 3], 1)

            def down(n):
                g, j = divmod(n, KC)
                half, q = divmod(g, NE // 2)
                first, final = q == 0 and j == 0, q == NE // 2 - 1 and j == KC - 1
                wh, wl = weights(DOWN + 2 * g)
                if first and half:
                    pe.wait_ge(s_yd, T // 2)
                pe.wait_ge(s_hl, 2 * n + 2)
                for i in range(T // 2):
                    t = half * (T // 2) + i
                    o_ = ybank[i][0:rows(t), :]
                    sl = slice(i * P, i * P + rows(t))
                    if first:
                        pe.matmul(o_, oh_t[:, cols(t)], b2_h[:, :], start=True, stop=False)
                        pe.matmul(o_, oh_t[:, cols(t)], b2_l[:, :], start=False, stop=False)
                    for k, (a, w) in enumerate(((hid_h, wh), (hid_h, wl), (hid_l, wh))):
                        last = pe.matmul(o_, a[:, n % 2, sl], w[:, j, :], start=False, stop=final and k == 2)
                last.then_inc(s_hused, 1)

            hbank = [slot["W1"][:, 1024:1536], slot["N0"], slot["N1"]]
            ybank = [slot["W0"][:, 0:512], slot["W0"][:, 512:1024], slot["W0"][:, 1024:1536],
                     slot["W1"][:, 0:512], slot["W1"][:, 512:1024]]
            for n in range(STEPS + 1):
                if n < STEPS:
                    up(n)
                if n:
                    down(n - 1)

        @block.scalar
        def _(act):
            ln_no = [0]

            def sqrt_of_variance():
                ln_no[0] += 1
                act.wait_ge(s_var, ln_no[0])
                act.activation(rs[:, :], ve[:, :], ACT.Sqrt).then_inc(s_sqrt, 1)

            def hi(key, out_ap, in_of, bias=None):
                o_ = wait_filled(act, key)
                if bias is None:
                    act.activation(out_ap, in_of(o_), ACT.Copy).then_inc(s_hi, 1)
                else:
                    act.activation(out_ap, in_of(o_), ACT.Identity, bias=bias).then_inc(s_hi, 1)

            sqrt_of_variance()
            for k in range(KC):
                hi(("xT", k), act_h[:, k, 0:N], lambda o_: o_[:, 0:N])
            for t in range(T):
                hi(("y", t), y_h[0:rows(t), t, :], lambda o_: o_[0:rows(t), :])
            for t in range(T):
                if t:
                    wait_filled(act, ("agg", t - 1))
                hi(("hist", t), adj_h[:, :], lambda o_: o_[:, 0:NP])
            act.wait_ge(s_rowc, 96)
            act.wait_ge(s_var, 2)
            act.activation(tmp[:, 1, 0:D], row_c[:, 4, :], ACT.Sqrt).then_inc(s_sqrt, 1)
            ln_no[0] += 1
            for m in range(KC):
                hi(("foldM", m), fold_h[:, m, :], lambda o_: o_[:, :])
            act.wait_ge(s_const, 96)
            wait_drained(act, "bt")
            wait_filled(act, ("agg", T - 1))
            for m in range(KC):
                hi(("tT", m), big[:, m, :], lambda o_: o_[:, 0:NP], bias=bt[:, m:m + 1])
            for t in range(T):
                act.wait_ge(s_max, t + 1)
                s, _n = jobs[("score", t)]
                if t >= 2:
                    act.wait_ge(s_pfree, t - 1)
                act.activation(prob[0:rows(t), t % 2, 0:N], slot[s][0:rows(t), 0:N], ACT.Exp,
                               bias=nmax[0:rows(t), t:t + 1], accum_out=z_mix[0:rows(t), t:t + 1]) \
                   .then_inc(s_exp, 1)
            for m in range(KC):
                if m == 0:
                    wait_filled(act, ("tT", KC - 1))
                hi(("foldN", m), fold_h[:, m, :], lambda o_: o_[:, :])
            sqrt_of_variance()
            for k in range(KC):
                hi(("uT", k), act_h[:, k, 0:N], lambda o_: o_[:, 0:N])
            for t in range(T):
                r = rows(t)
                v = tmp[0:r, t % 2, 0:D].rearrange("p (h d) -> p h d", h=NH)
                act.wait_ge(s_v32, t + 1)
                act.activation(val[0:r, t, :, 0:DH], v, ACT.Copy).then_inc(s_v1, 1)
                act.wait_ge(s_v2r, t + 1)
                act.activation(val[0:r, t, :, DH:2 * DH], v, ACT.Copy).then_inc(s_v2, 1)
            for i in range(2 * KC):
                c = cols_c[:, 2 * KC + i:2 * KC + i + 1]
                if i >= 4:
                    act.wait_ge(s_store[i % 4], 64)
                if i == 0:
                    wait_drained(act, ("uT", KC - 1))
                    act.wait_ge(s_bq8, 1)
                hi(("qk", i), big[:, i % KC, :], lambda o_: o_[:, 0:NP], bias=c)
            for i in range(UNITS + 1):
                if i < UNITS:
                    r = rows(i % T)
                    act.wait_ge(s_amax, i + 1)
                    if i == 0:
                        act.wait_ge(s_pads, 1)
                    if i >= 2:
                        wait_filled(act, ("PT", i - 2))
                        wait_drained(act, ("AV", i - 2))
                    act.activation(prob[0:r, i % 2, 0:N], slot["W0"][0:r, 0:N], ACT.Exp,
                                   bias=nm[0:r, i % 2:i % 2 + 1], accum_out=zz[0:r, i % 2:i % 2 + 1]) \
                       .then_inc(s_aexp, 1)
                if i:
                    j = i - 1
                    r = rows(j % T)
                    o_ = wait_filled(act, ("PT", j))
                    if j >= 2:
                        wait_filled(act, ("AV", j - 2))
                    act.activation(pt_h[:, j % 2, :, 0:r],
                                   o_[:, 0:NP].rearrange("p (a b) -> p a b", b=P)[:, :, 0:r], ACT.Copy) \
                       .then_inc(s_aptr, 1)
            wait_filled(act, ("S", UNITS - 1))
            for k in range(KC):
                hi(("cT", k), big[:, k, 0:N], lambda o_: o_[:, 0:N])
            sqrt_of_variance()
            act.wait_ge(s_pads, 2)
            for k in range(KC):
                hi(("tkT", k), act_h[:, k, 0:N], lambda o_: o_[:, 0:N])
            for e in range(NE):
                o_ = wait_filled(act, ("mask", e))
                act.activation(mask[:, e, :], o_[:, 0:NP], ACT.Copy).then_inc(drained[jobs[("mask", e)][0]], 1)

            hbank = [slot["W1"][:, 1024:1536], slot["N0"], slot["N1"]]
            for r in range(2 * STEPS + 1):
                if r < 2 * STEPS:
                    n = r // 2
                    g, j = divmod(n, KC)
                    ft = (g % (NE // 2)) * KC + j
                    act.wait_ge(s_hfill[r % 3], r // 3 + 1)
                    if r >= 2:
                        act.wait_ge(s_hm, r - 1)
                    act.activation(tmp[:, 0, (r % 2) * PW:(r % 2 + 1) * PW], hbank[r % 3][:, 0:PW], ACT.Gelu,
                                   bias=c_b1[:, ft:ft + 1]).then_inc(s_gelu, 1)
                if r:
                    q_ = r - 1
                    act.wait_ge(s_hm, q_ + 1)
                    if q_ >= 4:
                        act.wait_ge(s_hused, q_ // 2 - 1)
                    act.activation(hid_h[:, (q_ // 2) % 2, (q_ % 2) * PW:(q_ % 2 + 1) * PW],
                                   tmp[:, 1, (q_ % 2) * PW:(q_ % 2 + 1) * PW], ACT.Copy).then_inc(s_hh, 1)
            sqrt_of_variance()

        @block.vector
        def _(dve):
            chain, his, sq = [0], [0], [0]

            def step(ins):
                ins.then_inc(s_step, 1)
                chain[0] += 1
                dve.wait_ge(s_step, chain[0])

            def lo(key, out_ap, in_of, hi_ap, bias=None):
                o_ = slot[jobs[key][0]]
                his[0] += 1
                dve.wait_ge(s_hi, his[0])
                if bias is None:
                    ins = dve.tensor_tensor(out_ap, in_of(o_), hi_ap.bitcast(F32), ALU.subtract)
                else:
                    ins = dve.scalar_tensor_tensor(out_ap, in_of(o_), bias, hi_ap.bitcast(F32), ALU.add,
                                                   ALU.subtract)
                ins.then_inc(drained[jobs[key][0]], 1)

            def inverse_root(var, root, out_ap, work):
                step(dve.reciprocal(out_ap, root))
                step(dve.tensor_tensor(work, out_ap, out_ap, ALU.mult))
                step(dve.tensor_tensor(work, work, var, ALU.mult))
                step(dve.tensor_scalar(work, work, -0.5, 1.5, ALU.mult, ALU.add))
                step(dve.tensor_tensor(out_ap, out_ap, work, ALU.mult))

            def moments(t, row_ap):
                step(dve.bn_stats(st6[0:rows(t), 0, :], row_ap))
                step(dve.bn_aggr(mv[0:rows(t), t, :], st6[0:rows(t), 0, :]))

            def finish_moments():
                dve.tensor_scalar(ve[:, :], mv[:, :, 1], LN_EPS, None, ALU.add).then_inc(s_var, 1)
                sq[0] += 1
                dve.wait_ge(s_var, sq[0])
                dve.wait_ge(s_sqrt, sq[0])
                inverse_root(ve[:, :], rs[:, :], rs[:, :], nr[:, :])

            def normalise(out_ap, in_ap, t):
                r = rows(t)
                return dve.tensor_scalar(out_ap, in_ap, mv[0:r, t, 0:1], rs[0:r, t:t + 1], ALU.subtract, ALU.mult)

            dve.wait_ge(s_edge, 32)
            dve.tensor_copy(edge_f[:, :, :], edge_i[:, :, :]).then_inc(s_ef, 1)
            dve.wait_ge(s_ef, 1)
            step(dve.tensor_reduce(lohi[:, 0:2], edge_f[:, 2:4, :], AX.X, ALU.min))
            step(dve.tensor_reduce(lohi[:, 2:4], edge_f[:, 2:4, :], AX.X, ALU.max))
            dve.wait_ge(s_setup, 13)
            for j in range(4):
                dve.tensor_scalar(diag[:, j, :], ident[0:CP, 0:CP], lohi[:, j:j + 1], None, ALU.mult).then_inc(s_dg, 1)
            o_ = wait_filled(dve, "edges")
            dve.tensor_copy(edge_t[:, :], o_[0:CE, 0:2 * CH]).then_inc(drained["N0"], 1)
            o_ = wait_filled(dve, "ranges")
            step(dve.tensor_scalar(cover2[:, :], o_[0:T, 0:CH], tile_lo[:, 1:2], None, ALU.is_le))
            step(dve.scalar_tensor_tensor(cover[:, :], o_[0:T, CH:2 * CH], tile_lo[:, 0:1], cover2[:, :], ALU.is_ge,
                                          ALU.mult))
            step(dve.scalar_tensor_tensor(cover2[:, :], cover[:, :], -BIG, chunk_no[:, :], ALU.mult, ALU.add))
            step(dve.tensor_reduce(span[:, 0:1], cover2[:, :], AX.X, ALU.min))
            step(dve.tensor_scalar(span[:, 0:1], span[:, 0:1], BIG, CH - 1.0, ALU.add, ALU.min))
            step(dve.scalar_tensor_tensor(cover2[:, :], chunk_no[:, :], 1.0, cover[:, :], ALU.add, ALU.mult))
            step(dve.tensor_reduce(span[:, 1:2], cover2[:, :], AX.X, ALU.max))
            step(dve.tensor_scalar(span[:, 2:3], span[:, 0:1], 1.0, None, ALU.add))
            dve.tensor_tensor(span[:, 1:2], span[:, 1:2], span[:, 2:3], ALU.max).then_inc(drained["N1"], 1)
            wait_drained(dve, "ranges")
            dve.tensor_copy(span_i[:, :], span[:, 0:2]).then_inc(s_span, 1)

            for t in range(T):
                dve.wait_ge(s_x[t], 16)
                moments(t, acc[0:rows(t), t, :])
            finish_moments()
            for t in range(T):
                r = rows(t)
                normalise(rows_b[0:r, t, :], acc[0:r, t, :], t).then_inc(s_rows, 1)
                dve.wait_ge(s_rows, t + 1)
                dve.tensor_tensor(acc[0:r, t, :], acc[0:r, t, :], rows_b[0:r, t, :], ALU.add).then_inc(s_step, 1)
                chain[0] += 1
            for k in range(KC):
                lo(("xT", k), act_l[:, k, 0:N], lambda o_: o_[:, 0:N], act_h[:, k, 0:N])
            for t in range(T):
                r = rows(t)
                if t == 0:
                    dve.wait_ge(s_step, chain[0])
                lo(("y", t), y_l[0:r, t, :], lambda o_: o_[0:r, :], y_h[0:r, t, :])

            dve.wait_ge(s_rowc, 96)
            dve.wait_ge(s_span, 1)
            count = dve.alloc_register("dve_chunks")
            dve.reg_mov(count, 0)
            for t in range(T):
                r = rows(t)
                c_first = dve.value_load(span_i[t:t + 1, 0:1], min_val=0, max_val=CH - 1)
                c_end = dve.value_load(span_i[t:t + 1, 1:2], min_val=1, max_val=CH)
                with dve.Fori(c_first, c_end) as c:
                    dve.reg_add(count, count, 1)
                    ticket = dve.snap(count)
                    dve.wait_ge(s_hotfree, ticket)
                    buf = dve.snap(ticket & 1)
                    dve.tensor_scalar(hot_src[0:CE, bass.ds(buf * NP, NP)], iota16[0:CE, :],
                                      edge_t[:, bass.ds(c, 1)], None, ALU.is_equal)
                    dve.tensor_scalar(hot_dst[0:CE, bass.ds(buf * P, P)], iota16[0:CE, t * P:(t + 1) * P],
                                      edge_t[:, bass.ds(c + CH, 1)], None, ALU.is_equal).then_inc(s_hot, 1)
                o_ = wait_filled(dve, ("hist", t))
                dve.wait_ge(s_hi, his[0] + 1)
                step(dve.tensor_scalar(nr[:, 0:1], o_[:, NP:NP + 1], 1.0, None, ALU.max))
                step(dve.reciprocal(rdeg[:, t:t + 1], nr[:, 0:1]))
                if t:
                    wait_filled(dve, ("agg", t - 1))
                lo(("hist", t), adj_l[:, :], lambda o_: o_[:, 0:NP], adj_h[:, :])
                o_ = wait_filled(dve, ("self", t))
                own = work1[0:r, :]
                dve.tensor_tensor(own, o_[0:r, :], row_c[0:r, 0, :], ALU.add).then_inc(drained["N0"], 1)
                wait_drained(dve, ("self", t))
                o_ = wait_filled(dve, ("agg", t))
                dve.scalar_tensor_tensor(own, o_[0:r, :], rdeg[0:r, t:t + 1], own, ALU.mult, ALU.add) \
                   .then_inc(drained["N1"], 1)
                wait_drained(dve, ("agg", t))
                step(dve.scalar_tensor_tensor(acc[0:r, t, :], own, 0.0, acc[0:r, t, :], ALU.max, ALU.add))

            dve.tensor_scalar(row_c[:, 4, :], row_c[:, 4, :], LN_EPS, None, ALU.add).then_inc(s_var, 1)
            sq[0] += 1
            dve.wait_ge(s_var, sq[0])
            dve.wait_ge(s_sqrt, sq[0])
            inverse_root(row_c[:, 4, :], tmp[:, 1, 0:D], tmp[:, 1, 0:D], tmp[:, 1, D:2 * D])
            step(dve.tensor_tensor(row_c[:, 1, :], row_c[:, 1, :], tmp[:, 1, 0:D], ALU.mult))
            step(dve.tensor_tensor(row_c[:, 5, :], row_c[:, 5, :], row_c[:, 3, :], ALU.subtract))
            step(dve.tensor_tensor(row_c[:, 5, :], row_c[:, 5, :], row_c[:, 1, :], ALU.mult))
            step(dve.tensor_tensor(row_c[:, 5, :], row_c[:, 5, :], row_c[:, 2, :], ALU.add))
            dve.wait_ge(s_const, 96)
            dve.tensor_copy(bq_pair[:, :, 0], c_mbq).then_inc(s_bqp, 1)
            dve.wait_ge(s_bqp, 1)
            dve.tensor_tensor(bq_pair[:, :, 1], c_mbq, bq_pair[:, :, 0].bitcast(F32), ALU.subtract).then_inc(s_bqp, 1)
            for k in range(KC):
                dve.tensor_scalar(bv_rep_h[:, k, :], ones[:, :], c_mbv[:, k:k + 1], None, ALU.mult).then_inc(s_bvr, 1)
                dve.wait_ge(s_bvr, 2 * k + 1)
                dve.scalar_tensor_tensor(bv_rep_l[:, k, :], ones[:, :], c_mbv[:, k:k + 1],
                                         bv_rep_h[:, k, :].bitcast(F32), ALU.mult, ALU.subtract).then_inc(s_bvr, 1)
            dve.tensor_scalar(c_fbq, c_fbq, DH ** -0.5, None, ALU.mult).then_inc(s_bq8, 1)
            for m in range(KC):
                lo(("foldM", m), fold_l[:, m, :], lambda o_: o_[:, :], fold_h[:, m, :])
            o_ = wait_filled(dve, "bt")
            dve.tensor_reduce(bt[:, :], o_[:, 0:2 * KC].rearrange("p (m b) -> p m b", b=2), AX.X, ALU.add) \
               .then_inc(drained["N0"], 1)
            for m in range(KC):
                if m == 0:
                    wait_drained(dve, "bt")
                lo(("tT", m), big[:, KC + m, :], lambda o_: o_[:, 0:NP], big[:, m, :], bias=bt[:, m:m + 1])

            def column_sums(t):
                r = rows(t)
                dve.wait_ge(s_exp, t + 1)
                step(dve.reciprocal(zt[0:r, t:t + 1], z_mix[0:r, t:t + 1]))
                if t == 0:
                    ins = dve.tensor_scalar(col_acc[0:r, 0:N], prob[0:r, t % 2, 0:N], zt[0:r, t:t + 1], None, ALU.mult)
                else:
                    ins = dve.scalar_tensor_tensor(col_acc[0:r, 0:N], prob[0:r, t % 2, 0:N], zt[0:r, t:t + 1],
                                                   col_acc[0:r, 0:N], ALU.mult, ALU.add)
                ins.then_inc(s_pfree, 1)
                dve.wait_ge(s_pfree, t + 1)

            for t in range(T):
                r = rows(t)
                o_ = wait_filled(dve, ("score", t))
                dve.tensor_reduce(nmax[0:r, t:t + 1], o_[0:r, 0:N], AX.X, ALU.max, negate=True).then_inc(s_max, 1)
                dve.wait_ge(s_exp, t + 1)
                dve.wait_ge(s_max, t + 1)
                dve.engine_nop().then_inc(drained[jobs[("score", t)][0]], 1)
                column_sums(t)
            for m in range(KC):
                lo(("foldN", m), fold_l[:, m, :], lambda o_: o_[:, :], fold_h[:, m, :])
            o_ = wait_filled(dve, "bvo")
            dve.tensor_copy(row_c[:, 3, :], o_[:, :]).then_inc(drained["N0"], 1)
            wait_drained(dve, "bvo")
            o_ = wait_filled(dve, "colsum")
            last_r = rows(T - 1)
            step(dve.tensor_scalar(nr[:, 0:T - 1], o_[:, 0:T - 1], 1e-9, None, ALU.add))
            step(dve.tensor_scalar(nr[0:last_r, T - 1:T], o_[0:last_r, T - 1:T], 1e-9, None, ALU.add))
            step(dve.reciprocal(zt[:, 0:T - 1], nr[:, 0:T - 1]))
            step(dve.reciprocal(zt[0:last_r, T - 1:T], nr[0:last_r, T - 1:T]))
            step(dve.tensor_tensor(cfac[:, 0:T - 1], o_[:, 0:T - 1], zt[:, 0:T - 1], ALU.mult))
            dve.tensor_tensor(cfac[0:last_r, T - 1:T], o_[0:last_r, T - 1:T], zt[0:last_r, T - 1:T], ALU.mult) \
               .then_inc(drained["N1"], 1)
            wait_drained(dve, "colsum")
            for t in range(T):
                r = rows(t)
                o_ = wait_filled(dve, ("o", t))
                own = work1[0:r, :]
                dve.tensor_tensor(own, o_[0:r, :], row_c[0:r, 3, :], ALU.add).then_inc(drained[jobs[("o", t)][0]], 1)
                wait_drained(dve, ("o", t))
                step(dve.scalar_tensor_tensor(own, own, cfac[0:r, t:t + 1], row_c[0:r, 1, :], ALU.mult, ALU.mult))
                step(dve.tensor_tensor(own, own, row_c[0:r, 5, :], ALU.add))
                dve.scalar_tensor_tensor(acc[0:r, t, :], own, 0.0, acc[0:r, t, :], ALU.max, ALU.add) \
                   .then_inc(s_mixdone, 1)
                dve.wait_ge(s_mixdone, t + 1)

            for t in range(T):
                moments(t, acc[0:rows(t), t, :])
            finish_moments()
            for t in range(T):
                r = rows(t)
                normalise(rows_b[0:r, t, :], acc[0:r, t, :], t).then_inc(s_rows, 1)
            for k in range(KC):
                lo(("uT", k), act_l[:, k, 0:N], lambda o_: o_[:, 0:N], act_h[:, k, 0:N])
            dve.wait_ge(s_ffnrow, 96)
            for t in range(T):
                r = rows(t)
                v = tmp[0:r, t % 2, 0:D]
                vh = v.rearrange("p (h d) -> p h d", h=NH)
                o_ = wait_filled(dve, ("v", t))
                if t >= 2:
                    dve.wait_ge(s_v3, t - 1)
                dve.tensor_tensor(v, o_[0:r, :], row_c[0:r, 0, :], ALU.add).then_inc(drained[jobs[("v", t)][0]], 1)
                wait_drained(dve, ("v", t))
                dve.engine_nop().then_inc(s_v32, 1)
                dve.wait_ge(s_v1, t + 1)
                dve.tensor_tensor(vh, vh, val[0:r, t, :, 0:DH], ALU.subtract).then_inc(s_v2r, 1)
                dve.wait_ge(s_v2r, t + 1)
                dve.wait_ge(s_v2, t + 1)
                dve.tensor_tensor(val[0:r, t, :, 2 * DH:3 * DH], vh, val[0:r, t, :, DH:2 * DH], ALU.subtract) \
                   .then_inc(s_v3, 1)
            for i in range(2 * KC):
                if i >= 4:
                    dve.wait_ge(s_store[i % 4], 64)
                lo(("qk", i), big[:, KC + i % KC, :], lambda o_: o_[:, 0:NP], big[:, i % KC, :],
                   bias=cols_c[:, 2 * KC + i:2 * KC + i + 1])
            dve.wait_ge(s_v3, T)
            dve.memset(prob[:, :, N:NP], 0.0).then_inc(s_pads, 1)

            for i in range(UNITS + 2):
                if i < UNITS:
                    r = rows(i % T)
                    o_ = wait_filled(dve, ("S", i))
                    if i >= 2:
                        dve.wait_ge(s_aexp, i - 1)
                    dve.tensor_reduce(nm[0:r, i % 2:i % 2 + 1], o_[0:r, 0:N], AX.X, ALU.max, negate=True) \
                       .then_inc(s_amax, 1)
                if i >= 2:
                    j = i - 2
                    h, t = divmod(j, T)
                    r = rows(t)
                    o_ = wait_filled(dve, ("AV", j))
                    dve.wait_ge(s_aexp, j + 1)
                    step(dve.reciprocal(rz[0:r, 0:1], zz[0:r, j % 2:j % 2 + 1]))
                    step(dve.tensor_reduce(cten[0:r, :], o_[0:r, 0:3 * DH].rearrange("p (g d) -> p d g", g=3), AX.X,
                                           ALU.add))
                    dve.tensor_scalar(ctx_rows[0:r, t, h * DH:(h + 1) * DH], cten[0:r, :], rz[0:r, 0:1], None,
                                      ALU.mult).then_inc(drained[jobs[("AV", j)][0]], 1)
                    wait_drained(dve, ("AV", j))
                if i < UNITS:
                    dve.wait_ge(s_aexp, i + 1)
                    dve.wait_ge(s_amax, i + 1)
                    dve.engine_nop().then_inc(drained["W0"], 1)
                if 1 <= i <= UNITS:
                    j = i - 1
                    r = rows(j % T)
                    o_ = wait_filled(dve, ("PT", j))
                    dve.wait_ge(s_aptr, j + 1)
                    dve.tensor_tensor(pt_l[:, j % 2, :, 0:r],
                                      o_[:, 0:NP].rearrange("p (a b) -> p a b", b=P)[:, :, 0:r],
                                      pt_h[:, j % 2, :, 0:r], ALU.subtract).then_inc(drained["W1"], 1)

            for k in range(KC):
                lo(("cT", k), big[:, KC + k, 0:N], lambda o_: o_[:, 0:N], big[:, k, 0:N])
            for t in range(T):
                r = rows(t)
                own = tmp[0:r, 0, 0:D]
                step(normalise(own, acc[0:r, t, :], t))
                step(dve.tensor_tensor(own, own, row_c[0:r, 1, :], ALU.add))
                o_ = wait_filled(dve, ("sa", t))
                dve.tensor_tensor(tok[0:r, t, :], o_[0:r, :], own, ALU.add).then_inc(drained[jobs[("sa", t)][0]], 1)
                wait_drained(dve, ("sa", t))
            for t in range(T):
                moments(t, tok[0:rows(t), t, :])
            finish_moments()
            for t in range(T):
                r = rows(t)
                step(normalise(tok[0:r, t, :], tok[0:r, t, :], t))
                step(dve.tensor_tensor(tok[0:r, t, :], tok[0:r, t, :], row_c[0:r, 2, :], ALU.mult))
                dve.tensor_tensor(tok[0:r, t, :], tok[0:r, t, :], row_c[0:r, 3, :], ALU.add).then_inc(s_tok, 1)
            wait_filled(dve, ("cT", KC - 1))
            dve.memset(act_h[:, :, N:NP].bitcast(F32), 0.0).then_inc(s_pads, 1)
            wait_filled(dve, ("sa", T - 1))
            dve.memset(wg_f[:, :, :], 0.0).then_inc(s_pads, 1)
            for k in range(KC):
                lo(("tkT", k), act_l[:, k, 0:N], lambda o_: o_[:, 0:N], act_h[:, k, 0:N])
            dve.wait_ge(s_wg, 16)
            dve.tensor_copy(wg_h[:, :, :], wg_f[:, :, :]).then_inc(s_route, 1)
            dve.wait_ge(s_route, 1)
            dve.tensor_tensor(wg_l[:, :, :], wg_f[:, :, :], wg_h[:, :, :].bitcast(F32), ALU.subtract).then_inc(s_route, 1)
            o_ = wait_filled(dve, "logits")
            dve.tensor_scalar(lg_t[:, :], o_[0:NE, 0:NP], c_bg, None, ALU.add).then_inc(drained["W0"], 1)
            o_ = wait_filled(dve, "lgrows")
            step(dve.tensor_copy(lg[:, 0:T - 1, :], o_[:, 0:(T - 1) * NE].rearrange("p (t e) -> p t e", e=NE)))
            dve.tensor_copy(lg[0:last_r, T - 1, :], o_[0:last_r, (T - 1) * NE:T * NE]).then_inc(drained["N0"], 1)
            wait_drained(dve, "lgrows")
            for t in range(T):
                r = rows(t)
                step(dve.max(m8[0:r, t, :], lg[0:r, t, :]))
                step(dve.max_index(ix[0:r, t, :], m8[0:r, t, :], lg[0:r, t, :]))
                step(dve.tensor_copy(ixf[0:r, t:t + 1], ix[0:r, t, 0:1]))
                dve.tensor_scalar(oh[0:r, t, :], iota8[0:r, :], ixf[0:r, t:t + 1], None, ALU.is_equal).then_inc(s_route, 1)
            step(dve.memset(oh_t[:, N:NP].bitcast(F32), 0.0))
            o_ = wait_filled(dve, "ohT")
            dve.tensor_copy(oh_t[:, 0:N], o_[0:NE, 0:N]).then_inc(drained["W1"], 1)
            for e in range(NE):
                dve.tensor_scalar(sel[:, e, :], ones[0:NE, :], ident[0:NE, e:e + 1], None, ALU.mult).then_inc(s_route, 1)
            dve.wait_ge(s_b2, 16)
            dve.tensor_copy(b2_h[:, :], b2_f[:, :]).then_inc(s_route, 1)
            dve.wait_ge(s_route, 2 + T + NE + 1)
            dve.tensor_tensor(b2_l[:, :], b2_f[:, :], b2_h[:, :].bitcast(F32), ALU.subtract).then_inc(s_route, 1)
            for s in ("W0", "W1"):
                dve.wait_ge(drained[s], used[s])

            def fold_in(i, half):
                t = half * (T // 2) + i
                r = rows(t)
                dve.tensor_tensor(tok[0:r, t, :], ybank[i][0:r, :], tok[0:r, t, :], ALU.add).then_inc(s_yd, 1)

            ybank = [slot["W0"][:, 0:512], slot["W0"][:, 512:1024], slot["W0"][:, 1024:1536],
                     slot["W1"][:, 0:512], slot["W1"][:, 512:1024]]
            for r in range(2 * STEPS + 1):
                if r < 2 * STEPS:
                    g, j = divmod(r // 2, KC)
                    half, q = divmod(g, NE // 2)
                    e = 2 * q + j // 2
                    c0 = half * HT + (r % 2) * PW
                    dve.wait_ge(s_gelu, r + 1)
                    if r >= 2:
                        dve.wait_ge(s_hl, r - 1)
                    dve.tensor_tensor(tmp[:, 1, (r % 2) * PW:(r % 2 + 1) * PW], tmp[:, 0, (r % 2) * PW:(r % 2 + 1) * PW],
                                      mask[:, e, c0:c0 + PW], ALU.mult).then_inc(s_hm, 1)
                if r:
                    q_ = r - 1
                    sl = slice((q_ % 2) * PW, (q_ % 2 + 1) * PW)
                    dve.wait_ge(s_hh, q_ + 1)
                    dve.tensor_tensor(hid_l[:, (q_ // 2) % 2, sl], tmp[:, 1, sl],
                                      hid_h[:, (q_ // 2) % 2, sl].bitcast(F32), ALU.subtract).then_inc(s_hl, 1)
                if r == STEPS + 1:
                    dve.wait_ge(s_hused, STEPS // 2)
                    for i in range(T // 2):
                        fold_in(i, 0)
            dve.wait_ge(s_hused, STEPS)
            for i in range(T // 2):
                fold_in(i, 1)
            dve.wait_ge(s_yd, T)
            for t in range(T):
                moments(t, tok[0:rows(t), t, :])
            finish_moments()
            for t in range(T):
                r = rows(t)
                step(normalise(tok[0:r, t, :], tok[0:r, t, :], t))
                step(dve.tensor_tensor(tok[0:r, t, :], tok[0:r, t, :], row_c[0:r, 4, :], ALU.mult))
                step(dve.tensor_tensor(tok[0:r, t, :], tok[0:r, t, :], row_c[0:r, 5, :], ALU.add))
                dve.tensor_tensor(tok[0:r, t, :], tok[0:r, t, :], acc[0:r, t, :], ALU.add).then_inc(s_fin, 1)


_INS = ["x", "src", "dst", "w_all", "mix_bq", "mix_bv", "mix_rows", "ffn_bq", "ffn_bk", "ffn_rows",
        "wg", "bg", "b1", "b2"]


def kernel(**inputs):
    import numpy as np
    import concourse.bacc as bacc
    from concourse.bass_utils import run_bass_kernel_spmd

    a = {k: np.asarray(v) for k, v in inputs.items()}

    def chunked(w):
        return np.ascontiguousarray(w.reshape(KC, P, -1).transpose(1, 0, 2))

    def column(b):
        return np.ascontiguousarray(b.reshape(-1, P).T)

    m, f = "L0_mix_", "L0_ffn_"
    units = [a["L0_gnn_W_neigh"].T, a["L0_gnn_W_self"].T, a[m + "Wq"].T, a[m + "Wk"].T, a[m + "Wv"].T,
             a[m + "Wo"], a[f + "Wv"], a[f + "Wq"], a[f + "Wk"], a[f + "Wo"]]
    for q in range(NE // 2):
        units.append(a[f + "W1"][2 * q:2 * q + 2].transpose(1, 0, 2).reshape(D, 2 * HID))
        units.append(a[f + "W2"][2 * q:2 * q + 2].reshape(2 * HID, D))
    arrays = {
        "x": a["x"], "src": a["src"], "dst": a["dst"],
        "w_all": np.stack([chunked(w) for w in units]),
        "mix_bq": column(a[m + "bq"]), "mix_bv": column(a[m + "bv"]),
        "mix_rows": np.stack([a["L0_gnn_b"], a[m + "bn_scale"], a[m + "bn_bias"], a[m + "bn_mean"],
                              a[m + "bn_var"], a[m + "bo"]]),
        "ffn_bq": column(a[f + "bq"]), "ffn_bk": column(a[f + "bk"]),
        "ffn_rows": np.stack([a[f + "bv"], a[f + "bo"], a[f + "g1"], a[f + "beta1"], a[f + "g2"], a[f + "beta2"]]),
        "wg": chunked(a[f + "Wg"]), "bg": a[f + "bg"].reshape(NE, 1),
        "b1": column(a[f + "b1"]), "b2": a[f + "b2"],
    }
    nc = bacc.Bacc("TRN2", target_bir_lowering=False, num_devices=1)
    args = []
    for name in _INS:
        arrays[name] = np.ascontiguousarray(arrays[name])
        args.append(nc.dram_tensor("in_" + name, arrays[name].shape, mybir.dt.from_np(arrays[name].dtype),
                                   kind="ExternalInput").ap())
    args.append(nc.dram_tensor("out_rows", (N, D), F32, kind="ExternalOutput").ap())
    gps_layer(nc, *args)
    r = run_bass_kernel_spmd(nc, [{"in_" + k: v for k, v in arrays.items()}], core_ids=[0])
    return r.results[0]["out_rows"]
```

```python
import concourse.bass as bass
from concourse import mybir
from contextlib import ExitStack

F32 = mybir.dt.float32
F32R = mybir.dt.float32r
BF16 = mybir.dt.bfloat16
F16 = mybir.dt.float16
I32 = mybir.dt.int32
U32 = mybir.dt.uint32
ALU = mybir.AluOpType
ACT = mybir.ActivationFunctionType
AX = mybir.AxisListType

N, D, E = 1250, 512, 20000
P = 128
T = -(-N // P)
NP = T * P
KC = D // P
PIECES = [(0, 512), (512, 1024), (1024, NP)]
COUNT_PIECES = [(0, 512), (512, 1024), (1024, NP + 2)]
CE = 125
CH = E // CE
CP = CH // 2
NH, DH = 8, 64
NE, HID = 8, 256
UNITS = NH * T
LN_EPS = 1e-5
BIG = 10000.0


def rows(t):
    return min(P, N - t * P)


def cols(t):
    return slice(t * P, t * P + rows(t))


def gps_layer(nc, x, src, dst, w_all, mix_bq, mix_bv, mix_rows, ffn_bq, ffn_bk, ffn_rows,
              wg, bg, b1, b2, out):
    ctx = ExitStack()
    with ctx:
        arena = ctx.enter_context(nc.sbuf_tensor("arena", [P, 212480 // 4], F32))
        base = (nc.sbuf_base - 212480)
        at = [base + (-base) % 32]

        def place(name, shape, dt, offset):
            return nc.alloc_sbuf_tensor_at(name, shape, dt, offset=offset)

        def region(size):
            o = at[0]
            at[0] += -(-size // 32) * 32
            return o

        r_act, r_b, r_w, r_stage = region(40960), region(40960), region(32768), region(8192)
        r_acc, r_p, r_rows, r_over = region(20480), region(10240), region(12288), region(40960)

        def small(name, shape, dt):
            n = 1
            for s in shape[1:]:
                n *= s
            return place(name, shape, dt, region(n * mybir.dt.size(dt)))

        act_h = place("act_h", [P, KC, NP], F32R, r_act)
        act_l = place("act_l", [P, KC, NP], F32R, r_act + 20480)
        ctx_rows = place("ctx_rows", [P, T, D], F32, r_act)
        big = place("big", [P, 2 * KC, NP], F32R, r_b)
        y_h = place("y_h", [P, T, D], F32R, r_b)
        y_l = place("y_l", [P, T, D], F32R, r_b + 20480)
        rows_b = place("rows_b", [P, T, D], F32, r_b)
        mask = place("mask", [P, NE, NP], BF16, r_b)
        w_h = place("w_h", [P, 2, KC, D], F32R, r_w)
        w_l = place("w_l", [P, 2, KC, D], F32R, r_w + 16384)
        stage = place("stage", [P, KC, D], F32, r_stage)
        acc = place("acc", [P, T, D], F32, r_acc)
        prob = place("prob", [P, 2, NP], F32, r_p)
        adj_h = place("adj_h", [P, NP], F32R, r_p)
        adj_l = place("adj_l", [P, NP], F32R, r_p + 5120)
        tmp = place("tmp", [P, 2, NP], F32, r_p)
        row_c = place("row_c", [P, 6, D], F32, r_rows)
        fold_h = place("fold_h", [P, KC, D], F32R, r_over)
        fold_l = place("fold_l", [P, KC, D], F32R, r_over + 8192)
        o = r_over + 16384
        col_acc = place("col_acc", [P, NP], F32, o)
        counts = place("counts", [P, NP + 2], F32, o); o += 5152
        hot_src = place("hot_src", [P, 2, NP + 2], BF16, o); o += 5152
        hot_dst = place("hot_dst", [P, 2, P], BF16, o); o += 512
        iota16 = place("iota16", [P, NP], F16, o); o += 2560
        bv_rep_h = place("bv_rep_h", [P, KC, P], F32R, o); o += 2048
        bv_rep_l = place("bv_rep_l", [P, KC, P], F32R, o); o += 2048
        edge_i = place("edge_i", [CP, 4, CE], I32, o)
        edge_f = place("edge_f", [CP, 4, CE], F32, o + 2016); o += 4032
        work1 = place("work1", [P, D], F32, o); o += 2048
        assert o <= r_over + 40960
        val = place("val", [P, T, NH, 3 * DH], BF16, r_over)
        pt_h = place("pt_h", [P, 2, T, P], F16, r_over + 30720)
        pt_l = place("pt_l", [P, 2, T, P], F16, r_over + 35840)
        tok = place("tok", [P, T, D], F32, r_over)
        hid_h = place("hid_h", [P, 2, 640], F32R, r_over + 30720)
        hid_l = place("hid_l", [P, 2, 640], F32R, r_over + 35840)
        ident = small("ident", [P, P], F32)
        ones = small("ones", [P, P], F32)
        zero16 = small("zero16", [P, D], BF16)
        edge_t = small("edge_t", [CE, 2, CH + 1], F32)
        lohi = small("lohi", [CP, 4], F32)
        mv = small("mv", [P, T, 2], F32)
        st6 = small("st6", [P, 2, 6], F32)
        ve = small("ve", [P, T], F32)
        rs = small("rs", [P, T], F32)
        nr = small("nr", [P, T], F32)
        rdeg = small("rdeg", [P, T], F32)
        z_mix = small("z_mix", [P, T], F32)
        nmax = small("nmax", [P, T], F32)
        cfac = small("cfac", [P, T], F32)
        zt = small("zt", [P, T], F32)
        nm = small("nm", [P, 2], F32)
        zz = small("zz", [P, 2], F32)
        rz = small("rz", [P, 2], F32)
        cols_c = small("cols_c", [P, 4 * KC + 16 + 1], F32)
        bq_pair = small("bq_pair", [P, KC, 2], F32R)
        bt = small("bt", [P, KC], F32)
        tile_lo = small("tile_lo", [T, 2], F32)
        span = small("span", [T, 4], F32)
        span_i = small("span_i", [T, 2], I32)
        diag = place("diag", [CP, 4, CP], F32, r_w)
        cover = place("cover", [T, CH], F32, r_w + 1280)
        cover2 = place("cover2", [T, CH], F32, r_w + 1920)
        chunk_no = place("chunk_no", [T, CH], F32, r_w + 2560)
        wg_h = place("wg_h", [P, KC, P], F32R, r_b + 20480)
        wg_l = place("wg_l", [P, KC, P], F32R, r_b + 22528)
        wg_f = place("wg_f", [P, KC, P], F32, r_b + 24576)
        lg_t = place("lg_t", [NE, NP], F32, r_b + 26624)
        oh_t = place("oh_t", [NE, NP], F32R, r_b + 31744)
        b2_f = place("b2_f", [NE, D], F32, r_over + 26048)
        sel = place("sel", [NE, NE, P], F32R, r_b + 36864)
        b2_h = place("b2_h", [NE, D], F32R, r_over + 24000)
        b2_l = place("b2_l", [NE, D], F32R, r_over + 20480)
        lg = place("lg", [P, T, NE], F32, r_over + 22528)
        m8 = place("m8", [P, T, 8], F32, r_over + 22848)
        ix = place("ix", [P, T, 8], U32, r_over + 23168)
        ixf = place("ixf", [P, T], F32, r_over + 23488)
        oh = place("oh", [P, T, NE], F32, r_over + 23552)
        iota8 = small("iota8", [P, NE], F32)
        cten = place("cten", [P, DH], F32, region(256))
        assert at[0] <= nc.sbuf_usable_end, (at[0], nc.sbuf_usable_end)

        c_mbq, c_mbv = cols_c[:, 0:KC], cols_c[:, KC:2 * KC]
        c_fbq, c_fbk = cols_c[:, 2 * KC:3 * KC], cols_c[:, 3 * KC:4 * KC]
        c_b1, c_bg = cols_c[:, 4 * KC:4 * KC + 16], cols_c[0:NE, 4 * KC + 16:4 * KC + 17]

        qk_dram = nc.dram_tensor("qk_dram", [2, NH, 2, DH, NP], F32, kind="Internal").ap()

        slot = {s: ctx.enter_context(nc.psum_tensor(s, [P, 512 * n], F32))[:, :]
                for s, n in (("W0", 3), ("W1", 3), ("N0", 1), ("N1", 1))}

        def sem(name):
            return ctx.enter_context(nc.semaphore(name))

        filled = {s: sem("filled_" + s) for s in slot}
        drained = {s: sem("drained_" + s) for s in slot}
        jobs, used = {}, {s: 0 for s in slot}

        def book(key, s):
            jobs[key] = (s, used[s])
            used[s] += 1

        book("edges", "N0")
        book("ranges", "N1")
        for k in range(KC):
            book(("xT", k), "W%d" % (k % 2))
        for t in range(T):
            book(("y", t), "N%d" % (t % 2))
        for t in range(T):
            book(("hist", t), "W0")
            book(("AT", t), "W1")
            book(("self", t), "N0")
            book(("agg", t), "N1")
        for m in range(KC):
            book(("foldM", m), "N%d" % (m % 2))
        book("bt", "N0")
        for m in range(KC):
            book(("tT", m), "W%d" % (m % 2))
        for t in range(T):
            book(("score", t), "W%d" % (t % 2))
        for m in range(KC):
            book(("foldN", m), "N%d" % (m % 2))
        book("bvo", "N0")
        book("colsum", "N1")
        for t in range(T):
            book(("o", t), "N%d" % (t % 2))
        for k in range(KC):
            book(("uT", k), "W%d" % (k % 2))
        for t in range(T):
            book(("v", t), "N%d" % (t % 2))
        for i in range(2 * KC):
            book(("qk", i), "W%d" % (i % 2))
        for i in range(UNITS):
            book(("S", i), "W0")
            book(("PT", i), "W1")
            book(("AV", i), "N%d" % (i % 2))
        for k in range(KC):
            book(("cT", k), "W%d" % (k % 2))
        for t in range(T):
            book(("sa", t), "N%d" % (t % 2))
        for k in range(KC):
            book(("tkT", k), "W%d" % (k % 2))
        book("logits", "W0")
        book("lgrows", "N0")
        book("ohT", "W1")
        for e in range(NE):
            book(("mask", e), "W%d" % (e % 2))

        def wait_filled(eng, key):
            s, n = jobs[key]
            eng.wait_ge(filled[s], n + 1)
            return slot[s]

        def wait_drained(eng, key):
            s, n = jobs[key]
            eng.wait_ge(drained[s], n + 1)

        s_x = [sem("x_in%d" % t) for t in range(T)]
        s_edge, s_const = sem("edges_in"), sem("column_constants_in")
        s_rowc, s_ffnrow = sem("mix_rows_in"), sem("ffn_rows_in")
        s_stage, s_split, s_scaled = sem("weights_in"), sem("weights_split"), sem("q_weights_scaled")
        s_bq8 = sem("bq_scaled")
        s_setup = sem("setup")
        s_step = sem("vector_step")
        s_ef, s_dg, s_span = sem("edge_floats"), sem("diag_ready"), sem("span_ready")
        s_var, s_sqrt = sem("variance_ready"), sem("sqrt_ready")
        s_rows = sem("normalised_rows")
        s_hi = sem("hi_written")
        s_hot = [sem("onehots_ready%d" % i) for i in range(2)]
        s_hotfree = [sem("onehots_used%d" % i) for i in range(2)]
        s_deg = sem("degrees_read")
        s_max, s_exp, s_pfree = sem("mix_max"), sem("mix_exp"), sem("mix_prob_used")
        s_bqp, s_bvr = sem("bq_pair_ready"), sem("bv_rep_ready")
        s_v32, s_v1, s_v2r, s_v2, s_v3 = (sem("v_sum"), sem("v_part1"), sem("v_rest"), sem("v_part2"),
                                          sem("v_part3"))
        s_store = [sem("qk_store%d" % i) for i in range(4)]
        s_stack = [sem("stack_in%d" % i) for i in range(2)]
        s_amax, s_aexp, s_aptr = sem("att_max"), sem("att_exp"), sem("att_prob_hi")
        s_pads, s_mixdone = sem("pads_zeroed"), sem("mix_rows_done")
        s_tok, s_route = sem("tokens_ready"), sem("router_step")
        s_wg, s_b2 = sem("router_weights_in"), sem("b2_in")
        s_gelu, s_hm, s_hh, s_hl = sem("gelu"), sem("hidden_masked"), sem("hidden_hi"), sem("hidden_lo")
        s_hfill = [sem("h_filled%d" % i) for i in range(3)]
        s_y, s_yd, s_hused = sem("y_filled"), sem("y_drained"), sem("hidden_used")
        s_fin, s_out = sem("row_final"), sem("out_stored")

        W_NEIGH, W_SELF, W_QT, W_KT, W_VT, W_MO, W_V, W_Q, W_K, W_O = range(10)
        LAST_USE = {W_NEIGH: ("y", T - 1), W_SELF: ("self", T - 1), W_QT: ("foldM", KC - 1), W_KT: "bt",
                    W_VT: ("foldN", KC - 1), W_MO: "bvo", W_V: ("v", T - 1), W_Q: ("qk", KC - 1),
                    W_K: ("qk", 2 * KC - 1), W_O: ("sa", T - 1)}
        UP, DOWN = 10, 11
        GROUPS = NE // 2 * 2
        n_units = UP + NE
        STEPS = GROUPS * KC
        R_LN = 2 * KC * (GROUPS - 1) + 2
        HT = NP // 2
        PW = HT // 2

        block = ctx.enter_context(nc.Block())

        @block.sync
        def _(sp):
            sp.dma_start(edge_i[:, 0:2, :], src.rearrange("(j p e) -> p j e", j=2, p=CP)).then_inc(s_edge, 16)
            sp.dma_start(edge_i[:, 2:4, :], dst.rearrange("(j p e) -> p j e", j=2, p=CP)).then_inc(s_edge, 16)
            for t in range(T):
                sp.dma_start(acc[0:rows(t), t, :], x[cols(t), :]).then_inc(s_x[t], 16)
            for i, a in enumerate((mix_bq, mix_bv, ffn_bq, ffn_bk)):
                sp.dma_start(cols_c[:, i * KC:(i + 1) * KC], a).then_inc(s_const, 16)
            sp.dma_start(c_b1, b1).then_inc(s_const, 16)
            sp.dma_start(c_bg, bg).then_inc(s_const, 16)

            def unit(u):
                if u:
                    sp.wait_ge(s_split, 2 * u)
                sp.dma_start(stage[:, :, :], w_all[u]).then_inc(s_stage, 16)

            unit(0)
            for i in range(6):
                sp.dma_start(row_c[:, i, :], mix_rows[i:i + 1, :].to_broadcast([P, D])).then_inc(s_rowc, 16)
            for u in range(1, W_Q):
                unit(u)
            sp.wait_ge(s_mixdone, T)
            for i in range(6):
                sp.dma_start(row_c[:, i, :], ffn_rows[i:i + 1, :].to_broadcast([P, D])).then_inc(s_ffnrow, 16)
            for u in (W_Q, W_K):
                unit(u)
            for i in range(2 * KC):
                wait_drained(sp, ("qk", i))
                for part in range(2):
                    for hh in range(2):
                        sp.dma_start(qk_dram[i // KC, 2 * (i % KC) + hh, part],
                                     big[hh * DH:(hh + 1) * DH, part * KC + i % KC, :].bitcast(F32)) \
                          .then_inc(s_store[i % 4], 16)
            for i in range(4):
                sp.wait_ge(s_store[i], 2 * 64)
            for h in range(NH):
                if h >= 2:
                    wait_filled(sp, ("S", (h - 1) * T - 1))
                b = 3 * (h % 2)
                sp.dma_start(big[:, b, :].bitcast(F32), qk_dram[0, h].rearrange("a d n -> (a d) n")).then_inc(s_stack[h % 2], 16)
                for part in range(2):
                    for rep in range(2):
                        sp.dma_start(big[rep * DH:(rep + 1) * DH, b + 1 + part, :].bitcast(F32), qk_dram[1, h, part]) \
                          .then_inc(s_stack[h % 2], 16)
            unit(W_O)
            unit(UP)
            wait_filled(sp, ("sa", T - 1))
            sp.wait_ge(s_pads, 3)
            sp.dma_start(wg_f[:, :, 0:NE], wg).then_inc(s_wg, 16)
            sp.dma_start(b2_f[:, :], b2).then_inc(s_b2, 16)
            for u in range(DOWN, n_units):
                unit(u)
            for t in range(T):
                sp.wait_ge(s_fin, t + 1)
                sp.dma_start(out[cols(t), :], tok[0:rows(t), t, :]).then_inc(s_out, 16)
            sp.wait_ge(s_out, 16 * T)

        @block.gpsimd
        def _(pool):
            pool.memset(ident[:, :], 0.0).then_inc(s_setup, 1)
            pool.memset(ones[:, :], 1.0).then_inc(s_setup, 1)
            pool.memset(hot_src[:, :, NP:NP + 2], 1.0).then_inc(s_setup, 1)
            pool.memset(mv[:, :, :], 1.0).then_inc(s_setup, 1)
            pool.wait_ge(s_setup, 4)
            pool.affine_select(out=ident[:, :], in_=ident[:, :], compare_op=ALU.not_equal, fill=1.0,
                               base=0, pattern=[[-1, P]], channel_multiplier=1).then_inc(s_setup, 1)
            pool.iota(tile_lo[:, 0:1], [[0, 1]], 0, P, allow_small_or_imprecise_dtypes=True).then_inc(s_setup, 1)
            pool.iota(tile_lo[:, 1:2], [[0, 1]], P - 1, P, allow_small_or_imprecise_dtypes=True).then_inc(s_setup, 1)
            pool.iota(chunk_no[:, :], [[1, CH]], 0, 0, allow_small_or_imprecise_dtypes=True).then_inc(s_setup, 1)
            pool.iota(iota16[:, :], [[1, NP]], 0, 0, allow_small_or_imprecise_dtypes=True).then_inc(s_setup, 1)
            pool.memset(zero16[:, :], 0.0).then_inc(s_setup, 1)
            pool.iota(iota8[:, :], [[1, NE]], 0, 0, allow_small_or_imprecise_dtypes=True).then_inc(s_setup, 1)
            for b in range(2):
                pool.sem_inc(s_hotfree[b], 1)
            for a in (act_h, act_l):
                pool.memset(a[:, :, N:NP].bitcast(F32), 0.0).then_inc(s_setup, 1)
            for u in range(n_units):
                pool.wait_ge(s_stage, 16 * (u + 1))
                if u == 0:
                    pool.wait_ge(s_span, 1)
                elif u - 2 in LAST_USE:
                    wait_filled(pool, LAST_USE[u - 2])
                elif u >= 2:
                    n = KC * ((u - 2 - UP) // 2 * 2 + 2)
                    if (u - UP) % 2:
                        pool.wait_ge(s_hused, n)
                    else:
                        r = 2 * n - 1
                        pool.wait_ge(s_hfill[r % 3], r // 3 + 1)
                if u == W_Q:
                    pool.tensor_scalar(stage[:, :, :], stage[:, :, :], DH ** -0.5, None, ALU.mult).then_inc(s_scaled, 1)
                    pool.wait_ge(s_scaled, 1)
                pool.tensor_copy(w_h[:, u % 2], stage[:, :, :]).then_inc(s_split, 1)
                pool.wait_ge(s_split, 2 * u + 1)
                pool.tensor_tensor(w_l[:, u % 2], stage[:, :, :], w_h[:, u % 2].bitcast(F32), ALU.subtract) \
                    .then_inc(s_split, 1)

        @block.tensor
        def _(pe):
            def begin(key):
                s, n = jobs[key]
                if n:
                    pe.wait_ge(drained[s], n)
                return slot[s]

            def end(ins, key):
                ins.then_inc(filled[jobs[key][0]], 1)

            def weights(u):
                pe.wait_ge(s_split, 2 * (u + 1))
                return w_h[:, u % 2], w_l[:, u % 2]

            def rows_product(out_ap, ah, al, sl, wh, wl, start=True, stop=True):
                steps = [(a, w, k) for k in range(KC) for a, w in ((ah, wh), (ah, wl), (al, wh))]
                for i, (a, w, k) in enumerate(steps):
                    last = pe.matmul(out_ap, a[:, k, sl], w[:, k, :], start=start and i == 0,
                                     stop=stop and i == len(steps) - 1)
                return last

            def feature_product(out_t, wh, wl, m, ah, al, pieces=PIECES):
                for c0, c1 in pieces:
                    steps = [(a, w, k) for k in range(KC) for a, w in ((ah, wh), (al, wh), (ah, wl))]
                    for i, (a, w, k) in enumerate(steps):
                        last = pe.matmul(out_t[:, c0:c1], w[:, k, m], a[:, k, c0:c1],
                                         start=i == 0, stop=i == len(steps) - 1)
                return last

            def transposes(tag, src_rows, ready):
                for k in range(KC):
                    o_ = begin((tag, k))
                    for t in range(T):
                        if k == 0:
                            ready(t)
                        last = pe.transpose(o_[:, cols(t)], src_rows[0:rows(t), t, k * P:(k + 1) * P],
                                            ident[0:rows(t), 0:rows(t)])
                    end(last, (tag, k))

            def chunk(m):
                return slice(m * P, (m + 1) * P)

            pe.wait_ge(s_setup, 13)
            pe.wait_ge(s_ef, 1)
            o_ = begin("edges")
            for j in range(4):
                last = pe.transpose(o_[0:CE, j * CP:(j + 1) * CP], edge_f[:, j, :], ident[0:CP, 0:CP])
            end(last, "edges")
            pe.wait_ge(s_dg, 4)
            o_ = begin("ranges")
            end(pe.matmul(o_[0:T, 0:2 * CH], ones[0:CP, 0:T], diag[:, :, :], start=True, stop=True), "ranges")

            transposes("xT", rows_b, lambda t: pe.wait_ge(s_rows, t + 1))
            wh, wl = weights(W_NEIGH)
            for k in range(KC):
                wait_drained(pe, ("xT", k))
            for t in range(T):
                end(rows_product(begin(("y", t))[0:rows(t), :], act_h, act_l, cols(t), wh, wl), ("y", t))

            pe.wait_ge(s_span, 1)
            ticket = pe.alloc_register("pe_pairs")
            pe.reg_mov(ticket, 0)
            for t in range(T + 1):
                if t < T:
                    o_ = begin(("hist", t))
                    for c0, c1 in COUNT_PIECES:
                        pe.matmul(o_[:, c0:c1], zero16[:, 0:P], zero16[:, 0:c1 - c0], start=True, stop=True)
                    c_first = pe.value_load(span_i[t:t + 1, 0:1], min_val=0, max_val=CH - 1)
                    c_end = pe.value_load(span_i[t:t + 1, 1:2], min_val=1, max_val=CH)
                    with pe.Fori(c_first, c_end, 2):
                        pe.reg_add(ticket, ticket, 1)
                        for b in range(2):
                            pe.wait_ge(s_hot[b], pe.snap(ticket))
                            for c0, c1 in COUNT_PIECES:
                                last = pe.matmul(o_[:, c0:c1], hot_dst[0:CE, b, :], hot_src[0:CE, b, c0:c1],
                                                 start=False, stop=True, skip_group_check=True)
                            last.then_inc(s_hotfree[b], 1)
                    end(pe.matmul(o_[:, NP:NP + 2], zero16[:, 0:P], zero16[:, 0:2], start=False, stop=True,
                                  skip_group_check=True), ("hist", t))
                if t:
                    v = t - 1
                    wh, wl = weights(W_SELF)
                    end(rows_product(begin(("self", v))[0:rows(v), :], act_h, act_l, cols(v), wh, wl), ("self", v))
                    o_ = begin(("agg", v))
                    wait_drained(pe, ("AT", v))
                    if v == 0:
                        for tt in (T - 2, T - 1):
                            wait_drained(pe, ("y", tt))
                    steps = [(a, y, j) for j in range(T) for a, y in ((adj_h, y_h), (adj_h, y_l), (adj_l, y_h))]
                    for i, (a, y, j) in enumerate(steps):
                        last = pe.matmul(o_[0:rows(v), :], a[0:rows(j), j * P:j * P + rows(v)], y[0:rows(j), j, :],
                                         start=i == 0, stop=i == len(steps) - 1)
                    end(last, ("agg", v))
                if t < T:
                    wait_drained(pe, ("hist", t))
                    o_ = begin(("AT", t))
                    for j in range(T):
                        last = pe.transpose(o_[:, chunk(j)], counts[:, chunk(j)], ident[:, :])
                    end(last, ("AT", t))

            qh, ql = weights(W_QT)
            kh, kl = weights(W_KT)
            for m in range(KC):
                end(rows_product(begin(("foldM", m)), qh, ql, chunk(m), kh, kl), ("foldM", m))
            pe.wait_ge(s_bqp, 2)
            o_ = begin("bt")
            for m in range(KC):
                steps = [(w, k) for k in range(KC) for w in (kh, kl)]
                for i, (w, k) in enumerate(steps):
                    last = pe.matmul(o_[:, 2 * m:2 * m + 2], w[:, k, chunk(m)], bq_pair[:, k, :],
                                     start=i == 0, stop=i == len(steps) - 1)
            end(last, "bt")
            for m in range(KC):
                wait_drained(pe, ("foldM", m))
            for m in range(KC):
                end(feature_product(begin(("tT", m)), fold_h, fold_l, chunk(m), act_h, act_l), ("tT", m))
            for m in range(KC):
                wait_drained(pe, ("tT", m))
            for t in range(T):
                o_ = begin(("score", t))
                for c0, c1 in PIECES:
                    steps = [(a, b, k) for k in range(KC) for a, b in ((0, act_h), (0, act_l), (KC, act_h))]
                    for i, (a, b, k) in enumerate(steps):
                        last = pe.matmul(o_[0:rows(t), c0:c1], big[:, a + k, cols(t)], b[:, k, c0:c1],
                                         start=i == 0, stop=i == len(steps) - 1)
                end(last, ("score", t))

            vh, vl = weights(W_VT)
            oh_, ol_ = weights(W_MO)
            for m in range(KC):
                end(rows_product(begin(("foldN", m)), vh, vl, chunk(m), oh_, ol_), ("foldN", m))
            pe.wait_ge(s_bvr, 2 * KC)
            end(rows_product(begin("bvo"), bv_rep_h, bv_rep_l, slice(0, P), oh_, ol_), "bvo")
            pe.wait_ge(s_pfree, T)
            o_ = begin("colsum")
            for t in range(T):
                last = pe.matmul(o_[0:rows(t), t:t + 1], col_acc[:, cols(t)], ones[:, 0:1], start=True, stop=True)
            end(last, "colsum")
            for m in range(KC):
                wait_drained(pe, ("foldN", m))
            for t in range(T):
                end(rows_product(begin(("o", t))[0:rows(t), :], act_h, act_l, cols(t), fold_h, fold_l), ("o", t))

            transposes("uT", rows_b, lambda t: pe.wait_ge(s_rows, T + t + 1))
            for k in range(KC):
                wait_drained(pe, ("uT", k))
            wh, wl = weights(W_V)
            for t in range(T):
                end(rows_product(begin(("v", t))[0:rows(t), :], act_h, act_l, cols(t), wh, wl), ("v", t))
            for i in range(2 * KC):
                wh, wl = weights(W_Q + i // KC)
                end(feature_product(begin(("qk", i)), wh, wl, chunk(i % KC), act_h, act_l), ("qk", i))

            def scores(i):
                h, t = divmod(i, T)
                if t == 0:
                    pe.wait_ge(s_stack[h % 2], 80 * (h // 2 + 1))
                o_ = begin(("S", i))
                b = 3 * (h % 2)
                for c0, c1 in PIECES:
                    for part in range(2):
                        last = pe.matmul(o_[0:rows(t), c0:c1], big[:, b, cols(t)], big[:, b + 1 + part, c0:c1],
                                         start=part == 0, stop=part == 1)
                end(last, ("S", i))

            def turn(i):
                t = i % T
                pe.wait_ge(s_aexp, i + 1)
                o_ = begin(("PT", i))
                for kt in range(T):
                    last = pe.transpose(o_[:, kt * P:kt * P + rows(t)], prob[0:rows(t), i % 2, chunk(kt)],
                                        ident[0:rows(t), 0:rows(t)])
                end(last, ("PT", i))

            def values(i):
                h, t = divmod(i, T)
                wait_drained(pe, ("PT", i))
                if i == 0:
                    pe.wait_ge(s_v3, T)
                o_ = begin(("AV", i))
                for kt in range(T):
                    r = rows(kt)
                    pe.matmul(o_[0:rows(t), 0:3 * DH], pt_h[0:r, i % 2, kt, 0:rows(t)], val[0:r, kt, h, :],
                              start=kt == 0, stop=False, skip_group_check=True)
                    last = pe.matmul(o_[0:rows(t), 0:2 * DH], pt_l[0:r, i % 2, kt, 0:rows(t)],
                                     val[0:r, kt, h, 0:2 * DH], start=False, stop=kt == T - 1,
                                     skip_group_check=True)
                end(last, ("AV", i))

            for i in range(UNITS + 2):
                if i < UNITS:
                    scores(i)
                if i >= 2:
                    values(i - 2)
                if 1 <= i <= UNITS:
                    turn(i - 1)

            wait_drained(pe, ("AV", UNITS - 2))
            wait_drained(pe, ("AV", UNITS - 1))
            transposes("cT", ctx_rows, lambda t: None)
            for k in range(KC):
                wait_drained(pe, ("cT", k))
            wh, wl = weights(W_O)
            for t in range(T):
                end(rows_product(begin(("sa", t))[0:rows(t), :], big[:, 0:KC], big[:, KC:2 * KC], cols(t), wh, wl),
                    ("sa", t))

            transposes("tkT", tok, lambda t: pe.wait_ge(s_tok, t + 1))
            for k in range(KC):
                wait_drained(pe, ("tkT", k))
            pe.wait_ge(s_route, 2)
            end(feature_product(begin("logits"), wg_h, wg_l, slice(0, P), act_h, act_l), "logits")
            o_ = begin("lgrows")
            wait_drained(pe, "logits")
            for t in range(T):
                last = pe.transpose(o_[0:rows(t), t * NE:(t + 1) * NE], lg_t[:, cols(t)], ident[0:NE, 0:NE])
            end(last, "lgrows")
            o_ = begin("ohT")
            pe.wait_ge(s_route, 2 + T)
            for t in range(T):
                last = pe.transpose(o_[0:NE, cols(t)], oh[0:rows(t), t, :], ident[0:rows(t), 0:rows(t)])
            end(last, "ohT")
            wait_drained(pe, "ohT")
            pe.wait_ge(s_route, 2 + T + NE + 2)
            for e in range(NE):
                o_ = begin(("mask", e))
                for c0, c1 in PIECES:
                    last = pe.matmul(o_[:, c0:c1], sel[:, e, :], oh_t[:, c0:c1], start=True, stop=True)
                end(last, ("mask", e))
            for s in slot:
                pe.wait_ge(drained[s], used[s])

            def up(n):
                g, j = divmod(n, KC)
                q, half = divmod(g, 2)
                wh, wl = weights(UP + 2 * q)
                for p in range(2):
                    r = 2 * n + p
                    if r >= 3:
                        pe.wait_ge(s_gelu, r - 2)
                    c0 = half * HT + p * PW
                    last = feature_product(hbank[r % 3], wh, wl, chunk(j), act_h[:, :, c0:c0 + PW],
                                           act_l[:, :, c0:c0 + PW], pieces=[(0, PW)])
                    last.then_inc(s_hfill[r % 3], 1)

            def down(n):
                g, j = divmod(n, KC)
                q, half = divmod(g, 2)
                wh, wl = weights(DOWN + 2 * q)
                if j == 0 and g:
                    pe.wait_ge(s_yd, T // 2 * g)
                pe.wait_ge(s_hl, 2 * n + 2)
                for i in range(T // 2):
                    t = half * (T // 2) + i
                    o_ = ybank[i][0:rows(t), :]
                    sl = slice(i * P, i * P + rows(t))
                    if n in (0, KC):
                        pe.matmul(o_, oh_t[:, cols(t)], b2_h[:, :], start=True, stop=False)
                        pe.matmul(o_, oh_t[:, cols(t)], b2_l[:, :], start=False, stop=False)
                    for k, (a, w) in enumerate(((hid_h, wh), (hid_h, wl), (hid_l, wh))):
                        last = pe.matmul(o_, a[:, n % 2, sl], w[:, j, :], start=g >= 2 and j == 0 and k == 0,
                                         stop=j == KC - 1 and k == 2)
                last.then_inc(s_hused, 1)

            hbank = [slot["W1"][:, 1024:1536], slot["N0"], slot["N1"]]
            ybank = [slot["W0"][:, 0:512], slot["W0"][:, 512:1024], slot["W0"][:, 1024:1536],
                     slot["W1"][:, 0:512], slot["W1"][:, 512:1024]]
            for n in range(STEPS + 1):
                if n < STEPS:
                    up(n)
                if n:
                    down(n - 1)

        @block.scalar
        def _(act):
            ln_no = [0]

            def sqrt_of_variance(t0=0, t1=T):
                ln_no[0] += 1
                act.wait_ge(s_var, ln_no[0])
                act.activation(rs[:, t0:t1], ve[:, t0:t1], ACT.Sqrt).then_inc(s_sqrt, 1)

            def hi(key, out_ap, in_of, bias=None):
                o_ = wait_filled(act, key)
                if bias is None:
                    act.activation(out_ap, in_of(o_), ACT.Copy).then_inc(s_hi, 1)
                else:
                    act.activation(out_ap, in_of(o_), ACT.Identity, bias=bias).then_inc(s_hi, 1)

            sqrt_of_variance()
            for k in range(KC):
                hi(("xT", k), act_h[:, k, 0:N], lambda o_: o_[:, 0:N])
            for t in range(T):
                hi(("y", t), y_h[0:rows(t), t, :], lambda o_: o_[0:rows(t), :])
            for t in range(T):
                o_ = wait_filled(act, ("hist", t))
                if t:
                    act.wait_ge(s_deg, t)
                    wait_filled(act, ("AT", t - 1))
                act.activation(counts[:, :], o_[:, 0:NP + 2], ACT.Copy).then_inc(drained["W0"], 1)
                if t:
                    wait_filled(act, ("agg", t - 1))
                hi(("AT", t), adj_h[:, :], lambda o_: o_[:, 0:NP])
            act.wait_ge(s_rowc, 96)
            act.wait_ge(s_var, 2)
            act.activation(tmp[:, 1, 0:D], row_c[:, 4, :], ACT.Sqrt).then_inc(s_sqrt, 1)
            ln_no[0] += 1
            for m in range(KC):
                hi(("foldM", m), fold_h[:, m, :], lambda o_: o_[:, :])
            act.wait_ge(s_const, 96)
            wait_drained(act, "bt")
            wait_filled(act, ("agg", T - 1))
            for m in range(KC):
                hi(("tT", m), big[:, m, :], lambda o_: o_[:, 0:NP], bias=bt[:, m:m + 1])
            for t in range(T):
                act.wait_ge(s_max, t + 1)
                s, _n = jobs[("score", t)]
                if t >= 2:
                    act.wait_ge(s_pfree, t - 1)
                act.activation(prob[0:rows(t), t % 2, 0:N], slot[s][0:rows(t), 0:N], ACT.Exp,
                               bias=nmax[0:rows(t), t:t + 1], accum_out=z_mix[0:rows(t), t:t + 1]) \
                   .then_inc(s_exp, 1)
            for m in range(KC):
                if m == 0:
                    wait_filled(act, ("tT", KC - 1))
                hi(("foldN", m), fold_h[:, m, :], lambda o_: o_[:, :])
            sqrt_of_variance()
            for k in range(KC):
                hi(("uT", k), act_h[:, k, 0:N], lambda o_: o_[:, 0:N])
            for t in range(T):
                r = rows(t)
                v = tmp[0:r, t % 2, 0:D].rearrange("p (h d) -> p h d", h=NH)
                act.wait_ge(s_v32, t + 1)
                act.activation(val[0:r, t, :, 0:DH], v, ACT.Copy).then_inc(s_v1, 1)
                act.wait_ge(s_v2r, t + 1)
                act.activation(val[0:r, t, :, DH:2 * DH], v, ACT.Copy).then_inc(s_v2, 1)
            for i in range(2 * KC):
                c = cols_c[:, 2 * KC + i:2 * KC + i + 1]
                if i >= 4:
                    act.wait_ge(s_store[i % 4], 64)
                if i == 0:
                    wait_drained(act, ("uT", KC - 1))
                    act.wait_ge(s_bq8, 1)
                hi(("qk", i), big[:, i % KC, :], lambda o_: o_[:, 0:NP], bias=c)
            for i in range(UNITS + 1):
                if i < UNITS:
                    r = rows(i % T)
                    act.wait_ge(s_amax, i + 1)
                    if i == 0:
                        act.wait_ge(s_pads, 1)
                    if i >= 2:
                        wait_filled(act, ("PT", i - 2))
                        wait_drained(act, ("AV", i - 2))
                    act.activation(prob[0:r, i % 2, 0:N], slot["W0"][0:r, 0:N], ACT.Exp,
                                   bias=nm[0:r, i % 2:i % 2 + 1], accum_out=zz[0:r, i % 2:i % 2 + 1]) \
                       .then_inc(s_aexp, 1)
                if i:
                    j = i - 1
                    r = rows(j % T)
                    o_ = wait_filled(act, ("PT", j))
                    if j >= 2:
                        wait_filled(act, ("AV", j - 2))
                    act.activation(pt_h[:, j % 2, :, 0:r],
                                   o_[:, 0:NP].rearrange("p (a b) -> p a b", b=P)[:, :, 0:r], ACT.Copy) \
                       .then_inc(s_aptr, 1)
            wait_filled(act, ("S", UNITS - 1))
            for k in range(KC):
                hi(("cT", k), big[:, k, 0:N], lambda o_: o_[:, 0:N])
            sqrt_of_variance()
            act.wait_ge(s_pads, 2)
            for k in range(KC):
                hi(("tkT", k), act_h[:, k, 0:N], lambda o_: o_[:, 0:N])
            for e in range(NE):
                o_ = wait_filled(act, ("mask", e))
                act.activation(mask[:, e, :], o_[:, 0:NP], ACT.Copy).then_inc(drained[jobs[("mask", e)][0]], 1)

            hbank = [slot["W1"][:, 1024:1536], slot["N0"], slot["N1"]]
            for r in range(2 * STEPS + 1):
                if r < 2 * STEPS:
                    n = r // 2
                    g, j = divmod(n, KC)
                    ft = g // 2 * KC + j
                    act.wait_ge(s_hfill[r % 3], r // 3 + 1)
                    if r >= 2:
                        act.wait_ge(s_hm, r - 1)
                    act.activation(tmp[:, 0, (r % 2) * PW:(r % 2 + 1) * PW], hbank[r % 3][:, 0:PW], ACT.Gelu,
                                   bias=c_b1[:, ft:ft + 1]).then_inc(s_gelu, 1)
                if r:
                    q_ = r - 1
                    act.wait_ge(s_hm, q_ + 1)
                    if q_ >= 4:
                        act.wait_ge(s_hused, q_ // 2 - 1)
                    act.activation(hid_h[:, (q_ // 2) % 2, (q_ % 2) * PW:(q_ % 2 + 1) * PW],
                                   tmp[:, 1, (q_ % 2) * PW:(q_ % 2 + 1) * PW], ACT.Copy).then_inc(s_hh, 1)
                if r == R_LN:
                    sqrt_of_variance(0, T // 2)
            sqrt_of_variance(T // 2, T)

        @block.vector
        def _(dve):
            chain, his, sq = [0], [0], [0]

            def step(ins):
                ins.then_inc(s_step, 1)
                chain[0] += 1
                dve.wait_ge(s_step, chain[0])

            def lo(key, out_ap, in_of, hi_ap, bias=None):
                o_ = slot[jobs[key][0]]
                his[0] += 1
                dve.wait_ge(s_hi, his[0])
                if bias is None:
                    ins = dve.tensor_tensor(out_ap, in_of(o_), hi_ap.bitcast(F32), ALU.subtract)
                else:
                    ins = dve.scalar_tensor_tensor(out_ap, in_of(o_), bias, hi_ap.bitcast(F32), ALU.add,
                                                   ALU.subtract)
                ins.then_inc(drained[jobs[key][0]], 1)

            def inverse_root(var, root, out_ap, work):
                step(dve.reciprocal(out_ap, root))
                step(dve.tensor_tensor(work, out_ap, out_ap, ALU.mult))
                step(dve.tensor_tensor(work, work, var, ALU.mult))
                step(dve.tensor_scalar(work, work, -0.5, 1.5, ALU.mult, ALU.add))
                step(dve.tensor_tensor(out_ap, out_ap, work, ALU.mult))

            def moments(t, row_ap):
                step(dve.bn_stats(st6[0:rows(t), 0, :], row_ap))
                step(dve.bn_aggr(mv[0:rows(t), t, :], st6[0:rows(t), 0, :]))

            def variances(t0=0, t1=T):
                dve.tensor_scalar(ve[:, t0:t1], mv[:, t0:t1, 1], LN_EPS, None, ALU.add).then_inc(s_var, 1)
                sq[0] += 1

            def finish_moments(t0=0, t1=T, begun=False):
                if not begun:
                    variances(t0, t1)
                dve.wait_ge(s_var, sq[0])
                dve.wait_ge(s_sqrt, sq[0])
                inverse_root(ve[:, t0:t1], rs[:, t0:t1], rs[:, t0:t1], nr[:, t0:t1])

            def normalise(out_ap, in_ap, t):
                r = rows(t)
                return dve.tensor_scalar(out_ap, in_ap, mv[0:r, t, 0:1], rs[0:r, t:t + 1], ALU.subtract, ALU.mult)

            def scaled_norm(a, t, gain, offset):
                r = rows(t)
                step(dve.scalar_tensor_tensor(a[0:r, t, :], a[0:r, t, :], mv[0:r, t, 0:1], gain, ALU.subtract, ALU.mult))
                return dve.scalar_tensor_tensor(a[0:r, t, :], a[0:r, t, :], rs[0:r, t:t + 1], offset, ALU.mult, ALU.add)

            dve.wait_ge(s_edge, 32)
            dve.tensor_copy(edge_f[:, :, :], edge_i[:, :, :]).then_inc(s_ef, 1)
            dve.wait_ge(s_ef, 1)
            step(dve.tensor_reduce(lohi[:, 0:2], edge_f[:, 2:4, :], AX.X, ALU.min))
            step(dve.tensor_reduce(lohi[:, 2:4], edge_f[:, 2:4, :], AX.X, ALU.max))
            dve.wait_ge(s_setup, 13)
            for j in range(4):
                dve.tensor_scalar(diag[:, j, :], ident[0:CP, 0:CP], lohi[:, j:j + 1], None, ALU.mult).then_inc(s_dg, 1)
            o_ = wait_filled(dve, "edges")
            step(dve.memset(edge_t[:, :, CH:CH + 1], -1.0))
            dve.tensor_copy(edge_t[:, :, 0:CH], o_[0:CE, 0:2 * CH].rearrange("p (a c) -> p a c", a=2)) \
               .then_inc(drained["N0"], 1)
            o_ = wait_filled(dve, "ranges")
            step(dve.tensor_scalar(cover2[:, :], o_[0:T, 0:CH], tile_lo[:, 1:2], None, ALU.is_le))
            step(dve.scalar_tensor_tensor(cover[:, :], o_[0:T, CH:2 * CH], tile_lo[:, 0:1], cover2[:, :], ALU.is_ge,
                                          ALU.mult))
            step(dve.scalar_tensor_tensor(cover2[:, :], cover[:, :], -BIG, chunk_no[:, :], ALU.mult, ALU.add))
            step(dve.tensor_reduce(span[:, 0:1], cover2[:, :], AX.X, ALU.min))
            step(dve.tensor_scalar(span[:, 0:1], span[:, 0:1], BIG, CH - 1.0, ALU.add, ALU.min))
            step(dve.scalar_tensor_tensor(cover2[:, :], chunk_no[:, :], 1.0, cover[:, :], ALU.add, ALU.mult))
            step(dve.tensor_reduce(span[:, 1:2], cover2[:, :], AX.X, ALU.max))
            step(dve.tensor_scalar(span[:, 2:3], span[:, 0:1], 1.0, None, ALU.add))
            dve.tensor_tensor(span[:, 1:2], span[:, 1:2], span[:, 2:3], ALU.max).then_inc(drained["N1"], 1)
            wait_drained(dve, "ranges")
            dve.tensor_copy(span_i[:, :], span[:, 0:2]).then_inc(s_span, 1)

            for t in range(T):
                dve.wait_ge(s_x[t], 16)
                moments(t, acc[0:rows(t), t, :])
            finish_moments()
            for t in range(T):
                r = rows(t)
                normalise(rows_b[0:r, t, :], acc[0:r, t, :], t).then_inc(s_rows, 1)
                dve.wait_ge(s_rows, t + 1)
                dve.tensor_tensor(acc[0:r, t, :], acc[0:r, t, :], rows_b[0:r, t, :], ALU.add).then_inc(s_step, 1)
                chain[0] += 1
            for k in range(KC):
                lo(("xT", k), act_l[:, k, 0:N], lambda o_: o_[:, 0:N], act_h[:, k, 0:N])
            for t in range(T):
                r = rows(t)
                if t == 0:
                    dve.wait_ge(s_step, chain[0])
                lo(("y", t), y_l[0:r, t, :], lambda o_: o_[0:r, :], y_h[0:r, t, :])

            def finish_tile(t):
                r = rows(t)
                own = work1[0:r, :]
                o_ = wait_filled(dve, ("self", t))
                dve.tensor_tensor(own, o_[0:r, :], row_c[0:r, 0, :], ALU.add).then_inc(drained["N0"], 1)
                wait_drained(dve, ("self", t))
                o_ = wait_filled(dve, ("agg", t))
                dve.scalar_tensor_tensor(own, o_[0:r, :], rdeg[0:r, t:t + 1], own, ALU.mult, ALU.add) \
                   .then_inc(drained["N1"], 1)
                wait_drained(dve, ("agg", t))

            dve.wait_ge(s_rowc, 96)
            dve.wait_ge(s_span, 1)
            ticket = dve.alloc_register("dve_pairs")
            dve.reg_mov(ticket, 0)
            for t in range(T + 2):
                if t < T:
                    c_first = dve.value_load(span_i[t:t + 1, 0:1], min_val=0, max_val=CH - 1)
                    c_end = dve.value_load(span_i[t:t + 1, 1:2], min_val=1, max_val=CH)
                    with dve.Fori(c_first, c_end, 2) as c:
                        dve.reg_add(ticket, ticket, 1)
                        for b in range(2):
                            dve.wait_ge(s_hotfree[b], dve.snap(ticket))
                            dve.tensor_scalar(hot_src[0:CE, b, 0:NP], iota16[0:CE, :],
                                              edge_t[:, 0, bass.ds(c + b, 1)], None, ALU.is_equal)
                            dve.tensor_scalar(hot_dst[0:CE, b, :], iota16[0:CE, t * P:(t + 1) * P],
                                              edge_t[:, 1, bass.ds(c + b, 1)], None, ALU.is_equal) \
                               .then_inc(s_hot[b], 1)
                if t >= 2:
                    finish_tile(t - 2)
                if 1 <= t <= T:
                    if t >= 2:
                        wait_filled(dve, ("agg", t - 2))
                    lo(("AT", t - 1), adj_l[:, :], lambda o_: o_[:, 0:NP], adj_h[:, :])
                if t >= 2:
                    r = rows(t - 2)
                    step(dve.scalar_tensor_tensor(acc[0:r, t - 2, :], work1[0:r, :], 0.0, acc[0:r, t - 2, :],
                                                  ALU.max, ALU.add))
                if t < T:
                    wait_drained(dve, ("hist", t))
                    dve.tensor_scalar(nr[:, 0:1], counts[:, NP:NP + 1], 1.0, None, ALU.max).then_inc(s_deg, 1)
                    dve.wait_ge(s_deg, t + 1)
                    step(dve.reciprocal(rdeg[:, t:t + 1], nr[:, 0:1]))

            dve.tensor_scalar(row_c[:, 4, :], row_c[:, 4, :], LN_EPS, None, ALU.add).then_inc(s_var, 1)
            sq[0] += 1
            dve.wait_ge(s_var, sq[0])
            dve.wait_ge(s_sqrt, sq[0])
            inverse_root(row_c[:, 4, :], tmp[:, 1, 0:D], tmp[:, 1, 0:D], tmp[:, 1, D:2 * D])
            step(dve.tensor_tensor(row_c[:, 1, :], row_c[:, 1, :], tmp[:, 1, 0:D], ALU.mult))
            step(dve.tensor_tensor(row_c[:, 5, :], row_c[:, 5, :], row_c[:, 3, :], ALU.subtract))
            step(dve.tensor_tensor(row_c[:, 5, :], row_c[:, 5, :], row_c[:, 1, :], ALU.mult))
            step(dve.tensor_tensor(row_c[:, 5, :], row_c[:, 5, :], row_c[:, 2, :], ALU.add))
            dve.wait_ge(s_const, 96)
            dve.tensor_copy(bq_pair[:, :, 0], c_mbq).then_inc(s_bqp, 1)
            dve.wait_ge(s_bqp, 1)
            dve.tensor_tensor(bq_pair[:, :, 1], c_mbq, bq_pair[:, :, 0].bitcast(F32), ALU.subtract).then_inc(s_bqp, 1)
            for k in range(KC):
                dve.tensor_scalar(bv_rep_h[:, k, :], ones[:, :], c_mbv[:, k:k + 1], None, ALU.mult).then_inc(s_bvr, 1)
                dve.wait_ge(s_bvr, 2 * k + 1)
                dve.scalar_tensor_tensor(bv_rep_l[:, k, :], ones[:, :], c_mbv[:, k:k + 1],
                                         bv_rep_h[:, k, :].bitcast(F32), ALU.mult, ALU.subtract).then_inc(s_bvr, 1)
            dve.tensor_scalar(c_fbq, c_fbq, DH ** -0.5, None, ALU.mult).then_inc(s_bq8, 1)
            for m in range(KC):
                lo(("foldM", m), fold_l[:, m, :], lambda o_: o_[:, :], fold_h[:, m, :])
            o_ = wait_filled(dve, "bt")
            dve.tensor_reduce(bt[:, :], o_[:, 0:2 * KC].rearrange("p (m b) -> p m b", b=2), AX.X, ALU.add) \
               .then_inc(drained["N0"], 1)
            for m in range(KC):
                if m == 0:
                    wait_drained(dve, "bt")
                lo(("tT", m), big[:, KC + m, :], lambda o_: o_[:, 0:NP], big[:, m, :], bias=bt[:, m:m + 1])

            def column_sums(t):
                r = rows(t)
                dve.wait_ge(s_exp, t + 1)
                step(dve.reciprocal(zt[0:r, t:t + 1], z_mix[0:r, t:t + 1]))
                if t == 0:
                    ins = dve.tensor_scalar(col_acc[0:r, 0:N], prob[0:r, t % 2, 0:N], zt[0:r, t:t + 1], None, ALU.mult)
                else:
                    ins = dve.scalar_tensor_tensor(col_acc[0:r, 0:N], prob[0:r, t % 2, 0:N], zt[0:r, t:t + 1],
                                                   col_acc[0:r, 0:N], ALU.mult, ALU.add)
                ins.then_inc(s_pfree, 1)
                dve.wait_ge(s_pfree, t + 1)

            for t in range(T):
                r = rows(t)
                o_ = wait_filled(dve, ("score", t))
                dve.tensor_reduce(nmax[0:r, t:t + 1], o_[0:r, 0:N], AX.X, ALU.max, negate=True).then_inc(s_max, 1)
                dve.wait_ge(s_exp, t + 1)
                dve.wait_ge(s_max, t + 1)
                dve.engine_nop().then_inc(drained[jobs[("score", t)][0]], 1)
                column_sums(t)
            for m in range(KC):
                lo(("foldN", m), fold_l[:, m, :], lambda o_: o_[:, :], fold_h[:, m, :])
            o_ = wait_filled(dve, "bvo")
            dve.tensor_copy(row_c[:, 3, :], o_[:, :]).then_inc(drained["N0"], 1)
            wait_drained(dve, "bvo")
            o_ = wait_filled(dve, "colsum")
            last_r = rows(T - 1)
            step(dve.tensor_scalar(nr[:, 0:T - 1], o_[:, 0:T - 1], 1e-9, None, ALU.add))
            step(dve.tensor_scalar(nr[0:last_r, T - 1:T], o_[0:last_r, T - 1:T], 1e-9, None, ALU.add))
            step(dve.reciprocal(zt[:, 0:T - 1], nr[:, 0:T - 1]))
            step(dve.reciprocal(zt[0:last_r, T - 1:T], nr[0:last_r, T - 1:T]))
            step(dve.tensor_tensor(cfac[:, 0:T - 1], o_[:, 0:T - 1], zt[:, 0:T - 1], ALU.mult))
            dve.tensor_tensor(cfac[0:last_r, T - 1:T], o_[0:last_r, T - 1:T], zt[0:last_r, T - 1:T], ALU.mult) \
               .then_inc(drained["N1"], 1)
            wait_drained(dve, "colsum")
            for t in range(T):
                r = rows(t)
                o_ = wait_filled(dve, ("o", t))
                own = work1[0:r, :]
                dve.tensor_tensor(own, o_[0:r, :], row_c[0:r, 3, :], ALU.add).then_inc(drained[jobs[("o", t)][0]], 1)
                wait_drained(dve, ("o", t))
                step(dve.scalar_tensor_tensor(own, own, cfac[0:r, t:t + 1], row_c[0:r, 1, :], ALU.mult, ALU.mult))
                step(dve.tensor_tensor(own, own, row_c[0:r, 5, :], ALU.add))
                dve.scalar_tensor_tensor(acc[0:r, t, :], own, 0.0, acc[0:r, t, :], ALU.max, ALU.add) \
                   .then_inc(s_mixdone, 1)
                dve.wait_ge(s_mixdone, t + 1)

            for t in range(T):
                moments(t, acc[0:rows(t), t, :])
            finish_moments()
            for t in range(T):
                r = rows(t)
                normalise(rows_b[0:r, t, :], acc[0:r, t, :], t).then_inc(s_rows, 1)
            for k in range(KC):
                lo(("uT", k), act_l[:, k, 0:N], lambda o_: o_[:, 0:N], act_h[:, k, 0:N])
            dve.wait_ge(s_ffnrow, 96)
            for t in range(T):
                r = rows(t)
                v = tmp[0:r, t % 2, 0:D]
                vh = v.rearrange("p (h d) -> p h d", h=NH)
                o_ = wait_filled(dve, ("v", t))
                if t >= 2:
                    dve.wait_ge(s_v3, t - 1)
                dve.tensor_tensor(v, o_[0:r, :], row_c[0:r, 0, :], ALU.add).then_inc(drained[jobs[("v", t)][0]], 1)
                wait_drained(dve, ("v", t))
                dve.engine_nop().then_inc(s_v32, 1)
                dve.wait_ge(s_v1, t + 1)
                dve.tensor_tensor(vh, vh, val[0:r, t, :, 0:DH], ALU.subtract).then_inc(s_v2r, 1)
                dve.wait_ge(s_v2r, t + 1)
                dve.wait_ge(s_v2, t + 1)
                dve.tensor_tensor(val[0:r, t, :, 2 * DH:3 * DH], vh, val[0:r, t, :, DH:2 * DH], ALU.subtract) \
                   .then_inc(s_v3, 1)
            for i in range(2 * KC):
                if i >= 4:
                    dve.wait_ge(s_store[i % 4], 64)
                lo(("qk", i), big[:, KC + i % KC, :], lambda o_: o_[:, 0:NP], big[:, i % KC, :],
                   bias=cols_c[:, 2 * KC + i:2 * KC + i + 1])
            dve.wait_ge(s_v3, T)
            dve.memset(prob[:, :, N:NP], 0.0).then_inc(s_pads, 1)

            for i in range(UNITS + 2):
                if i < UNITS:
                    r = rows(i % T)
                    o_ = wait_filled(dve, ("S", i))
                    if i >= 2:
                        dve.wait_ge(s_aexp, i - 1)
                    dve.tensor_reduce(nm[0:r, i % 2:i % 2 + 1], o_[0:r, 0:N], AX.X, ALU.max, negate=True) \
                       .then_inc(s_amax, 1)
                if i >= 2:
                    j = i - 2
                    h, t = divmod(j, T)
                    r = rows(t)
                    o_ = wait_filled(dve, ("AV", j))
                    dve.wait_ge(s_aexp, j + 1)
                    step(dve.reciprocal(rz[0:r, 0:1], zz[0:r, j % 2:j % 2 + 1]))
                    step(dve.tensor_reduce(cten[0:r, :], o_[0:r, 0:3 * DH].rearrange("p (g d) -> p d g", g=3), AX.X,
                                           ALU.add))
                    dve.tensor_scalar(ctx_rows[0:r, t, h * DH:(h + 1) * DH], cten[0:r, :], rz[0:r, 0:1], None,
                                      ALU.mult).then_inc(drained[jobs[("AV", j)][0]], 1)
                    wait_drained(dve, ("AV", j))
                if i < UNITS:
                    dve.wait_ge(s_aexp, i + 1)
                    dve.wait_ge(s_amax, i + 1)
                    dve.engine_nop().then_inc(drained["W0"], 1)
                if 1 <= i <= UNITS:
                    j = i - 1
                    r = rows(j % T)
                    o_ = wait_filled(dve, ("PT", j))
                    dve.wait_ge(s_aptr, j + 1)
                    dve.tensor_tensor(pt_l[:, j % 2, :, 0:r],
                                      o_[:, 0:NP].rearrange("p (a b) -> p a b", b=P)[:, :, 0:r],
                                      pt_h[:, j % 2, :, 0:r], ALU.subtract).then_inc(drained["W1"], 1)

            for k in range(KC):
                lo(("cT", k), big[:, KC + k, 0:N], lambda o_: o_[:, 0:N], big[:, k, 0:N])
            for t in range(T):
                r = rows(t)
                own = tmp[0:r, 0, 0:D]
                step(normalise(own, acc[0:r, t, :], t))
                step(dve.tensor_tensor(own, own, row_c[0:r, 1, :], ALU.add))
                o_ = wait_filled(dve, ("sa", t))
                dve.tensor_tensor(tok[0:r, t, :], o_[0:r, :], own, ALU.add).then_inc(drained[jobs[("sa", t)][0]], 1)
                wait_drained(dve, ("sa", t))
            for t in range(T):
                moments(t, tok[0:rows(t), t, :])
            finish_moments()
            for t in range(T):
                r = rows(t)
                scaled_norm(tok, t, row_c[0:r, 2, :], row_c[0:r, 3, :]).then_inc(s_tok, 1)
            wait_filled(dve, ("cT", KC - 1))
            dve.memset(act_h[:, :, N:NP].bitcast(F32), 0.0).then_inc(s_pads, 1)
            wait_filled(dve, ("sa", T - 1))
            dve.memset(wg_f[:, :, :], 0.0).then_inc(s_pads, 1)
            for k in range(KC):
                lo(("tkT", k), act_l[:, k, 0:N], lambda o_: o_[:, 0:N], act_h[:, k, 0:N])
            dve.wait_ge(s_wg, 16)
            dve.tensor_copy(wg_h[:, :, :], wg_f[:, :, :]).then_inc(s_route, 1)
            dve.wait_ge(s_route, 1)
            dve.tensor_tensor(wg_l[:, :, :], wg_f[:, :, :], wg_h[:, :, :].bitcast(F32), ALU.subtract).then_inc(s_route, 1)
            o_ = wait_filled(dve, "logits")
            dve.tensor_scalar(lg_t[:, :], o_[0:NE, 0:NP], c_bg, None, ALU.add).then_inc(drained["W0"], 1)
            o_ = wait_filled(dve, "lgrows")
            step(dve.tensor_copy(lg[:, 0:T - 1, :], o_[:, 0:(T - 1) * NE].rearrange("p (t e) -> p t e", e=NE)))
            dve.tensor_copy(lg[0:last_r, T - 1, :], o_[0:last_r, (T - 1) * NE:T * NE]).then_inc(drained["N0"], 1)
            wait_drained(dve, "lgrows")
            for t in range(T):
                r = rows(t)
                step(dve.max(m8[0:r, t, :], lg[0:r, t, :]))
                step(dve.max_index(ix[0:r, t, :], m8[0:r, t, :], lg[0:r, t, :]))
                step(dve.tensor_copy(ixf[0:r, t:t + 1], ix[0:r, t, 0:1]))
                dve.tensor_scalar(oh[0:r, t, :], iota8[0:r, :], ixf[0:r, t:t + 1], None, ALU.is_equal).then_inc(s_route, 1)
            step(dve.memset(oh_t[:, N:NP].bitcast(F32), 0.0))
            o_ = wait_filled(dve, "ohT")
            dve.tensor_copy(oh_t[:, 0:N], o_[0:NE, 0:N]).then_inc(drained["W1"], 1)
            for e in range(NE):
                dve.tensor_scalar(sel[:, e, :], ones[0:NE, :], ident[0:NE, e:e + 1], None, ALU.mult).then_inc(s_route, 1)
            dve.wait_ge(s_b2, 16)
            dve.tensor_copy(b2_h[:, :], b2_f[:, :]).then_inc(s_route, 1)
            dve.wait_ge(s_route, 2 + T + NE + 1)
            dve.tensor_tensor(b2_l[:, :], b2_f[:, :], b2_h[:, :].bitcast(F32), ALU.subtract).then_inc(s_route, 1)
            for s in ("W0", "W1"):
                dve.wait_ge(drained[s], used[s])

            def fold_in(i, half):
                t = half * (T // 2) + i
                r = rows(t)
                dve.tensor_tensor(tok[0:r, t, :], ybank[i][0:r, :], tok[0:r, t, :], ALU.add).then_inc(s_yd, 1)

            def finish_rows(t):
                r = rows(t)
                scaled_norm(tok, t, row_c[0:r, 4, :], acc[0:r, t, :]).then_inc(s_fin, 1)

            ybank = [slot["W0"][:, 0:512], slot["W0"][:, 512:1024], slot["W0"][:, 1024:1536],
                     slot["W1"][:, 0:512], slot["W1"][:, 512:1024]]
            for r in range(2 * STEPS + 1):
                if r < 2 * STEPS:
                    g, j = divmod(r // 2, KC)
                    q, half = divmod(g, 2)
                    e = 2 * q + j // 2
                    c0 = half * HT + (r % 2) * PW
                    dve.wait_ge(s_gelu, r + 1)
                    if r >= 2:
                        dve.wait_ge(s_hl, r - 1)
                    dve.tensor_tensor(tmp[:, 1, (r % 2) * PW:(r % 2 + 1) * PW], tmp[:, 0, (r % 2) * PW:(r % 2 + 1) * PW],
                                      mask[:, e, c0:c0 + PW], ALU.mult).then_inc(s_hm, 1)
                if r:
                    q_ = r - 1
                    sl = slice((q_ % 2) * PW, (q_ % 2 + 1) * PW)
                    dve.wait_ge(s_hh, q_ + 1)
                    dve.tensor_tensor(hid_l[:, (q_ // 2) % 2, sl], tmp[:, 1, sl],
                                      hid_h[:, (q_ // 2) % 2, sl].bitcast(F32), ALU.subtract).then_inc(s_hl, 1)
                if 2 <= r < 2 + T:
                    t = r - 2
                    step(dve.tensor_tensor(acc[0:rows(t), t, :], acc[0:rows(t), t, :], row_c[0:rows(t), 5, :], ALU.add))
                if r > 1 and r % (2 * KC) == 1:
                    g = r // (2 * KC) - 1
                    dve.wait_ge(s_hused, KC * (g + 1))
                    for i in range(T // 2):
                        fold_in(i, g % 2)
                    if g == GROUPS - 2:
                        dve.wait_ge(s_yd, T // 2 * (g + 1))
                        for t in range(T // 2):
                            moments(t, tok[0:rows(t), t, :])
                        variances(0, T // 2)
                if r == R_LN + 1:
                    finish_moments(0, T // 2, begun=True)
                if R_LN + 1 <= r < R_LN + 1 + T // 2:
                    finish_rows(r - R_LN - 1)
            dve.wait_ge(s_hused, STEPS)
            for i in range(T // 2):
                fold_in(i, 1)
            dve.wait_ge(s_yd, T // 2 * GROUPS)
            for t in range(T // 2, T):
                moments(t, tok[0:rows(t), t, :])
            finish_moments(T // 2, T)
            for t in range(T // 2, T):
                finish_rows(t)


_INS = ["x", "src", "dst", "w_all", "mix_bq", "mix_bv", "mix_rows", "ffn_bq", "ffn_bk", "ffn_rows",
        "wg", "bg", "b1", "b2"]


def kernel(**inputs):
    import numpy as np
    import concourse.bacc as bacc
    from concourse.bass_utils import run_bass_kernel_spmd

    a = {k: np.asarray(v) for k, v in inputs.items()}

    def chunked(w):
        return np.ascontiguousarray(w.reshape(KC, P, -1).transpose(1, 0, 2))

    def column(b):
        return np.ascontiguousarray(b.reshape(-1, P).T)

    m, f = "L0_mix_", "L0_ffn_"
    units = [a["L0_gnn_W_neigh"].T, a["L0_gnn_W_self"].T, a[m + "Wq"].T, a[m + "Wk"].T, a[m + "Wv"].T,
             a[m + "Wo"], a[f + "Wv"], a[f + "Wq"], a[f + "Wk"], a[f + "Wo"]]
    for q in range(NE // 2):
        units.append(a[f + "W1"][2 * q:2 * q + 2].transpose(1, 0, 2).reshape(D, 2 * HID))
        units.append(a[f + "W2"][2 * q:2 * q + 2].reshape(2 * HID, D))
    arrays = {
        "x": a["x"], "src": a["src"], "dst": a["dst"],
        "w_all": np.stack([chunked(w) for w in units]),
        "mix_bq": column(a[m + "bq"]), "mix_bv": column(a[m + "bv"]),
        "mix_rows": np.stack([a["L0_gnn_b"], a[m + "bn_scale"], a[m + "bn_bias"], a[m + "bn_mean"],
                              a[m + "bn_var"], a[m + "bo"]]),
        "ffn_bq": column(a[f + "bq"]), "ffn_bk": column(a[f + "bk"]),
        "ffn_rows": np.stack([a[f + "bv"], a[f + "bo"], a[f + "g1"], a[f + "beta1"], a[f + "g2"], a[f + "beta2"]]),
        "wg": chunked(a[f + "Wg"]), "bg": a[f + "bg"].reshape(NE, 1),
        "b1": column(a[f + "b1"]), "b2": a[f + "b2"],
    }
    nc = bacc.Bacc("TRN2", target_bir_lowering=False, num_devices=1)
    args = []
    for name in _INS:
        arrays[name] = np.ascontiguousarray(arrays[name])
        args.append(nc.dram_tensor("in_" + name, arrays[name].shape, mybir.dt.from_np(arrays[name].dtype),
                                   kind="ExternalInput").ap())
    args.append(nc.dram_tensor("out_rows", (N, D), F32, kind="ExternalOutput").ap())
    gps_layer(nc, *args)
    r = run_bass_kernel_spmd(nc, [{"in_" + k: v for k, v in arrays.items()}], core_ids=[0])
    return r.results[0]["out_rows"]
```

```python
import concourse.bass as bass
from concourse import mybir
from contextlib import ExitStack

F32 = mybir.dt.float32
F32R = mybir.dt.float32r
BF16 = mybir.dt.bfloat16
F16 = mybir.dt.float16
I32 = mybir.dt.int32
U32 = mybir.dt.uint32
ALU = mybir.AluOpType
ACT = mybir.ActivationFunctionType
AX = mybir.AxisListType

N, D, E = 1250, 512, 20000
P = 128
T = -(-N // P)
NP = T * P
KC = D // P
HT = NP // 2
PW = HT // 2
PIECES = [(0, 512), (512, 1024), (1024, NP)]
COUNT_PIECES = [(0, 512), (512, 1024), (1024, NP + 2)]
HB = 3
CE = 125
CH = E // CE
FEW = 4096 // CE
CP = CH // 2
NH, DH = 8, 64
UB = 5
ZR = 32
NE, HID = 8, 256
UNITS = NH * T
LN_EPS = 1e-5
BIG = 10000.0


def rows(t):
    return min(P, N - t * P)


def cols(t):
    return slice(t * P, t * P + rows(t))


def gps_layer(nc, x, src, dst, w_all, mix_bq, mix_bv, mix_rows, ffn_bq, ffn_bk, ffn_g1, ffn_beta1,
              ffn_rows, wg, bg, b1, b2, out):
    ctx = ExitStack()
    with ctx:
        arena = ctx.enter_context(nc.sbuf_tensor("arena", [P, 212480 // 4], F32))
        base = (nc.sbuf_base - 212480)
        at = [base + (-base) % 32]

        def place(name, shape, dt, offset):
            return nc.alloc_sbuf_tensor_at(name, shape, dt, offset=offset)

        def region(size):
            o = at[0]
            at[0] += -(-size // 32) * 32
            return o

        r_act, r_b, r_w, r_stage = region(40960), region(40960), region(32768), region(8192)
        r_acc, r_rows, r_p, r_over = region(20480), region(12288), region(10240), region(40960)

        def small(name, shape, dt):
            n = 1
            for s in shape[1:]:
                n *= s
            return place(name, shape, dt, region(n * mybir.dt.size(dt)))

        act_h = place("act_h", [P, KC, NP], F32R, r_act)
        act_l = place("act_l", [P, KC, NP], F32R, r_act + 20480)
        context_f = place("context_f", [P, KC, NP], F32, r_act + 20480)
        big = place("big", [P, 2 * KC, NP], F32R, r_b)
        y_h = place("y_h", [P, T, D], F32R, r_b)
        y_l = place("y_l", [P, T, D], F32R, r_b + 20480)
        rows_b = place("rows_b", [P, T, D], F32, r_b)
        mask = place("mask", [P, NE, NP], BF16, r_b)
        w_h = place("w_h", [P, 2, KC, D], F32R, r_w)
        w_l = place("w_l", [P, 2, KC, D], F32R, r_w + 16384)
        w3_h = place("w3_h", [P, KC, D], F32R, r_b + 20480)
        w3_l = place("w3_l", [P, KC, D], F32R, r_b + 28672)
        stage = place("stage", [P, KC, D], F32, r_stage)
        acc = place("acc", [P, T, D], F32, r_acc)
        prob = place("prob", [P, 2, NP], F32, r_p)
        adj_h = place("adj_h", [P, NP], F32R, r_p)
        adj_l = place("adj_l", [P, NP], F32R, r_p + 5120)
        tmp = place("tmp", [P, 2, NP], F32, r_p)
        scaled = place("scaled", [P, KC, D], F32, r_p)
        row_c = place("row_c", [P, 6, D], F32, r_rows)
        fold_h = place("fold_h", [P, KC, D], F32R, r_over)
        fold_l = place("fold_l", [P, KC, D], F32R, r_over + 8192)
        o = r_over + 16384
        col_acc = place("col_acc", [P, NP], F32, o)
        counts = place("counts", [P, NP + 2], F32, o); o += 5152
        hot_src = place("hot_src", [P, HB, NP + 2], BF16, o)
        bv_rep_h = place("bv_rep_h", [P, KC, P], F32R, o)
        bv_rep_l = place("bv_rep_l", [P, KC, P], F32R, o + 2048); o += 7712
        hot_dst = place("hot_dst", [P, HB, P], BF16, o); o += 768
        bn_work = place("bn_work", [P, 2, D], F32, o)
        iota16 = place("iota16", [P, NP], F16, o); o += 2560
        edge_i = place("edge_i", [CP, 4, CE], I32, o)
        edge_f = place("edge_f", [CP, 4, CE], F32, o + 2016); o += 4032
        work1 = place("work1", [P, D], F32, o); o += 2048
        assert o <= r_over + 40960
        val_h = place("val_h", [P, T, NH, DH + ZR], F32R, r_p)
        val_l = place("val_l", [P, T, NH, DH], F32R, r_p + 30720)
        val_f = place("val_f", [P, T, NH, DH], F32, r_p + 30720)
        stack_x = place("stack_x", [P, 4, NP], F32R, r_acc)
        sums = [place("sums%d" % i, [P, NP], F32, o) for i, o in enumerate((r_b, r_b + 20480, r_acc))]
        pr = place("pr", [P, 2, NP], F32, r_w)
        pr_l = place("pr_l", [P, 2, NP], F32R, r_w)
        pr_h = place("pr_h", [P, 2, NP], F32R, r_w + 10240)
        piece_max = place("piece_max", [P, T, 3], F32, r_w + 20480)
        neg_max = place("neg_max", [P, P], F32, r_w + 20608)
        inverse = place("inverse", [P, P], F32, r_w + 21120)
        row_parts = place("row_parts", [P, P], F32, r_w + 21632)
        tile_mask = place("tile_mask", [P, T], F32, r_w + 22144)
        u_rows = place("u_rows", [P, UB, D], F32, r_p)
        tok = place("tok", [P, T, D], F32, r_over)
        hid_h = place("hid_h", [P, 2, 640], F32R, r_over + 30720)
        hid_l = place("hid_l", [P, 2, 640], F32R, r_over + 35840)
        ident = small("ident", [P, P], F32)
        ones = small("ones", [P, P], F32)
        zero16 = small("zero16", [P, D], BF16)
        edge_t = small("edge_t", [CE, 2, CH + HB - 1], F32)
        lohi = small("lohi", [CP, 4], F32)
        mv = small("mv", [P, T, 2], F32)
        st6 = small("st6", [P, 2, 6], F32)
        ve = small("ve", [P, T], F32)
        rs = small("rs", [P, T], F32)
        nr = small("nr", [P, T], F32)
        rdeg = small("rdeg", [P, T], F32)
        z_mix = small("z_mix", [P, T], F32)
        nmax = small("nmax", [P, T], F32)
        gain_u = small("gain_u", [P, T], F32)
        shift_u = small("shift_u", [P, T], F32)
        rs_u = small("rs_u", [P, T], F32)
        cfac = small("cfac", [P, T], F32)
        zt = small("zt", [P, T], F32)
        cols_c = small("cols_c", [P, 6 * KC + 16 + 1], F32)
        bq_pair = small("bq_pair", [P, KC, 2], F32R)
        bt = small("bt", [P, KC], F32)
        tile_lo = small("tile_lo", [T, 2], F32)
        span = small("span", [T, 4], F32)
        span_i = small("span_i", [T, 3], I32)
        o = r_over + 16384
        diag = place("diag", [CP, 4, CP], F32, o)
        cover = place("cover", [T, CH], F32, o + 1280)
        cover2 = place("cover2", [T, CH], F32, o + 1920)
        chunk_no = place("chunk_no", [T, CH], F32, o + 2560)
        wg_h = place("wg_h", [P, KC, P], F32R, r_over + 30720)
        wg_l = place("wg_l", [P, KC, P], F32R, r_over + 32768)
        wg_f = place("wg_f", [P, KC, P], F32, r_over + 34816)
        lg_t = place("lg_t", [NE, NP], F32, r_p)
        gel = place("gel", [P, 2, 2 * PW], F32, r_p)
        oh_t = place("oh_t", [NE, NP], F32R, r_p + 5120)
        b2_f = place("b2_f", [NE, D], F32, r_over + 26048)
        sel = place("sel", [NE, NE, P], BF16, r_b + 36864)
        oh_t16 = place("oh_t16", [NE, NP], BF16, r_over + 28096)
        b2_h = place("b2_h", [NE, D], F32R, r_over + 24000)
        b2_l = place("b2_l", [NE, D], F32R, r_over + 20480)
        lg = place("lg", [P, T, NE], F32, r_over + 22528)
        cand = place("cand", [P, T, NE], F32, r_over + 22848)
        best = place("best", [P, T], F32, r_over + 23168)
        oh = place("oh", [P, T, NE], F32, r_over + 23552)
        iota8 = small("iota8", [P, NE], F32)
        assert at[0] <= nc.sbuf_usable_end, (at[0], nc.sbuf_usable_end)

        c_mbq, c_mbv = cols_c[:, 0:KC], cols_c[:, KC:2 * KC]
        c_fbq, c_fbk = cols_c[:, 2 * KC:3 * KC], cols_c[:, 3 * KC:4 * KC]
        c_g1, c_beta1 = cols_c[:, 4 * KC:5 * KC], cols_c[:, 5 * KC:6 * KC]
        c_b1, c_bg = cols_c[:, 6 * KC:6 * KC + 16], cols_c[0:NE, 6 * KC + 16:6 * KC + 17]

        qk_dram = nc.dram_tensor("qk_dram", [2, NH, 2, DH, NP], F32, kind="Internal").ap()
        x1_dram = nc.dram_tensor("x1_dram", [N, D], F32, kind="Internal").ap()

        slot = {s: ctx.enter_context(nc.psum_tensor(s, [P, 512 * n], F32))[:, :]
                for s, n in (("W0", 3), ("W1", 3), ("N0", 1), ("N1", 1))}

        A1, A2 = T // 2, T - 2

        def sem(name):
            return ctx.enter_context(nc.semaphore(name))

        filled = {s: sem("filled_" + s) for s in slot}
        drained = {s: sem("drained_" + s) for s in slot}
        jobs, used = {}, {s: 0 for s in slot}

        def book(key, s):
            jobs[key] = (s, used[s])
            used[s] += 1

        for k in range(KC):
            book(("xT", k), "W%d" % (k % 2))
        for t in range(T):
            book(("y", t), "N%d" % (t % 2))
        book("edges", "W0")
        book("ranges", "W1")
        for t in range(T):
            book(("hist", t), "W0")
            book(("AT", t), "W1")
            book(("self", t), "N0")
            book(("agg", t), "N1")
        for m in range(KC):
            book(("foldM", m), "N%d" % (m % 2))
        book("bt", "N0")
        for m in range(KC):
            book(("tT", m), "W%d" % (m % 2))
        for t in range(T):
            book(("score", t), "W%d" % (t % 2))
        for m in range(KC):
            book(("foldN", m), "N%d" % (m % 2))
        book("bvo", "N0")
        book("colsum", "N1")
        for t in range(T):
            book(("o", t), "N%d" % (t % 2))
        for k in range(KC):
            book(("uT", k), "W%d" % (k % 2))
        for i in range(2 * KC):
            book(("qk", i), "W%d" % (i % 2))
        for t in range(T):
            book(("v", t), "W%d" % (t % 2))
        pieces_no = [0]

        def book_narrow(key):
            book(key, "N%d" % (pieces_no[0] % 2))
            pieces_no[0] += 1

        def max_tiles(i):
            h, t = divmod(i, T)
            return [(h + 1, a) for a in ([0, 1] if t == 0 else [t + 1] if t < T - 1 else []) if h + 1 < NH]

        def book_maxima(h, t):
            for c in range(len(PIECES)):
                book_narrow(("max", h, t, c))
            if t == T - 1:
                book_narrow(("turn", h))

        for t in range(T):
            book_maxima(0, t)
        def chores(h, t):
            return {1: [("divisors", h)], 2: [("inverse", h)], 3: [("spread", h, 0), ("spread", h, 1)],
                    4: [("spread", h, 2)]}.get(t, [])

        def narrow_jobs(i):
            h, t = divmod(i, T)
            jobs_ = [("max", a, b, c) for a, b in max_tiles(i) for c in range(len(PIECES))]
            if any(b == T - 1 for a, b in max_tiles(i)):
                jobs_.append(("turn", h + 1))
            extra = chores(h - 1, t) if h else []
            return extra + jobs_ if t == 4 else jobs_ + extra

        for i in range(UNITS):
            book(("ST", i), "W0")
            for key in narrow_jobs(i):
                book_narrow(key)
        for t in range(1, 5):
            for key in chores(NH - 1, t):
                book_narrow(key)
        for h in range(NH):
            book(("AV", h), "W1")
        for g in range(2):
            book(("sa3", g), "W%d" % g)
        for t in range(6, T):
            book(("sa", t), "N%d" % (t % 2))
        for k in range(KC):
            book(("tkT", k), "W%d" % (k % 2))
        book("logits", "W0")
        book("lgrows", "W1")
        book("ohT", "W1")
        for e in range(NE):
            book(("mask", e), "W%d" % (e % 2))

        def wait_filled(eng, key):
            s, n = jobs[key]
            eng.wait_ge(filled[s], n + 1)
            return slot[s]

        def wait_drained(eng, key):
            s, n = jobs[key]
            eng.wait_ge(drained[s], n + 1)

        s_x = [sem("x_in%d" % t) for t in range(T)]
        s_edge, s_const = sem("edges_in"), sem("column_constants_in")
        s_rowc, s_ffnrow = sem("mix_rows_in"), sem("ffn_rows_in")
        s_stage, s_split, s_scaled = sem("weights_in"), sem("weights_split"), sem("q_weights_scaled")
        s_bq8 = sem("bq_scaled")
        s_setup = sem("setup")
        s_step = sem("vector_step")
        s_ef, s_dg, s_span = sem("edge_floats"), sem("diag_ready"), sem("span_ready")
        s_var, s_sqrt = sem("variance_ready"), sem("sqrt_ready")
        s_rows = sem("rows_by_vector")
        s_rows_a = sem("rows_by_scalar")
        s_stats, s_aggr = sem("x_statistics"), sem("x_moments")
        s_shift_u = sem("row_shifts")
        s_hi = sem("hi_written")
        s_hot = [sem("onehots_ready%d" % i) for i in range(HB)]
        s_hotfree = [sem("onehots_used%d" % i) for i in range(HB)]
        s_deg = sem("degrees_read")
        s_gain, s_fold = sem("fold_scaled"), sem("fold_split")
        s_max, s_exp, s_pfree = sem("mix_max"), sem("mix_exp"), sem("mix_prob_used")
        s_bqp, s_bvr = sem("bq_pair_ready"), sem("bv_rep_ready")
        s_vh, s_vl, s_vpad = sem("v_hi"), sem("v_lo"), sem("v_blocks")
        s_store = [sem("qk_store%d" % i) for i in range(4)]
        s_stack = [sem("stack_in%d" % i) for i in range(3)]
        s_amax, s_spread = sem("maxima_found"), sem("inverses_in_stack")
        s_clear, s_shift, s_ppad = sem("stack_cleared"), sem("maxima_in_stack"), sem("prob_pads")
        s_phi, s_plo, s_av = sem("prob_hi"), sem("prob_lo"), sem("prob_used")
        s_ctx, s_chi, s_clo = sem("context_ready"), sem("context_hi"), sem("context_lo")
        s_spill, s_x1 = sem("x1_stored"), sem("x1_back")
        s_pads, s_mixdone = sem("pads_zeroed"), sem("mix_rows_done")
        s_u, s_ubo, s_tile = sem("u_ready"), sem("u_with_bias"), sem("last_sums")
        s_summed, s_scaled_t, s_tlo = sem("u_used"), sem("token_columns"), sem("token_columns_used")
        s_tok, s_route = sem("tokens_ready"), sem("router_step")
        s_oh = sem("onehot_columns")
        s_wg, s_b2 = sem("router_weights_in"), sem("b2_in")
        s_gelu, s_hm, s_hh, s_hl = sem("gelu"), sem("hidden_masked"), sem("hidden_hi"), sem("hidden_lo")
        s_hfill = [sem("h_filled%d" % i) for i in range(3)]
        s_yd, s_hused = sem("sums_added"), sem("hidden_used")
        s_fin, s_out = sem("row_final"), sem("out_stored")

        W_NEIGH, W_SELF, W_QT, W_KT, W_VT, W_MO, W_Q, W_K, W_V, W_O = range(10)
        FREE = {W_KT: ("y", T - 1), W_VT: ("foldM", KC - 1), W_MO: "bt", W_Q: ("foldN", KC - 1), W_K: "bvo",
                W_V: ("qk", 5)}
        QK = [(0, 0), (0, 1), (1, 0), (1, 1), (0, 2), (0, 3), (1, 2), (1, 3)]
        Q1, Q2, K1, K2 = range(4)

        def stack(h):
            b = (h + 2) % 3
            return stack_x if b == 2 else big[:, 4 * b:4 * b + 4, :]
        UP, DOWN = 10, 11
        GROUPS = NE // 2 * 2
        n_units = UP + NE
        STEPS = GROUPS * KC
        R_LN = 2 * KC * (GROUPS - 1) + 2

        def ring(u):
            if u == W_SELF:
                return fold_h[:, :, :], fold_l[:, :, :]
            s_ = (0, None, 1, 0, 1, 0, 1, 0, 1, 2)[u] if u < UP else (u - UP) % 3
            return (w3_h[:, :, :], w3_l[:, :, :]) if s_ == 2 else (w_h[:, s_], w_l[:, s_])

        block = ctx.enter_context(nc.Block())

        @block.sync
        def _(sp):
            for t in range(T):
                sp.dma_start(acc[0:rows(t), t, :], x[cols(t), :]).then_inc(s_x[t], 16)
            sp.dma_start(edge_i[:, 0:2, :], src.rearrange("(j p e) -> p j e", j=2, p=CP)).then_inc(s_edge, 16)
            sp.dma_start(edge_i[:, 2:4, :], dst.rearrange("(j p e) -> p j e", j=2, p=CP)).then_inc(s_edge, 16)
            for i, a in enumerate((mix_bq, mix_bv, ffn_bq, ffn_bk, ffn_g1, ffn_beta1)):
                sp.dma_start(cols_c[:, i * KC:(i + 1) * KC], a).then_inc(s_const, 16)
            sp.dma_start(c_b1, b1).then_inc(s_const, 16)
            sp.dma_start(c_bg, bg).then_inc(s_const, 16)

            def unit(u):
                if u:
                    sp.wait_ge(s_split, 2 * u)
                sp.dma_start(stage[:, :, :], w_all[u]).then_inc(s_stage, 16)

            unit(0)
            for i in range(6):
                sp.dma_start(row_c[:, i, :], mix_rows[i:i + 1, :].to_broadcast([P, D])).then_inc(s_rowc, 16)
            for u in range(1, W_O):
                unit(u)
            sp.wait_ge(s_mixdone, T)
            for i in range(6):
                sp.dma_start(row_c[:, i, :], ffn_rows[i:i + 1, :].to_broadcast([P, D])).then_inc(s_ffnrow, 16)
            for t in range(T):
                sp.dma_start(x1_dram[cols(t), :], acc[0:rows(t), t, :]).then_inc(s_spill, 16)

            def load_stack(h):
                b, st = (h + 2) % 3, stack(h)
                sp.dma_start(st[:, Q1, :].bitcast(F32), qk_dram[0, h].rearrange("a d n -> (a d) n")).then_inc(s_stack[b], 16)
                for dst_, which, part in ((st[0:DH, Q2, :], 0, 0), (st[0:DH, K1, :], 1, 0),
                                          (st[DH:P, K1, :], 1, 0), (st[0:DH, K2, :], 1, 1)):
                    sp.dma_start(dst_.bitcast(F32), qk_dram[which, h, part]).then_inc(s_stack[b], 16)

            for i, (which, k) in enumerate(QK):
                wait_drained(sp, ("qk", i))
                for part in range(2):
                    for hh in range(2):
                        sp.dma_start(qk_dram[which, 2 * k + hh, part],
                                     big[hh * DH:(hh + 1) * DH, part * KC + i % KC, :].bitcast(F32)) \
                          .then_inc(s_store[i % 4], 16)
                if i == 3:
                    sp.wait_ge(s_store[0], 64)
                    sp.wait_ge(s_store[2], 64)
                    sp.wait_ge(s_spill, 16 * T)
                    sp.wait_ge(s_rows_a, A1 + A2)
                    sp.wait_ge(s_rows, 2 * T - A1 - A2)
                    load_stack(0)
            for i in range(4):
                sp.wait_ge(s_store[i], 2 * 64)
            unit(W_O)
            for h in range(1, NH):
                if h >= 3:
                    sp.wait_ge(s_ctx, h - 2)
                load_stack(h)
            sp.wait_ge(s_ctx, 7)
            for t in range(T):
                sp.dma_start(acc[0:rows(t), t, :], x1_dram[cols(t), :]).then_inc(s_x1, 16)
            wait_filled(sp, ("AV", NH - 1))
            sp.wait_ge(s_pads, 1)
            sp.dma_start(wg_f[:, :, 0:NE], wg).then_inc(s_wg, 16)
            sp.dma_start(b2_f[:, :], b2).then_inc(s_b2, 16)
            unit(UP)
            for u in range(DOWN, n_units):
                unit(u)
            for t in range(T):
                sp.wait_ge(s_fin, t + 1)
                sp.dma_start(out[cols(t), :], tok[0:rows(t), t, :]).then_inc(s_out, 16)
            sp.wait_ge(s_out, 16 * T)

        @block.gpsimd
        def _(pool):
            pool.memset(ident[:, :], 0.0).then_inc(s_setup, 1)
            pool.memset(ones[:, :], 1.0).then_inc(s_setup, 1)
            pool.memset(hot_src[:, :, NP:NP + 2], 1.0).then_inc(s_setup, 1)
            pool.memset(mv[:, :, :], 1.0).then_inc(s_setup, 1)
            pool.wait_ge(s_setup, 4)
            pool.affine_select(out=ident[:, :], in_=ident[:, :], compare_op=ALU.not_equal, fill=1.0,
                               base=0, pattern=[[-1, P]], channel_multiplier=1).then_inc(s_setup, 1)
            pool.iota(tile_lo[:, 0:1], [[0, 1]], 0, P, allow_small_or_imprecise_dtypes=True).then_inc(s_setup, 1)
            pool.iota(tile_lo[:, 1:2], [[0, 1]], P - 1, P, allow_small_or_imprecise_dtypes=True).then_inc(s_setup, 1)
            pool.iota(chunk_no[:, :], [[1, CH]], 0, 0, allow_small_or_imprecise_dtypes=True).then_inc(s_setup, 1)
            pool.iota(iota16[:, :], [[1, NP]], 0, 0, allow_small_or_imprecise_dtypes=True).then_inc(s_setup, 1)
            pool.memset(zero16[:, :], 0.0).then_inc(s_setup, 1)
            pool.iota(iota8[:, :], [[1, NE]], 0, 0, allow_small_or_imprecise_dtypes=True).then_inc(s_setup, 1)
            for b in range(HB):
                pool.sem_inc(s_hotfree[b], 1)
            for a in (act_h, act_l):
                pool.memset(a[:, :, N:NP].bitcast(F32), 0.0).then_inc(s_setup, 1)
            for u in range(n_units):
                pool.wait_ge(s_stage, 16 * (u + 1))
                if u == UP + 2:
                    wait_filled(pool, ("sa", T - 1))
                elif u > UP + 2:
                    v = u - 3
                    n = KC * ((v - UP) // 2 * 2 + 2)
                    if (v - UP) % 2:
                        pool.wait_ge(s_hused, n)
                    else:
                        r = 2 * n - 1
                        pool.wait_ge(s_hfill[r % 3], r // 3 + 1)
                elif u in FREE:
                    wait_filled(pool, FREE[u])
                if u == W_O:
                    pool.wait_ge(s_ctx, 6)
                if u == UP:
                    for t in range(T):
                        r = rows(t)
                        pool.wait_ge(s_u, t + 1)
                        pool.wait_ge(s_split, 2 * u)
                        if t:
                            pool.wait_ge(s_ubo, t)
                        pool.tensor_tensor(u_rows[0:r, t % UB, :], u_rows[0:r, t % UB, :], row_c[0:r, 1, :], ALU.add) \
                            .then_inc(s_ubo, 1)
                    pool.wait_ge(s_ubo, T)
                    pool.wait_ge(s_ctx, NH)
                if u == W_Q:
                    pool.tensor_scalar(stage[:, :, :], stage[:, :, :], DH ** -0.5, None, ALU.mult).then_inc(s_scaled, 1)
                    pool.wait_ge(s_scaled, 1)
                u_h, u_l = ring(u)
                pool.tensor_copy(u_h, stage[:, :, :]).then_inc(s_split, 1)
                pool.wait_ge(s_split, 2 * u + 1)
                pool.tensor_tensor(u_l, stage[:, :, :], u_h.bitcast(F32), ALU.subtract) \
                    .then_inc(s_split, 1)
                if u == W_V:
                    pool.wait_ge(s_split, 2 * (u + 1))
                    for h in range(NH):
                        if h == 0:
                            pool.wait_ge(s_spill, 16 * T)
                            pool.wait_ge(s_rows_a, A1 + A2)
                            pool.wait_ge(s_rows, 2 * T - A1 - A2)
                        elif h < 3:
                            for i in range(4):
                                pool.wait_ge(s_store[i], 2 * 64)
                        else:
                            pool.wait_ge(s_ctx, h - 2)
                        for c, (a, v) in enumerate(((Q2, 0.0), (K2, 1.0))):
                            pool.memset(stack(h)[DH:P, a, :].bitcast(F32), v).then_inc(s_clear, 1)
                            pool.wait_ge(s_clear, 2 * h + c + 1)

        @block.tensor
        def _(pe):
            def begin(key):
                s, n = jobs[key]
                if n:
                    pe.wait_ge(drained[s], n)
                return slot[s]

            def end(ins, key):
                ins.then_inc(filled[jobs[key][0]], 1)

            def weights(u):
                pe.wait_ge(s_split, 2 * (u + 1))
                return ring(u)

            def rows_product(out_ap, ah, al, sl, wh, wl, start=True, stop=True, ready=None):
                steps = [(a, w, k) for k in range(KC) for a, w in ((ah, wh), (ah, wl), (al, wh))]
                for i, (a, w, k) in enumerate(steps):
                    if ready and i % 3 == 0:
                        ready(k)
                    last = pe.matmul(out_ap, a[:, k, sl], w[:, k, :], start=start and i == 0,
                                     stop=stop and i == len(steps) - 1)
                return last

            def feature_product(out_t, wh, wl, m, ah, al, pieces=PIECES, ready=None):
                for c0, c1 in pieces:
                    steps = [(a, w, k) for k in range(KC) for a, w in ((ah, wh), (al, wh), (ah, wl))]
                    for i, (a, w, k) in enumerate(steps):
                        if ready and c0 == 0 and i % 3 == 0:
                            ready(k)
                        last = pe.matmul(out_t[:, c0:c1], w[:, k, m], a[:, k, c0:c1],
                                         start=i == 0, stop=i == len(steps) - 1)
                return last

            def transposes(tag, src_rows, ready):
                for k in range(KC):
                    o_ = begin((tag, k))
                    for t in range(T):
                        if k == 0:
                            ready(t)
                        last = pe.transpose(o_[:, cols(t)], src_rows[0:rows(t), t, k * P:(k + 1) * P],
                                            ident[0:rows(t), 0:rows(t)])
                    end(last, (tag, k))

            def chunk(m):
                return slice(m * P, (m + 1) * P)

            def split_of(tag, first):
                return (lambda k: wait_drained(pe, (tag, k))) if first else None

            pe.wait_ge(s_setup, 13)
            transposes("xT", rows_b, lambda t: pe.wait_ge(s_rows_a, t + 1) if t < A1
                       else pe.wait_ge(s_rows, t + 1 - A1))
            wh, wl = weights(W_NEIGH)
            for t in range(T):
                end(rows_product(begin(("y", t))[0:rows(t), :], act_h, act_l, cols(t), wh, wl,
                                 ready=split_of("xT", t == 0)), ("y", t))
                if t == 3:
                    pe.wait_ge(s_ef, 1)
                    o_ = begin("edges")
                    for j in range(4):
                        last = pe.transpose(o_[0:CE, j * CP:(j + 1) * CP], edge_f[:, j, :], ident[0:CP, 0:CP])
                    end(last, "edges")
                if t == 5:
                    pe.wait_ge(s_dg, 4)
                    o_ = begin("ranges")
                    end(pe.matmul(o_[0:T, 0:2 * CH], ones[0:CP, 0:T], diag[:, :, :], start=True, stop=True), "ranges")

            pe.wait_ge(s_span, 1)
            ticket = pe.alloc_register("pe_steps")
            pe.reg_mov(ticket, 0)
            for t in range(T + 1):
                if t < T:
                    o_ = begin(("hist", t))
                    for c0, c1 in COUNT_PIECES:
                        pe.matmul(o_[:, c1 - 2:c1], zero16[:, 0:P], zero16[:, 0:2], start=True, stop=True)
                    c_first = pe.value_load(span_i[t:t + 1, 0:1], min_val=0, max_val=CH - 1)
                    c_end = pe.value_load(span_i[t:t + 1, 1:2], min_val=1, max_val=CH)
                    with pe.Fori(c_first, c_end, HB):
                        pe.reg_add(ticket, ticket, 1)
                        for b in range(HB):
                            pe.wait_ge(s_hot[b], pe.snap(ticket))
                            for c0, c1 in COUNT_PIECES:
                                last = pe.matmul(o_[:, c0:c1], hot_dst[0:CE, b, :], hot_src[0:CE, b, c0:c1],
                                                 start=False, stop=True, skip_group_check=True)
                            last.then_inc(s_hotfree[b], 1)
                    end(pe.matmul(o_[:, NP:NP + 2], zero16[:, 0:P], zero16[:, 0:2], start=False, stop=True,
                                  skip_group_check=True), ("hist", t))
                if t:
                    v = t - 1
                    wh, wl = weights(W_SELF)
                    end(rows_product(begin(("self", v))[0:rows(v), :], act_h, act_l, cols(v), wh, wl), ("self", v))
                    o_ = begin(("agg", v))
                    wait_drained(pe, ("AT", v))
                    if v == 0:
                        for tt in (T - 2, T - 1):
                            wait_drained(pe, ("y", tt))

                    def neighbours(a, y, j, start=False, stop=False):
                        return pe.matmul(o_[0:rows(v), :], a[0:rows(j), j * P:j * P + rows(v)], y[0:rows(j), j, :],
                                         start=start, stop=stop, skip_group_check=True)

                    for j in range(T):
                        neighbours(adj_h, y_h, j, start=j == 0)
                    many = pe.value_load(span_i[v:v + 1, 2:3], min_val=0, max_val=1)
                    with pe.If(many > 0):
                        for j in range(T):
                            neighbours(adj_l, y_h, j)
                    for j in range(T):
                        last = neighbours(adj_h, y_l, j, stop=j == T - 1)
                    end(last, ("agg", v))
                if t < T:
                    wait_drained(pe, ("hist", t))
                    o_ = begin(("AT", t))
                    for j in range(T):
                        last = pe.transpose(o_[:, chunk(j)], counts[:, chunk(j)], ident[:, :])
                    end(last, ("AT", t))

            qh, ql = weights(W_QT)
            kh, kl = weights(W_KT)
            for m in range(KC):
                end(rows_product(begin(("foldM", m)), qh, ql, chunk(m), kh, kl), ("foldM", m))
            pe.wait_ge(s_bqp, 2)
            o_ = begin("bt")
            for m in range(KC):
                steps = [(w, k) for k in range(KC) for w in (kh, kl)]
                for i, (w, k) in enumerate(steps):
                    last = pe.matmul(o_[:, 2 * m:2 * m + 2], w[:, k, chunk(m)], bq_pair[:, k, :],
                                     start=i == 0, stop=i == len(steps) - 1)
            end(last, "bt")
            for m in range(KC):
                end(feature_product(begin(("tT", m)), fold_h, fold_l, chunk(m), act_h, act_l,
                                    ready=split_of("foldM", m == 0)), ("tT", m))
            for t in range(T):
                o_ = begin(("score", t))
                for c0, c1 in PIECES:
                    steps = [(a, b, k) for k in range(KC) for a, b in ((0, act_h), (0, act_l), (KC, act_h))]
                    for i, (a, b, k) in enumerate(steps):
                        if t == 0 and c0 == 0 and i % 3 == 0:
                            wait_drained(pe, ("tT", k))
                        last = pe.matmul(o_[0:rows(t), c0:c1], big[:, a + k, cols(t)], b[:, k, c0:c1],
                                         start=i == 0, stop=i == len(steps) - 1)
                end(last, ("score", t))

            vh, vl = weights(W_VT)
            oh_, ol_ = weights(W_MO)
            for m in range(KC):
                end(rows_product(begin(("foldN", m)), vh, vl, chunk(m), oh_, ol_), ("foldN", m))
            pe.wait_ge(s_bvr, 2 * KC)
            end(rows_product(begin("bvo"), bv_rep_h, bv_rep_l, slice(0, P), oh_, ol_), "bvo")
            pe.wait_ge(s_pfree, T)
            o_ = begin("colsum")
            for t in range(T):
                last = pe.matmul(o_[0:rows(t), t:t + 1], col_acc[:, cols(t)], ones[:, 0:1], start=True, stop=True)
            end(last, "colsum")
            wait_drained(pe, "bvo")
            for t in range(T):
                o_ = begin(("o", t))[0:rows(t), :]
                rows_product(o_, act_h, act_l, cols(t), fold_h, fold_l, stop=False,
                             ready=(lambda k: pe.wait_ge(s_fold, k + 1)) if t == 0 else None)
                end(pe.matmul(o_, ones[0:1, 0:rows(t)], row_c[0:1, 3, :], start=False, stop=True), ("o", t))

            transposes("uT", rows_b, lambda t: pe.wait_ge(s_rows_a, A1 + t + 1) if t < A2
                       else pe.wait_ge(s_rows, T - A1 + t + 1 - A2))
            for i in range(2 * KC):
                which, k = QK[i]
                wh, wl = weights(W_Q + which)
                end(feature_product(begin(("qk", i)), wh, wl, chunk(k), act_h, act_l,
                                    ready=split_of("uT", i == 0)), ("qk", i))

            def narrow(key):
                kind, h = key[:2]
                st, raw = stack(h), sums[(h + 2) % 3]
                if kind == "max":
                    t, c = key[2:]
                    c0, c1 = PIECES[c]
                    if t == 0 and c == 0:
                        pe.wait_ge(s_stack[(h + 2) % 3], 80 * (h // 3 + 1))
                        pe.wait_ge(s_clear, 2 * h + 2)
                    o_ = begin(key)
                    pe.matmul(o_[0:rows(t), 0:c1 - c0], st[:, Q1, cols(t)], st[:, K1, c0:c1], start=True, stop=False)
                    last = pe.matmul(o_[0:rows(t), 0:c1 - c0], st[:, Q2, cols(t)], st[:, K2, c0:c1], start=False,
                                     stop=True)
                if kind == "turn":
                    o_ = begin(key)
                    pe.wait_ge(s_amax, h + 1)
                    last = pe.transpose(o_[:, 0:P], neg_max[:, :], ident[:, :])
                if kind == "divisors":
                    o_ = begin(key)
                    wait_drained(pe, ("AV", h))
                    for j in range(T):
                        last = pe.transpose(o_[0:rows(j), j * ZR:(j + 1) * ZR], raw[DH:DH + ZR, cols(j)],
                                            ident[DH:DH + ZR, DH:DH + ZR])
                if kind == "inverse":
                    o_ = begin(key)
                    wait_drained(pe, ("divisors", h))
                    last = pe.transpose(o_[:, 0:P], inverse[:, :], ident[:, :])
                if kind == "spread":
                    c0, c1 = PIECES[key[2]]
                    o_ = begin(key)
                    pe.wait_ge(s_spread, h + 1)
                    last = pe.matmul(o_[:, 0:c1 - c0], st[DH:P, K2, 0:P], st[DH:P, Q2, c0:c1], start=True, stop=True)
                end(last, key)

            def shifted_scores(i):
                h, t = divmod(i, T)
                st = stack(h)
                if t == 0:
                    pe.wait_ge(s_shift, h + 1)
                o_ = begin(("ST", i))
                for c0, c1 in PIECES:
                    pe.matmul(o_[0:rows(t), c0:c1], st[:, K1, cols(t)], st[:, Q1, c0:c1], start=True, stop=False)
                    last = pe.matmul(o_[0:rows(t), c0:c1], st[:, K2, cols(t)], st[:, Q2, c0:c1], start=False, stop=True)
                end(last, ("ST", i))

            def values(i, between):
                h, t = divmod(i, T)
                r = rows(t)
                if t == 0:
                    begin(("AV", h))
                if i == 0:
                    pe.wait_ge(s_vl, T)
                    pe.wait_ge(s_vpad, 1)
                    pe.wait_ge(s_ppad, 2)
                o_ = slot["W1"]
                pe.wait_ge(s_phi, i + 1)
                for n, (a, b) in enumerate(((val_h, pr_h), (val_l, pr_h), (val_h, pr_l))):
                    if n == 2:
                        pe.wait_ge(s_plo, i + 1)
                    for c0, c1 in PIECES:
                        last = pe.matmul(o_[0:DH if a is val_l else DH + ZR, c0:c1], a[0:r, t, h, :],
                                         b[0:r, i % 2, c0:c1], start=t == 0 and n == 0, stop=t == T - 1 and n == 2)
                    if n == 2:
                        if t == T - 1:
                            end(last, ("AV", h))
                        else:
                            last.then_inc(s_av, 1)
                    for key in between[2 * n:2 * n + 2] if n < 2 else between[4:]:
                        narrow(key)

            wh, wl = weights(W_V)
            for t in range(T):
                end(rows_product(begin(("v", t))[0:rows(t), 0:D], act_h, act_l, cols(t), wh, wl), ("v", t))
                for a in (2 * t, 2 * t + 1):
                    for c in range(len(PIECES)):
                        if a < T:
                            narrow(("max", 0, a, c))
                if t == T // 2:
                    narrow(("turn", 0))
            for i in range(UNITS + 1):
                keys = narrow_jobs(i) if i < UNITS else []
                if i < UNITS:
                    shifted_scores(i)
                    for key in keys[0:2] if i else keys:
                        narrow(key)
                if i:
                    values(i - 1, keys[2:])
            def project(o_, t, ks):
                for k in ks:
                    for i, (a, w) in enumerate(((act_h, wh), (act_h, wl), (act_l, wh))):
                        last = pe.matmul(o_[0:rows(t), :], a[:, k, cols(t)], w[:, k, :], start=k == 0 and i == 0,
                                         stop=k == KC - 1 and i == 2)
                return last

            wh, wl = weights(W_O)
            pe.wait_ge(s_clo, NH - 2)
            early = list(range(6))

            def project_early():
                t = early.pop(0)
                if t % 3 == 0:
                    begin(("sa3", t // 3))
                project(slot["W%d" % (t // 3)][:, t % 3 * D:(t % 3 + 1) * D], t, range(KC - 1))

            for t in range(1, 5):
                for key in chores(NH - 1, t):
                    narrow(key)
                project_early()
            project_early()
            project_early()
            pe.wait_ge(s_clo, NH)
            for t in range(6):
                last = project(slot["W%d" % (t // 3)][:, t % 3 * D:(t % 3 + 1) * D], t, [KC - 1])
                if t % 3 == 2:
                    end(last, ("sa3", t // 3))
            for t in range(6, T):
                end(project(begin(("sa", t)), t, range(KC)), ("sa", t))

            transposes("tkT", tok, lambda t: pe.wait_ge(s_tok, t + 1))
            pe.wait_ge(s_route, 2)
            end(feature_product(begin("logits"), wg_h, wg_l, slice(0, P), act_h, act_l,
                                ready=lambda k: pe.wait_ge(s_tlo, k + 1)), "logits")
            o_ = begin("lgrows")
            wait_drained(pe, "logits")
            for t in range(T):
                last = pe.transpose(o_[0:rows(t), t * NE:(t + 1) * NE], lg_t[:, cols(t)], ident[0:NE, 0:NE])
            end(last, "lgrows")

            def up(n):
                g, j = divmod(n, KC)
                q, half = divmod(g, 2)
                wh, wl = weights(UP + 2 * q)
                for p in range(2):
                    r = 2 * n + p
                    if r >= 3:
                        pe.wait_ge(s_gelu, r - 2)
                    c0 = half * HT + p * PW
                    last = feature_product(hbank[r % 3], wh, wl, chunk(j), act_h[:, :, c0:c0 + PW],
                                           act_l[:, :, c0:c0 + PW], pieces=[(0, PW)])
                    last.then_inc(s_hfill[r % 3], 1)

            def down(n):
                g, j = divmod(n, KC)
                q, half = divmod(g, 2)
                wh, wl = weights(DOWN + 2 * q)
                pe.wait_ge(s_hl, 2 * n + 2)
                for i in range(T // 2):
                    t = half * (T // 2) + i
                    o_ = ybank[i][0:rows(t), :]
                    sl = slice(i * P, i * P + rows(t))
                    if j == 0 and g:
                        pe.wait_ge(s_yd, T // 2 * (g - 1) + i + 1)
                    if n in (0, KC):
                        pe.matmul(o_, oh_t[:, cols(t)], b2_h[:, :], start=True, stop=False)
                        pe.matmul(o_, oh_t[:, cols(t)], b2_l[:, :], start=False, stop=False)
                    for k, (a, w) in enumerate(((hid_h, wh), (hid_h, wl), (hid_l, wh))):
                        last = pe.matmul(o_, a[:, n % 2, sl], w[:, j, :], start=g >= 2 and j == 0 and k == 0,
                                         stop=j == KC - 1 and k == 2)
                    if n == STEPS - 1:
                        last.then_inc(s_tile, 1)
                if n < STEPS - 1:
                    last.then_inc(s_hused, 1)

            hbank = [slot["N0"], slot["N1"], slot["W1"][:, 1024:1536]]
            ybank = [slot["W0"][:, 0:512], slot["W0"][:, 512:1024], slot["W0"][:, 1024:1536],
                     slot["W1"][:, 0:512], slot["W1"][:, 512:1024]]
            for w in ("N0", "N1"):
                pe.wait_ge(drained[w], used[w])
            up(0)
            o_ = begin("ohT")
            pe.wait_ge(s_route, 4 + NE + 1)
            for t in range(T):
                last = pe.transpose(o_[0:NE, cols(t)], oh[0:rows(t), t, :], ident[0:rows(t), 0:rows(t)])
            end(last, "ohT")
            wait_drained(pe, "ohT")
            for e in range(NE):
                o_ = begin(("mask", e))
                for c0, c1 in PIECES:
                    last = pe.matmul(o_[:, c0:c1], sel[:, e, :], oh_t16[:, c0:c1], start=True, stop=True)
                end(last, ("mask", e))
            for w in ("W0", "W1"):
                pe.wait_ge(drained[w], used[w])

            for n in range(STEPS + 1):
                if 0 < n < STEPS:
                    up(n)
                if n:
                    down(n - 1)

        @block.scalar
        def _(act):
            ln_no = [0]

            def sqrt_of_variance(t0=0, t1=T):
                ln_no[0] += 1
                act.wait_ge(s_var, ln_no[0])
                act.activation(rs[:, t0:t1], ve[:, t0:t1], ACT.Sqrt).then_inc(s_sqrt, 1)

            def hi(key, out_ap, in_of, bias=None):
                o_ = wait_filled(act, key)
                if bias is None:
                    act.activation(out_ap, in_of(o_), ACT.Copy).then_inc(s_hi, 1)
                else:
                    act.activation(out_ap, in_of(o_), ACT.Identity, bias=bias).then_inc(s_hi, 1)

            def sums_out(h):
                o_ = wait_filled(act, ("AV", h))
                act.activation(sums[(h + 2) % 3][0:DH + ZR, 0:N], o_[0:DH + ZR, 0:N], ACT.Copy).then_inc(drained["W1"], 1)

            def normalise(out_of, tiles, n):
                act.wait_ge(s_shift_u, n)
                for t in tiles:
                    r = rows(t)
                    act.activation(out_of(t), acc[0:r, t, :], ACT.Identity, bias=shift_u[0:r, t:t + 1],
                                   scale=rs[0:r, t:t + 1]).then_inc(s_rows_a, 1)

            def context_hi(h):
                p0 = h % 2 * DH
                act.wait_ge(s_ctx, h + 1)
                act.activation(act_h[p0:p0 + DH, h // 2, 0:N], context_f[p0:p0 + DH, h // 2, 0:N], ACT.Copy) \
                   .then_inc(s_chi, 1)

            sqrt_of_variance()
            normalise(lambda t: rows_b[0:rows(t), t, :], range(A1), 1)
            for k in range(KC):
                hi(("xT", k), act_h[:, k, 0:N], lambda o_: o_[:, 0:N])
            for t in range(T):
                hi(("y", t), y_h[0:rows(t), t, :], lambda o_: o_[0:rows(t), :])
            for t in range(T):
                o_ = wait_filled(act, ("hist", t))
                if t:
                    act.wait_ge(s_deg, t)
                    wait_filled(act, ("AT", t - 1))
                act.activation(counts[:, :], o_[:, 0:NP + 2], ACT.Copy).then_inc(drained["W0"], 1)
                if t:
                    wait_filled(act, ("agg", t - 1))
                hi(("AT", t), adj_h[:, :], lambda o_: o_[:, 0:NP])
            act.wait_ge(s_rowc, 96)
            act.wait_ge(s_var, 2)
            act.activation(bn_work[:, 0, :], row_c[:, 4, :], ACT.Sqrt).then_inc(s_sqrt, 1)
            ln_no[0] += 1
            for m in range(KC):
                hi(("foldM", m), fold_h[:, m, :], lambda o_: o_[:, :])
            act.wait_ge(s_const, 128)
            wait_drained(act, "bt")
            wait_filled(act, ("agg", T - 1))
            for m in range(KC):
                hi(("tT", m), big[:, m, :], lambda o_: o_[:, 0:NP], bias=bt[:, m:m + 1])
            for t in range(T):
                act.wait_ge(s_max, t + 1)
                s, _n = jobs[("score", t)]
                if t >= 2:
                    act.wait_ge(s_pfree, t - 1)
                act.activation(prob[0:rows(t), t % 2, 0:N], slot[s][0:rows(t), 0:N], ACT.Exp,
                               bias=nmax[0:rows(t), t:t + 1], accum_out=z_mix[0:rows(t), t:t + 1]) \
                   .then_inc(s_exp, 1)
            for m in range(KC):
                act.wait_ge(s_gain, m + 1)
                act.activation(fold_h[:, m, :], scaled[:, m, :], ACT.Copy).then_inc(s_hi, 1)
            sqrt_of_variance(0, A2)
            normalise(lambda t: rows_b[0:rows(t), t, :], range(A2 // 2), 2)
            sqrt_of_variance(A2, T)
            normalise(lambda t: rows_b[0:rows(t), t, :], range(A2 // 2, A2), 2)
            for k in range(KC):
                hi(("uT", k), act_h[:, k, 0:N], lambda o_: o_[:, 0:N])
            for i, (which, k) in enumerate(QK):
                c = cols_c[:, 2 * KC + which * KC + k:2 * KC + which * KC + k + 1]
                if i >= 4:
                    act.wait_ge(s_store[i % 4], 64)
                if i == 0:
                    act.wait_ge(s_bq8, 1)
                hi(("qk", i), big[:, i % KC, :], lambda o_: o_[:, 0:NP], bias=c)
            for t in range(T):
                r = rows(t)
                wait_drained(act, ("v", t))
                if t == 0:
                    wait_filled(act, ("o", T - 1))
                act.activation(val_h[0:r, t, :, 0:DH], val_f[0:r, t, :, :], ACT.Copy) \
                   .then_inc(s_vh, 1)
            for i in range(UNITS):
                h, t = divmod(i, T)
                r = rows(t)
                o_ = wait_filled(act, ("ST", i))
                if i >= 2:
                    if (i - 2) % T == T - 1:
                        wait_filled(act, ("AV", (i - 2) // T))
                    else:
                        act.wait_ge(s_av, i - 1 - (i - 1) // T)
                act.activation(pr[0:r, i % 2, 0:N], o_[0:r, 0:N], ACT.Exp).then_inc(drained["W0"], 1)
                wait_drained(act, ("ST", i))
                act.activation(pr_h[0:r, i % 2, 0:N], pr[0:r, i % 2, 0:N], ACT.Copy).then_inc(s_phi, 1)
                if t == 0 and h:
                    sums_out(h - 1)
                if t == 5 and h:
                    context_hi(h - 1)
            sums_out(NH - 1)
            act.wait_ge(s_x1, 16 * T)

            def u_of(t):
                if t >= UB:
                    act.wait_ge(s_summed, t - UB + 1)
                r = rows(t)
                act.activation(u_rows[0:r, t % UB, :], acc[0:r, t, :], ACT.Identity, bias=shift_u[0:r, t:t + 1],
                               scale=rs_u[0:r, t:t + 1]).then_inc(s_u, 1)

            for t in range(UB):
                u_of(t)
            context_hi(NH - 1)
            for t in range(UB, 8):
                u_of(t)
            sqrt_of_variance(0, 4)
            for t in range(8, T):
                u_of(t)
            sqrt_of_variance(4, 8)
            sqrt_of_variance(8, T)
            for k in range(KC):
                o_ = wait_filled(act, ("tkT", k))
                if k >= 2:
                    act.wait_ge(s_tlo, k - 1)
                act.activation(tmp[:, k % 2, 0:N], o_[:, 0:N], ACT.Identity, bias=c_beta1[:, k:k + 1],
                               scale=c_g1[:, k:k + 1]).then_inc(drained[jobs[("tkT", k)][0]], 1)
                wait_drained(act, ("tkT", k))
                act.activation(act_h[:, k, 0:N], tmp[:, k % 2, 0:N], ACT.Copy).then_inc(s_scaled_t, 1)
            hbank = [slot["N0"], slot["N1"], slot["W1"][:, 1024:1536]]
            for r in range(2 * STEPS + 1):
                if r < 2 * STEPS:
                    n = r // 2
                    g, j = divmod(n, KC)
                    ft = g // 2 * KC + j
                    act.wait_ge(s_hfill[r % 3], r // 3 + 1)
                    if r >= 2:
                        act.wait_ge(s_hm, r - 1)
                    act.activation(gel[:, 0, (r % 2) * PW:(r % 2 + 1) * PW], hbank[r % 3][:, 0:PW], ACT.Gelu,
                                   bias=c_b1[:, ft:ft + 1]).then_inc(s_gelu, 1)
                if r == 1:
                    for e in range(0, NE, 2):
                        o_ = wait_filled(act, ("mask", e))
                        act.activation(mask[:, e, :], o_[:, 0:NP], ACT.Copy).then_inc(drained[jobs[("mask", e)][0]], 1)
                if r:
                    q_ = r - 1
                    act.wait_ge(s_hm, q_ + 1)
                    if q_ >= 4:
                        act.wait_ge(s_hused, q_ // 2 - 1)
                    act.activation(hid_h[:, (q_ // 2) % 2, (q_ % 2) * PW:(q_ % 2 + 1) * PW],
                                   gel[:, 1, (q_ % 2) * PW:(q_ % 2 + 1) * PW], ACT.Copy).then_inc(s_hh, 1)
                if r == R_LN + 2:
                    sqrt_of_variance(0, T // 2)
            sqrt_of_variance(T // 2, T)

        @block.vector
        def _(dve):
            chain, his, sq = [0], [0], [0]

            def step(ins):
                ins.then_inc(s_step, 1)
                chain[0] += 1
                dve.wait_ge(s_step, chain[0])

            def lo(key, out_ap, in_of, hi_ap, bias=None):
                o_ = slot[jobs[key][0]]
                his[0] += 1
                dve.wait_ge(s_hi, his[0])
                if bias is None:
                    ins = dve.tensor_tensor(out_ap, in_of(o_), hi_ap.bitcast(F32), ALU.subtract)
                else:
                    ins = dve.scalar_tensor_tensor(out_ap, in_of(o_), bias, hi_ap.bitcast(F32), ALU.add,
                                                   ALU.subtract)
                ins.then_inc(drained[jobs[key][0]], 1)

            def inverse_root(var, root, out_ap, work):
                step(dve.reciprocal(out_ap, root))
                step(dve.tensor_tensor(work, out_ap, out_ap, ALU.mult))
                step(dve.tensor_tensor(work, work, var, ALU.mult))
                step(dve.tensor_scalar(work, work, -0.5, 1.5, ALU.mult, ALU.add))
                step(dve.tensor_tensor(out_ap, out_ap, work, ALU.mult))

            def moments(t, row_ap):
                step(dve.bn_stats(st6[0:rows(t), 0, :], row_ap))
                step(dve.bn_aggr(mv[0:rows(t), t, :], st6[0:rows(t), 0, :]))

            def variances(t0=0, t1=T):
                dve.tensor_scalar(ve[:, t0:t1], mv[:, t0:t1, 1], LN_EPS, None, ALU.add).then_inc(s_var, 1)
                sq[0] += 1

            def finish_moments(t0=0, t1=T, begun=False):
                if not begun:
                    variances(t0, t1)
                dve.wait_ge(s_var, sq[0])
                dve.wait_ge(s_sqrt, sq[0])
                inverse_root(ve[:, t0:t1], rs[:, t0:t1], rs[:, t0:t1], nr[:, t0:t1])

            def shifts(t0, t1):
                dve.scalar_tensor_tensor(shift_u[:, t0:t1], mv[:, t0:t1, 0], -1.0, rs[:, t0:t1], ALU.mult, ALU.mult) \
                   .then_inc(s_shift_u, 1)
                dve.wait_ge(s_shift_u, 1 if t1 - t0 == T else 2 if t0 == 0 else 3)

            def normalise(out_ap, in_ap, t):
                r = rows(t)
                return dve.tensor_scalar(out_ap, in_ap, mv[0:r, t, 0:1], rs[0:r, t:t + 1], ALU.subtract, ALU.mult)

            def scaled_norm(a, t, gain, offset):
                r = rows(t)
                step(dve.scalar_tensor_tensor(a[0:r, t, :], a[0:r, t, :], mv[0:r, t, 0:1], gain, ALU.subtract, ALU.mult))
                return dve.scalar_tensor_tensor(a[0:r, t, :], a[0:r, t, :], rs[0:r, t:t + 1], offset, ALU.mult, ALU.add)

            def token_norm(t):
                normalise(tok[0:rows(t), t, :], tok[0:rows(t), t, :], t).then_inc(s_tok, 1)

            def token_affine(t):
                r = rows(t)
                step(dve.tensor_tensor(tok[0:r, t, :], tok[0:r, t, :], row_c[0:r, 2, :], ALU.mult))
                step(dve.tensor_tensor(tok[0:r, t, :], tok[0:r, t, :], row_c[0:r, 3, :], ALU.add))

            dve.wait_ge(s_setup, 4)
            for t in range(T + 1):
                if t < T:
                    dve.wait_ge(s_x[t], 16)
                    if t >= 2:
                        dve.wait_ge(s_aggr, t - 1)
                    dve.bn_stats(st6[0:rows(t), t % 2, :], acc[0:rows(t), t, :]).then_inc(s_stats, 1)
                if t:
                    dve.wait_ge(s_stats, t)
                    dve.bn_aggr(mv[0:rows(t - 1), t - 1, :], st6[0:rows(t - 1), (t - 1) % 2, :]).then_inc(s_aggr, 1)
            dve.wait_ge(s_aggr, T)
            dve.wait_ge(s_setup, 13)
            finish_moments()
            shifts(0, T)
            for t in range(A1, T):
                normalise(rows_b[0:rows(t), t, :], acc[0:rows(t), t, :], t).then_inc(s_rows, 1)
            step(dve.tensor_scalar(gain_u[:, :], rs[:, :], 1.0, None, ALU.add))
            dve.wait_ge(s_edge, 32)
            dve.tensor_copy(edge_f[:, :, :], edge_i[:, :, :]).then_inc(s_ef, 1)
            dve.wait_ge(s_ef, 1)
            step(dve.tensor_reduce(lohi[:, 0:2], edge_f[:, 2:4, :], AX.X, ALU.min))
            step(dve.tensor_reduce(lohi[:, 2:4], edge_f[:, 2:4, :], AX.X, ALU.max))
            for j in range(4):
                dve.tensor_scalar(diag[:, j, :], ident[0:CP, 0:CP], lohi[:, j:j + 1], None, ALU.mult).then_inc(s_dg, 1)
            for k in range(KC):
                lo(("xT", k), act_l[:, k, 0:N], lambda o_: o_[:, 0:N], act_h[:, k, 0:N])
            for t in range(T):
                r = rows(t)
                lo(("y", t), y_l[0:r, t, :], lambda o_: o_[0:r, :], y_h[0:r, t, :])
                if t == 3:
                    o_ = wait_filled(dve, "edges")
                    step(dve.memset(edge_t[:, :, CH:], -1.0))
                    dve.tensor_copy(edge_t[:, :, 0:CH], o_[0:CE, 0:2 * CH].rearrange("p (a c) -> p a c", a=2)) \
                       .then_inc(drained["W0"], 1)
                if t == 5:
                    o_ = wait_filled(dve, "ranges")
                    step(dve.tensor_scalar(cover2[:, :], o_[0:T, 0:CH], tile_lo[:, 1:2], None, ALU.is_le))
                    step(dve.scalar_tensor_tensor(cover[:, :], o_[0:T, CH:2 * CH], tile_lo[:, 0:1], cover2[:, :], ALU.is_ge,
                                                  ALU.mult))
                    step(dve.scalar_tensor_tensor(cover2[:, :], cover[:, :], -BIG, chunk_no[:, :], ALU.mult, ALU.add))
                    step(dve.tensor_reduce(span[:, 0:1], cover2[:, :], AX.X, ALU.min))
                    step(dve.tensor_scalar(span[:, 0:1], span[:, 0:1], BIG, CH - 1.0, ALU.add, ALU.min))
                    step(dve.scalar_tensor_tensor(cover2[:, :], chunk_no[:, :], 1.0, cover[:, :], ALU.add, ALU.mult))
                    step(dve.tensor_reduce(span[:, 1:2], cover2[:, :], AX.X, ALU.max))
                    step(dve.tensor_scalar(span[:, 3:4], span[:, 0:1], 1.0, None, ALU.add))
                    dve.tensor_tensor(span[:, 1:2], span[:, 1:2], span[:, 3:4], ALU.max).then_inc(drained["W1"], 1)
                    wait_drained(dve, "ranges")
                    step(dve.scalar_tensor_tensor(span[:, 2:3], span[:, 1:2], -float(FEW), span[:, 0:1], ALU.add,
                                                  ALU.is_gt))
                    dve.tensor_copy(span_i[:, :], span[:, 0:3]).then_inc(s_span, 1)

            def finish_tile(t):
                r = rows(t)
                own = work1[0:r, :]
                o_ = wait_filled(dve, ("self", t))
                dve.tensor_tensor(own, o_[0:r, :], row_c[0:r, 0, :], ALU.add).then_inc(drained["N0"], 1)
                wait_drained(dve, ("self", t))
                o_ = wait_filled(dve, ("agg", t))
                dve.scalar_tensor_tensor(own, o_[0:r, :], rdeg[0:r, t:t + 1], own, ALU.mult, ALU.add) \
                   .then_inc(drained["N1"], 1)
                wait_drained(dve, ("agg", t))

            dve.wait_ge(s_rowc, 96)
            dve.wait_ge(s_span, 1)
            ticket = dve.alloc_register("dve_steps")
            dve.reg_mov(ticket, 0)
            for t in range(T + 2):
                if t < T:
                    c_first = dve.value_load(span_i[t:t + 1, 0:1], min_val=0, max_val=CH - 1)
                    c_end = dve.value_load(span_i[t:t + 1, 1:2], min_val=1, max_val=CH)
                    with dve.Fori(c_first, c_end, HB) as c:
                        dve.reg_add(ticket, ticket, 1)
                        for b in range(HB):
                            dve.wait_ge(s_hotfree[b], dve.snap(ticket))
                            dve.tensor_scalar(hot_src[0:CE, b, 0:NP], iota16[0:CE, :],
                                              edge_t[:, 0, bass.ds(c + b, 1)], None, ALU.is_equal)
                            dve.tensor_scalar(hot_dst[0:CE, b, :], iota16[0:CE, t * P:(t + 1) * P],
                                              edge_t[:, 1, bass.ds(c + b, 1)], None, ALU.is_equal) \
                               .then_inc(s_hot[b], 1)
                if t >= 2:
                    finish_tile(t - 2)
                if 1 <= t <= T:
                    if t >= 2:
                        wait_filled(dve, ("agg", t - 2))
                    lo(("AT", t - 1), adj_l[:, :], lambda o_: o_[:, 0:NP], adj_h[:, :])
                if t < T:
                    r = rows(t)
                    step(dve.tensor_scalar(acc[0:r, t, :], acc[0:r, t, :], gain_u[0:r, t:t + 1], shift_u[0:r, t:t + 1],
                                           ALU.mult, ALU.add))
                if t >= 2:
                    r = rows(t - 2)
                    step(dve.scalar_tensor_tensor(acc[0:r, t - 2, :], work1[0:r, :], 0.0, acc[0:r, t - 2, :],
                                                  ALU.max, ALU.add))
                if t < T:
                    wait_drained(dve, ("hist", t))
                    dve.tensor_scalar(nr[:, 0:1], counts[:, NP:NP + 1], 1.0, None, ALU.max).then_inc(s_deg, 1)
                    dve.wait_ge(s_deg, t + 1)
                    step(dve.reciprocal(rdeg[:, t:t + 1], nr[:, 0:1]))

            dve.tensor_scalar(row_c[:, 4, :], row_c[:, 4, :], LN_EPS, None, ALU.add).then_inc(s_var, 1)
            sq[0] += 1
            dve.wait_ge(s_const, 128)
            dve.tensor_copy(bq_pair[:, :, 0], c_mbq).then_inc(s_bqp, 1)
            dve.wait_ge(s_bqp, 1)
            dve.tensor_tensor(bq_pair[:, :, 1], c_mbq, bq_pair[:, :, 0].bitcast(F32), ALU.subtract).then_inc(s_bqp, 1)
            dve.tensor_scalar(c_fbq, c_fbq, DH ** -0.5, None, ALU.mult).then_inc(s_bq8, 1)
            for m in range(KC):
                lo(("foldM", m), fold_l[:, m, :], lambda o_: o_[:, :], fold_h[:, m, :])
            o_ = wait_filled(dve, "bt")
            dve.tensor_reduce(bt[:, :], o_[:, 0:2 * KC].rearrange("p (m b) -> p m b", b=2), AX.X, ALU.add) \
               .then_inc(drained["N0"], 1)
            for m in range(KC):
                if m == 0:
                    wait_drained(dve, "bt")
                lo(("tT", m), big[:, KC + m, :], lambda o_: o_[:, 0:NP], big[:, m, :], bias=bt[:, m:m + 1])

            def norm_root():
                dve.wait_ge(s_var, sq[0])
                dve.wait_ge(s_sqrt, sq[0])
                inverse_root(row_c[:, 4, :], bn_work[:, 0, :], bn_work[:, 0, :], bn_work[:, 1, :])

            def norm_constants():
                step(dve.tensor_tensor(row_c[:, 1, :], row_c[:, 1, :], bn_work[:, 0, :], ALU.mult))
                step(dve.tensor_tensor(row_c[:, 5, :], row_c[:, 5, :], row_c[:, 3, :], ALU.subtract))
                step(dve.tensor_tensor(row_c[:, 5, :], row_c[:, 5, :], row_c[:, 1, :], ALU.mult))
                step(dve.tensor_tensor(row_c[:, 5, :], row_c[:, 5, :], row_c[:, 2, :], ALU.add))

            def value_bias():
                for k in range(KC):
                    dve.tensor_scalar(bv_rep_h[:, k, :], ones[:, :], c_mbv[:, k:k + 1], None, ALU.mult).then_inc(s_bvr, 1)
                    dve.wait_ge(s_bvr, 2 * k + 1)
                    dve.scalar_tensor_tensor(bv_rep_l[:, k, :], ones[:, :], c_mbv[:, k:k + 1],
                                             bv_rep_h[:, k, :].bitcast(F32), ALU.mult, ALU.subtract).then_inc(s_bvr, 1)

            def column_sums(t):
                r = rows(t)
                dve.wait_ge(s_exp, t + 1)
                step(dve.reciprocal(zt[0:r, t:t + 1], z_mix[0:r, t:t + 1]))
                if t == 0:
                    ins = dve.tensor_scalar(col_acc[0:r, 0:N], prob[0:r, t % 2, 0:N], zt[0:r, t:t + 1], None, ALU.mult)
                else:
                    ins = dve.scalar_tensor_tensor(col_acc[0:r, 0:N], prob[0:r, t % 2, 0:N], zt[0:r, t:t + 1],
                                                   col_acc[0:r, 0:N], ALU.mult, ALU.add)
                ins.then_inc(s_pfree, 1)
                dve.wait_ge(s_pfree, t + 1)

            for t in range(T):
                r = rows(t)
                o_ = wait_filled(dve, ("score", t))
                dve.tensor_reduce(nmax[0:r, t:t + 1], o_[0:r, 0:N], AX.X, ALU.max, negate=True).then_inc(s_max, 1)
                dve.wait_ge(s_exp, t + 1)
                dve.wait_ge(s_max, t + 1)
                dve.engine_nop().then_inc(drained[jobs[("score", t)][0]], 1)
                column_sums(t)
                if t == 1:
                    norm_root()
                if t == 3:
                    norm_constants()
                if t == 4:
                    value_bias()
            for m in range(KC):
                o_ = wait_filled(dve, ("foldN", m))
                dve.tensor_tensor(scaled[:, m, :], o_[:, :], row_c[:, 1, :], ALU.mult) \
                   .then_inc(drained[jobs[("foldN", m)][0]], 1)
                wait_drained(dve, ("foldN", m))
                dve.engine_nop().then_inc(s_gain, 1)
                his[0] += 1
                dve.wait_ge(s_hi, his[0])
                dve.tensor_tensor(fold_l[:, m, :], scaled[:, m, :], fold_h[:, m, :].bitcast(F32), ALU.subtract) \
                   .then_inc(s_fold, 1)
            o_ = wait_filled(dve, "bvo")
            dve.tensor_tensor(row_c[:, 3, :], o_[:, :], row_c[:, 1, :], ALU.mult).then_inc(drained["N0"], 1)
            wait_drained(dve, "bvo")
            o_ = wait_filled(dve, "colsum")
            last_r = rows(T - 1)
            step(dve.tensor_scalar(nr[:, 0:T - 1], o_[:, 0:T - 1], 1e-9, None, ALU.add))
            step(dve.tensor_scalar(nr[0:last_r, T - 1:T], o_[0:last_r, T - 1:T], 1e-9, None, ALU.add))
            step(dve.reciprocal(zt[:, 0:T - 1], nr[:, 0:T - 1]))
            step(dve.reciprocal(zt[0:last_r, T - 1:T], nr[0:last_r, T - 1:T]))
            step(dve.tensor_tensor(cfac[:, 0:T - 1], o_[:, 0:T - 1], zt[:, 0:T - 1], ALU.mult))
            dve.tensor_tensor(cfac[0:last_r, T - 1:T], o_[0:last_r, T - 1:T], zt[0:last_r, T - 1:T], ALU.mult) \
               .then_inc(drained["N1"], 1)
            wait_drained(dve, "colsum")
            for t in range(T):
                r = rows(t)
                o_ = wait_filled(dve, ("o", t))
                own = work1[0:r, :]
                dve.scalar_tensor_tensor(own, o_[0:r, :], cfac[0:r, t:t + 1], row_c[0:r, 5, :], ALU.mult, ALU.add) \
                   .then_inc(drained[jobs[("o", t)][0]], 1)
                wait_drained(dve, ("o", t))
                dve.scalar_tensor_tensor(acc[0:r, t, :], own, 0.0, acc[0:r, t, :], ALU.max, ALU.add) \
                   .then_inc(s_mixdone, 1)
                dve.wait_ge(s_mixdone, t + 1)
                moments(t, acc[0:r, t, :])
                if t == A2 - 1:
                    variances(0, A2)
                if t == A2:
                    wait_filled(dve, ("agg", T - 1))
                    finish_moments(0, A2, begun=True)
                    shifts(0, A2)
            finish_moments(A2, T)
            shifts(A2, T)
            step(dve.tensor_copy(rs_u[:, :], rs[:, :]))
            for t in range(A2, T):
                normalise(rows_b[0:rows(t), t, :], acc[0:rows(t), t, :], t).then_inc(s_rows, 1)
            for k in range(KC):
                lo(("uT", k), act_l[:, k, 0:N], lambda o_: o_[:, 0:N], act_h[:, k, 0:N])
            dve.wait_ge(s_ffnrow, 96)
            dve.memset(val_h[:, :, :, DH:DH + ZR].bitcast(F32), 1.0).then_inc(s_vpad, 1)

            def value_lo(t):
                dve.wait_ge(s_vh, t + 1)
                dve.tensor_tensor(val_l[0:rows(t), t, :, :], val_f[0:rows(t), t, :, :], val_h[0:rows(t), t, :, 0:DH].bitcast(F32), ALU.subtract) \
                   .then_inc(s_vl, 1)

            for i, (which, k) in enumerate(QK):
                if i >= 4:
                    dve.wait_ge(s_store[i % 4], 64)
                c = 2 * KC + which * KC + k
                lo(("qk", i), big[:, KC + i % KC, :], lambda o_: o_[:, 0:NP], big[:, i % KC, :], bias=cols_c[:, c:c + 1])
            step(dve.memset(piece_max[:, :, :], 0.0))
            step(dve.memset(neg_max[:, :], 0.0))
            step(dve.memset(inverse[:, :], 0.0))
            step(dve.tensor_tensor(tile_mask[:, :], ident[:, DH:DH + T], ident[:, 96:96 + T], ALU.add))

            def maxima(h, t):
                r = rows(t)
                for c, (c0, c1) in enumerate(PIECES):
                    o_ = wait_filled(dve, ("max", h, t, c))
                    dve.tensor_reduce(piece_max[0:r, t, c:c + 1], o_[0:r, 0:min(c1, N) - c0], AX.X, ALU.max) \
                       .then_inc(drained[jobs[("max", h, t, c)][0]], 1)
                if t == T - 1:
                    for c in range(2):
                        wait_drained(dve, ("max", h, t, 1 + c))
                    if h:
                        dve.wait_ge(s_shift, h)
                    step(dve.tensor_reduce(neg_max[:, DH:DH + T], piece_max[:, :, :], AX.X, ALU.max, negate=True))
                    dve.tensor_reduce(neg_max[:, 96:96 + T], piece_max[:, :, :], AX.X, ALU.max, negate=True) \
                       .then_inc(s_amax, 1)

            def rows_to_stack(h, key):
                o_ = wait_filled(dve, key)
                parts = row_parts[DH:P, :]
                step(dve.tensor_copy(parts.bitcast(F32R), o_[DH:P, 0:P]))
                dve.tensor_tensor(row_parts[96:P, :], o_[96:P, 0:P], row_parts[96:P, :], ALU.subtract) \
                   .then_inc(drained[jobs[key][0]], 1)
                wait_drained(dve, key)
                return dve.tensor_tensor(stack(h)[DH:P, Q2, :].rearrange("p (t q) -> p t q", t=T),
                                         parts.unsqueeze(1).to_broadcast([DH, T, P]),
                                         tile_mask[DH:P, :].unsqueeze(2).to_broadcast([DH, T, P]), ALU.mult)

            def shift(h):
                rows_to_stack(h, ("turn", h)).then_inc(s_shift, 1)

            def inverses(h):
                o_ = wait_filled(dve, ("divisors", h))
                for c in (DH, 96):
                    step(dve.reciprocal(inverse[:, c:c + T - 1], o_[:, 0:(T - 1) * ZR:ZR]))
                    last = dve.reciprocal(inverse[0:last_r, c + T - 1:c + T], o_[0:last_r, (T - 1) * ZR:(T - 1) * ZR + 1])
                    if c == DH:
                        step(last)
                last.then_inc(drained[jobs[("divisors", h)][0]], 1)

            def spread(h):
                rows_to_stack(h, ("inverse", h)).then_inc(s_spread, 1)

            def context(h):
                p0 = h % 2 * DH
                for c, (c0, c1) in enumerate(PIECES):
                    c1 = min(c1, N)
                    o_ = wait_filled(dve, ("spread", h, c))
                    dve.tensor_tensor(context_f[p0:p0 + DH, h // 2, c0:c1], sums[(h + 2) % 3][0:DH, c0:c1],
                                      o_[0:DH, 0:c1 - c0], ALU.mult).then_inc(drained[jobs[("spread", h, c)][0]], 1)
                for c in (1, 2):
                    wait_drained(dve, ("spread", h, c))
                dve.engine_nop().then_inc(s_ctx, 1)

            def context_lo(h):
                p0 = h % 2 * DH
                dve.wait_ge(s_chi, h + 1)
                dve.tensor_tensor(act_l[p0:p0 + DH, h // 2, 0:N], context_f[p0:p0 + DH, h // 2, 0:N],
                                  act_h[p0:p0 + DH, h // 2, 0:N].bitcast(F32), ALU.subtract) \
                   .then_inc(s_clo, 1)

            for t in range(T):
                r = rows(t)
                for a in (2 * t, 2 * t + 1):
                    if a < T:
                        maxima(0, a)
                if t == T // 2 + 1:
                    shift(0)
                o_ = wait_filled(dve, ("v", t))
                dve.tensor_tensor(val_f[0:r, t, :, :], o_[0:r, 0:D].rearrange("p (h d) -> p h d", h=NH),
                                  row_c[0:r, 0, :].rearrange("p (h d) -> p h d", h=NH), ALU.add) \
                   .then_inc(drained[jobs[("v", t)][0]], 1)
                if t:
                    value_lo(t - 1)
            value_lo(T - 1)
            dve.memset(pr_l[:, :, N:NP].bitcast(F32), 0.0).then_inc(s_ppad, 1)
            dve.memset(pr_h[:, :, N:NP].bitcast(F32), 0.0).then_inc(s_ppad, 1)
            for i in range(UNITS):
                h, t = divmod(i, T)
                r = rows(t)
                for s, stage_of in ((2, inverses), (3, spread), (4, context)):
                    if t == s and h:
                        stage_of(h - 1)
                for a, b in max_tiles(i):
                    maxima(a, b)
                dve.wait_ge(s_phi, i + 1)
                dve.tensor_tensor(pr_l[0:r, i % 2, 0:N], pr[0:r, i % 2, 0:N], pr_h[0:r, i % 2, 0:N].bitcast(F32),
                                  ALU.subtract).then_inc(s_plo, 1)
                if t == T - 2 and h + 1 < NH:
                    shift(h + 1)
                if t == 6 and h:
                    context_lo(h - 1)
            wait_filled(dve, ("AV", NH - 1))
            dve.memset(wg_f[:, :, :], 0.0).then_inc(s_pads, 1)
            for stage_of in (inverses, spread, context, context_lo):
                stage_of(NH - 1)
            dve.wait_ge(s_wg, 16)
            dve.tensor_copy(wg_h[:, :, :], wg_f[:, :, :]).then_inc(s_route, 1)
            dve.wait_ge(s_route, 1)
            dve.tensor_tensor(wg_l[:, :, :], wg_f[:, :, :], wg_h[:, :, :].bitcast(F32), ALU.subtract).then_inc(s_route, 1)
            dve.wait_ge(s_b2, 16)
            dve.tensor_copy(b2_h[:, :], b2_f[:, :]).then_inc(s_route, 1)
            dve.wait_ge(s_route, 3)
            dve.tensor_tensor(b2_l[:, :], b2_f[:, :], b2_h[:, :].bitcast(F32), ALU.subtract).then_inc(s_route, 1)
            for e in range(NE):
                dve.tensor_scalar(sel[:, e, :], ones[0:NE, :], ident[0:NE, e:e + 1], None, ALU.mult).then_inc(s_route, 1)
            for t in range(T):
                r = rows(t)
                if t < 6:
                    o_ = wait_filled(dve, ("sa3", t // 3))[:, t % 3 * D:(t % 3 + 1) * D]
                else:
                    o_ = wait_filled(dve, ("sa", t))
                dve.wait_ge(s_ubo, t + 1)
                dve.tensor_tensor(tok[0:r, t, :], o_[0:r, :], u_rows[0:r, t % UB, :], ALU.add).then_inc(s_summed, 1)
                dve.wait_ge(s_summed, t + 1)
                if t in (2, 5) or t >= 6:
                    dve.engine_nop().then_inc(drained["W%d" % (t // 3) if t < 6 else "N%d" % (t % 2)], 1)
                moments(t, tok[0:r, t, :])
                for g in range(2):
                    if t == 4 * g + 3:
                        variances(4 * g, 4 * g + 4)
                    if t == 4 * g + 4:
                        finish_moments(4 * g, 4 * g + 4, begun=True)
                if t == T - 1:
                    variances(8, T)
                if t >= 4:
                    token_norm(t - 4)
            for t in range(T - 4, 8):
                token_norm(t)
            finish_moments(8, T, begun=True)
            for t in range(8, T):
                token_norm(t)
            for k in range(KC):
                dve.wait_ge(s_scaled_t, k + 1)
                dve.tensor_tensor(act_l[:, k, 0:N], tmp[:, k % 2, 0:N], act_h[:, k, 0:N].bitcast(F32), ALU.subtract) \
                   .then_inc(s_tlo, 1)
            dve.wait_ge(s_tlo, KC)
            for t in range(T // 2):
                token_affine(t)
            o_ = wait_filled(dve, "logits")
            dve.tensor_scalar(lg_t[:, :], o_[0:NE, 0:NP], c_bg, None, ALU.add).then_inc(drained["W0"], 1)
            step(dve.memset(lg[:, T - 1, :], 0.0))
            o_ = wait_filled(dve, "lgrows")
            step(dve.tensor_copy(lg[:, 0:T - 1, :], o_[:, 0:(T - 1) * NE].rearrange("p (t e) -> p t e", e=NE)))
            dve.tensor_copy(lg[0:last_r, T - 1, :], o_[0:last_r, (T - 1) * NE:T * NE]).then_inc(drained["W1"], 1)
            wait_drained(dve, "lgrows")
            step(dve.tensor_reduce(best[:, :], lg[:, :, :], AX.X, ALU.max))
            step(dve.tensor_tensor(cand[:, :, :], lg[:, :, :], best[:, :].unsqueeze(2).to_broadcast([P, T, NE]), ALU.is_equal))
            step(dve.scalar_tensor_tensor(cand[:, :, :], cand[:, :, :], -BIG,
                                          iota8[:, :].unsqueeze(1).to_broadcast([P, T, NE]), ALU.mult, ALU.add))
            step(dve.tensor_reduce(best[:, :], cand[:, :, :], AX.X, ALU.min))
            dve.tensor_tensor(oh[:, :, :], cand[:, :, :], best[:, :].unsqueeze(2).to_broadcast([P, T, NE]), ALU.is_equal) \
               .then_inc(s_route, 1)
            step(dve.memset(oh_t[:, N:NP].bitcast(F32), 0.0))
            step(dve.memset(oh_t16[:, N:NP], 0.0))
            o_ = wait_filled(dve, "ohT")
            dve.tensor_copy(oh_t[:, 0:N], o_[0:NE, 0:N]).then_inc(s_oh, 1)
            dve.wait_ge(s_oh, 1)
            dve.tensor_copy(oh_t16[:, 0:N], o_[0:NE, 0:N]).then_inc(drained["W1"], 1)
            for e in range(1, NE, 2):
                o_ = wait_filled(dve, ("mask", e))
                dve.tensor_copy(mask[:, e, :], o_[:, 0:NP]).then_inc(drained[jobs[("mask", e)][0]], 1)
            for s in ("W0", "W1"):
                dve.wait_ge(drained[s], used[s])

            def fold_in(i, half):
                t = half * (T // 2) + i
                r = rows(t)
                dve.tensor_tensor(tok[0:r, t, :], ybank[i][0:r, :], tok[0:r, t, :], ALU.add).then_inc(s_yd, 1)

            def finish_rows(t):
                r = rows(t)
                scaled_norm(tok, t, row_c[0:r, 4, :], acc[0:r, t, :]).then_inc(s_fin, 1)

            ybank = [slot["W0"][:, 0:512], slot["W0"][:, 512:1024], slot["W0"][:, 1024:1536],
                     slot["W1"][:, 0:512], slot["W1"][:, 512:1024]]
            for r in range(2 * STEPS + 1):
                if r < 2 * STEPS:
                    g, j = divmod(r // 2, KC)
                    q, half = divmod(g, 2)
                    e = 2 * q + j // 2
                    c0 = half * HT + (r % 2) * PW
                    dve.wait_ge(s_gelu, r + 1)
                    if r >= 2:
                        dve.wait_ge(s_hl, r - 1)
                    dve.tensor_tensor(gel[:, 1, (r % 2) * PW:(r % 2 + 1) * PW], gel[:, 0, (r % 2) * PW:(r % 2 + 1) * PW],
                                      mask[:, e, c0:c0 + PW], ALU.mult).then_inc(s_hm, 1)
                if r:
                    q_ = r - 1
                    sl = slice((q_ % 2) * PW, (q_ % 2 + 1) * PW)
                    dve.wait_ge(s_hh, q_ + 1)
                    dve.tensor_tensor(hid_l[:, (q_ // 2) % 2, sl], gel[:, 1, sl],
                                      hid_h[:, (q_ // 2) % 2, sl].bitcast(F32), ALU.subtract).then_inc(s_hl, 1)
                if r in range(1, 1 + 3 * (T // 2), 3):
                    token_affine(T // 2 + r // 3)
                if 20 <= r < 20 + T:
                    t = r - 20
                    step(dve.tensor_tensor(acc[0:rows(t), t, :], acc[0:rows(t), t, :], row_c[0:rows(t), 5, :], ALU.add))
                if r > 2 and r % (2 * KC) in (1, 2):
                    g = r // (2 * KC) - 1
                    dve.wait_ge(s_hused, KC * (g + 1))
                    for i in range(2) if r % 2 else range(2, T // 2):
                        fold_in(i, g % 2)
                    if g == GROUPS - 2:
                        dve.wait_ge(s_yd, T // 2 * g + (2 if r % 2 else T // 2))
                for t in {R_LN - 1: (0,), R_LN: (1, 2), R_LN + 1: (3, 4)}.get(r, ()):
                    moments(t, tok[0:rows(t), t, :])
                if r == R_LN + 1:
                    variances(0, T // 2)
                if r == R_LN + 2:
                    finish_moments(0, T // 2, begun=True)
                if R_LN + 2 <= r < R_LN + 2 + T // 2:
                    finish_rows(r - R_LN - 2)
            for i in range(T // 2):
                t = T // 2 + i
                dve.wait_ge(s_tile, i + 1)
                fold_in(i, 1)
                dve.wait_ge(s_yd, T // 2 * (GROUPS - 1) + i + 1)
                moments(t, tok[0:rows(t), t, :])
            finish_moments(T // 2, T)
            for t in range(T // 2, T):
                finish_rows(t)


_INS = ["x", "src", "dst", "w_all", "mix_bq", "mix_bv", "mix_rows", "ffn_bq", "ffn_bk", "ffn_g1", "ffn_beta1",
        "ffn_rows", "wg", "bg", "b1", "b2"]


def kernel(**inputs):
    import numpy as np
    import concourse.bacc as bacc
    from concourse.bass_utils import run_bass_kernel_spmd

    a = {k: np.asarray(v) for k, v in inputs.items()}

    def chunked(w):
        return np.ascontiguousarray(w.reshape(KC, P, -1).transpose(1, 0, 2))

    def column(b):
        return np.ascontiguousarray(b.reshape(-1, P).T)

    m, f = "L0_mix_", "L0_ffn_"
    units = [a["L0_gnn_W_neigh"].T, a["L0_gnn_W_self"].T, a[m + "Wq"].T, a[m + "Wk"].T, a[m + "Wv"].T,
             a[m + "Wo"], a[f + "Wq"], a[f + "Wk"], a[f + "Wv"], a[f + "Wo"]]
    for q in range(NE // 2):
        units.append(a[f + "W1"][2 * q:2 * q + 2].transpose(1, 0, 2).reshape(D, 2 * HID))
        units.append(a[f + "W2"][2 * q:2 * q + 2].reshape(2 * HID, D))
    arrays = {
        "x": a["x"], "src": a["src"], "dst": a["dst"],
        "w_all": np.stack([chunked(w) for w in units]),
        "mix_bq": column(a[m + "bq"]), "mix_bv": column(a[m + "bv"]),
        "mix_rows": np.stack([a["L0_gnn_b"], a[m + "bn_scale"], a[m + "bn_bias"], a[m + "bn_mean"],
                              a[m + "bn_var"], a[m + "bo"]]),
        "ffn_bq": column(a[f + "bq"]), "ffn_bk": column(a[f + "bk"]),
        "ffn_g1": column(a[f + "g1"]), "ffn_beta1": column(a[f + "beta1"]),
        "ffn_rows": np.stack([a[f + "bv"], a[f + "bo"], a[f + "g1"], a[f + "beta1"], a[f + "g2"], a[f + "beta2"]]),
        "wg": chunked(a[f + "Wg"]), "bg": a[f + "bg"].reshape(NE, 1),
        "b1": column(a[f + "b1"]), "b2": a[f + "b2"],
    }
    nc = bacc.Bacc("TRN2", target_bir_lowering=False, num_devices=1)
    args = []
    for name in _INS:
        arrays[name] = np.ascontiguousarray(arrays[name])
        args.append(nc.dram_tensor("in_" + name, arrays[name].shape, mybir.dt.from_np(arrays[name].dtype),
                                   kind="ExternalInput").ap())
    args.append(nc.dram_tensor("out_rows", (N, D), F32, kind="ExternalOutput").ap())
    gps_layer(nc, *args)
    r = run_bass_kernel_spmd(nc, [{"in_" + k: v for k, v in arrays.items()}], core_ids=[0])
    return r.results[0]["out_rows"]
```
